# Optimizing a Trainium2 kernel written in Bass

```python
import numpy as np
import jax
import jax.numpy as jnp

def _softmax(x, axis=-1):
    return jax.nn.softmax(x, axis=axis)
def _gelu(x):
    return jax.nn.gelu(x, approximate=True)
def _silu(x):
    return jax.nn.silu(x)
def _sigmoid(x):
    return jax.nn.sigmoid(x)
def _layernorm(x, axis=-1, eps=1e-5):
    m = jnp.mean(x, axis=axis, keepdims=True)
    v = jnp.var(x, axis=axis, keepdims=True)
    return (x - m) / jnp.sqrt(v + eps)
def _scatter_add(tgt, idx, src, axis=0):
    return tgt.at[idx].add(src)
def _segment_sum(src, seg, n):
    return jax.ops.segment_sum(src, seg, n)

kernel_name = 'mk_conv_preact_d4_conv_nchw2048_85688a'

def setup_inputs(seed: int = 0):
    np.random.seed(seed)
    _w = jnp.asarray
    def _rec_inputs():
        import jax
        import jax.numpy as jnp
        _gk = jax.random.key(seed)
        x = -0.0001329 + 0.9999 * jax.random.normal(jax.random.fold_in(_gk, 1), (64, 2048, 24, 12), jnp.float32)
        return x
    x = _rec_inputs()
    def _L0_conv_setup():
        import jax, jax.numpy as jnp
        import numpy as np
        STATE = 16
        DT_RANK = 48
        INNER = 1536
        LN_EPS = 1e-05

        def _forward(x, pe_w, pe_b, ln_g, ln_b, in_w, conv_w, conv_b, A_log, xproj_w, dtproj_w, dtproj_b, D_param, out_w):
            B, C, H, W = x.shape
            xp = x.reshape(B, C, 3, H // 3, 3, W // 3).mean(axis=(3, 5))
            tok = xp.reshape(B, C, 9).transpose(0, 2, 1)
            tok = tok @ pe_w + pe_b
            mu = tok.mean(-1, keepdims=True)
            var = tok.var(-1, keepdims=True)
            h = (tok - mu) / jnp.sqrt(var + LN_EPS) * ln_g + ln_b
            xz = h @ in_w
            xs, z = (xz[..., :INNER], xz[..., INNER:])
            xc = jax.lax.conv_general_dilated(xs.transpose(0, 2, 1), conv_w, window_strides=(1,), padding=[(1, 1)], feature_group_count=INNER, dimension_numbers=('NCH', 'OIH', 'NCH'))
            xc = (xc + conv_b[None, :, None]).transpose(0, 2, 1)
            xc = jax.nn.silu(xc)
            A = -jnp.exp(A_log)
            dbc = xc @ xproj_w
            d_r = dbc[..., :DT_RANK]
            Bp = dbc[..., DT_RANK:DT_RANK + STATE]
            Cp = dbc[..., DT_RANK + STATE:]
            delta = jax.nn.softplus(d_r @ dtproj_w + dtproj_b)
            dA = jnp.exp(delta[..., None] * A)
            dBu = delta[..., None] * Bp[:, :, None, :] * xc[..., None]

            def step(s, t):
                dA_i, dBu_i, C_i = t
                s = dA_i * s + dBu_i
                y = jnp.einsum('bdn,bn->bd', s, C_i)
                return (s, y)
            s0 = jnp.zeros((B, INNER, STATE), xc.dtype)
            _, ys = jax.lax.scan(step, s0, (dA.transpose(1, 0, 2, 3), dBu.transpose(1, 0, 2, 3), Cp.transpose(1, 0, 2)))
            y = ys.transpose(1, 0, 2) + xc * D_param
            y = y * jax.nn.silu(z)
            out = y @ out_w
            out = out.transpose(0, 2, 1).reshape(B, C, 3, 3)
            out = jax.image.resize(out, (B, C, H, W), method='bilinear')
            return out
        key = jax.random.key(seed)
        ks = jax.random.split(key, 10)
        B, C, H, W = (128, 2048, 24, 12)
        hid = 768
        inp = {}
        inp['x'] = jax.random.normal(ks[0], (B, C, H, W), jnp.float32)
        inp['pe_w'] = jax.random.normal(ks[1], (C, hid), jnp.float32) * 0.02
        inp['pe_b'] = jnp.zeros((hid,), jnp.float32)
        inp['ln_g'] = jnp.ones((hid,), jnp.float32)
        inp['ln_b'] = jnp.zeros((hid,), jnp.float32)
        inp['in_w'] = jax.random.normal(ks[2], (hid, 2 * INNER), jnp.float32) * 0.02
        inp['conv_w'] = jax.random.normal(ks[3], (INNER, 1, 3), jnp.float32) * 0.1
        inp['conv_b'] = jnp.zeros((INNER,), jnp.float32)
        inp['A_log'] = jnp.log(jnp.broadcast_to(jnp.arange(1, STATE + 1, dtype=jnp.float32), (INNER, STATE)))
        inp['xproj_w'] = jax.random.normal(ks[4], (INNER, DT_RANK + 2 * STATE), jnp.float32) * 0.02
        inp['dtproj_w'] = jax.random.normal(ks[5], (DT_RANK, INNER), jnp.float32) * 0.02
        inp['dtproj_b'] = jnp.zeros((INNER,), jnp.float32)
        inp['D_param'] = jnp.ones((INNER,), jnp.float32)
        inp['out_w'] = jax.random.normal(ks[6], (INNER, C), jnp.float32) * 0.02
        return inp
    _L0_conv_all = _L0_conv_setup()
    _L0_conv_in = {k: v for k, v in _L0_conv_all.items() if k in ('pe_w', 'pe_b', 'ln_g', 'ln_b', 'in_w', 'conv_w', 'conv_b', 'A_log', 'xproj_w', 'dtproj_w', 'dtproj_b', 'D_param', 'out_w', )}
    del _L0_conv_all

    def _L1_conv_setup():
        import jax, jax.numpy as jnp
        import numpy as np
        STATE = 16
        DT_RANK = 48
        INNER = 1536
        LN_EPS = 1e-05

        def _forward(x, pe_w, pe_b, ln_g, ln_b, in_w, conv_w, conv_b, A_log, xproj_w, dtproj_w, dtproj_b, D_param, out_w):
            B, C, H, W = x.shape
            xp = x.reshape(B, C, 3, H // 3, 3, W // 3).mean(axis=(3, 5))
            tok = xp.reshape(B, C, 9).transpose(0, 2, 1)
            tok = tok @ pe_w + pe_b
            mu = tok.mean(-1, keepdims=True)
            var = tok.var(-1, keepdims=True)
            h = (tok - mu) / jnp.sqrt(var + LN_EPS) * ln_g + ln_b
            xz = h @ in_w
            xs, z = (xz[..., :INNER], xz[..., INNER:])
            xc = jax.lax.conv_general_dilated(xs.transpose(0, 2, 1), conv_w, window_strides=(1,), padding=[(1, 1)], feature_group_count=INNER, dimension_numbers=('NCH', 'OIH', 'NCH'))
            xc = (xc + conv_b[None, :, None]).transpose(0, 2, 1)
            xc = jax.nn.silu(xc)
            A = -jnp.exp(A_log)
            dbc = xc @ xproj_w
            d_r = dbc[..., :DT_RANK]
            Bp = dbc[..., DT_RANK:DT_RANK + STATE]
            Cp = dbc[..., DT_RANK + STATE:]
            delta = jax.nn.softplus(d_r @ dtproj_w + dtproj_b)
            dA = jnp.exp(delta[..., None] * A)
            dBu = delta[..., None] * Bp[:, :, None, :] * xc[..., None]

            def step(s, t):
                dA_i, dBu_i, C_i = t
                s = dA_i * s + dBu_i
                y = jnp.einsum('bdn,bn->bd', s, C_i)
                return (s, y)
            s0 = jnp.zeros((B, INNER, STATE), xc.dtype)
            _, ys = jax.lax.scan(step, s0, (dA.transpose(1, 0, 2, 3), dBu.transpose(1, 0, 2, 3), Cp.transpose(1, 0, 2)))
            y = ys.transpose(1, 0, 2) + xc * D_param
            y = y * jax.nn.silu(z)
            out = y @ out_w
            out = out.transpose(0, 2, 1).reshape(B, C, 3, 3)
            out = jax.image.resize(out, (B, C, H, W), method='bilinear')
            return out
        key = jax.random.key(seed)
        ks = jax.random.split(key, 10)
        B, C, H, W = (128, 2048, 24, 12)
        hid = 768
        inp = {}
        inp['x'] = jax.random.normal(ks[0], (B, C, H, W), jnp.float32)
        inp['pe_w'] = jax.random.normal(ks[1], (C, hid), jnp.float32) * 0.02
        inp['pe_b'] = jnp.zeros((hid,), jnp.float32)
        inp['ln_g'] = jnp.ones((hid,), jnp.float32)
        inp['ln_b'] = jnp.zeros((hid,), jnp.float32)
        inp['in_w'] = jax.random.normal(ks[2], (hid, 2 * INNER), jnp.float32) * 0.02
        inp['conv_w'] = jax.random.normal(ks[3], (INNER, 1, 3), jnp.float32) * 0.1
        inp['conv_b'] = jnp.zeros((INNER,), jnp.float32)
        inp['A_log'] = jnp.log(jnp.broadcast_to(jnp.arange(1, STATE + 1, dtype=jnp.float32), (INNER, STATE)))
        inp['xproj_w'] = jax.random.normal(ks[4], (INNER, DT_RANK + 2 * STATE), jnp.float32) * 0.02
        inp['dtproj_w'] = jax.random.normal(ks[5], (DT_RANK, INNER), jnp.float32) * 0.02
        inp['dtproj_b'] = jnp.zeros((INNER,), jnp.float32)
        inp['D_param'] = jnp.ones((INNER,), jnp.float32)
        inp['out_w'] = jax.random.normal(ks[6], (INNER, C), jnp.float32) * 0.02
        return inp
    _L1_conv_all = _L1_conv_setup()
    _L1_conv_in = {k: v for k, v in _L1_conv_all.items() if k in ('pe_w', 'pe_b', 'ln_g', 'ln_b', 'in_w', 'conv_w', 'conv_b', 'A_log', 'xproj_w', 'dtproj_w', 'dtproj_b', 'D_param', 'out_w', )}
    del _L1_conv_all

    def _L2_conv_setup():
        import jax, jax.numpy as jnp
        import numpy as np
        STATE = 16
        DT_RANK = 48
        INNER = 1536
        LN_EPS = 1e-05

        def _forward(x, pe_w, pe_b, ln_g, ln_b, in_w, conv_w, conv_b, A_log, xproj_w, dtproj_w, dtproj_b, D_param, out_w):
            B, C, H, W = x.shape
            xp = x.reshape(B, C, 3, H // 3, 3, W // 3).mean(axis=(3, 5))
            tok = xp.reshape(B, C, 9).transpose(0, 2, 1)
            tok = tok @ pe_w + pe_b
            mu = tok.mean(-1, keepdims=True)
            var = tok.var(-1, keepdims=True)
            h = (tok - mu) / jnp.sqrt(var + LN_EPS) * ln_g + ln_b
            xz = h @ in_w
            xs, z = (xz[..., :INNER], xz[..., INNER:])
            xc = jax.lax.conv_general_dilated(xs.transpose(0, 2, 1), conv_w, window_strides=(1,), padding=[(1, 1)], feature_group_count=INNER, dimension_numbers=('NCH', 'OIH', 'NCH'))
            xc = (xc + conv_b[None, :, None]).transpose(0, 2, 1)
            xc = jax.nn.silu(xc)
            A = -jnp.exp(A_log)
            dbc = xc @ xproj_w
            d_r = dbc[..., :DT_RANK]
            Bp = dbc[..., DT_RANK:DT_RANK + STATE]
            Cp = dbc[..., DT_RANK + STATE:]
            delta = jax.nn.softplus(d_r @ dtproj_w + dtproj_b)
            dA = jnp.exp(delta[..., None] * A)
            dBu = delta[..., None] * Bp[:, :, None, :] * xc[..., None]

            def step(s, t):
                dA_i, dBu_i, C_i = t
                s = dA_i * s + dBu_i
                y = jnp.einsum('bdn,bn->bd', s, C_i)
                return (s, y)
            s0 = jnp.zeros((B, INNER, STATE), xc.dtype)
            _, ys = jax.lax.scan(step, s0, (dA.transpose(1, 0, 2, 3), dBu.transpose(1, 0, 2, 3), Cp.transpose(1, 0, 2)))
            y = ys.transpose(1, 0, 2) + xc * D_param
            y = y * jax.nn.silu(z)
            out = y @ out_w
            out = out.transpose(0, 2, 1).reshape(B, C, 3, 3)
            out = jax.image.resize(out, (B, C, H, W), method='bilinear')
            return out
        key = jax.random.key(seed)
        ks = jax.random.split(key, 10)
        B, C, H, W = (128, 2048, 24, 12)
        hid = 768
        inp = {}
        inp['x'] = jax.random.normal(ks[0], (B, C, H, W), jnp.float32)
        inp['pe_w'] = jax.random.normal(ks[1], (C, hid), jnp.float32) * 0.02
        inp['pe_b'] = jnp.zeros((hid,), jnp.float32)
        inp['ln_g'] = jnp.ones((hid,), jnp.float32)
        inp['ln_b'] = jnp.zeros((hid,), jnp.float32)
        inp['in_w'] = jax.random.normal(ks[2], (hid, 2 * INNER), jnp.float32) * 0.02
        inp['conv_w'] = jax.random.normal(ks[3], (INNER, 1, 3), jnp.float32) * 0.1
        inp['conv_b'] = jnp.zeros((INNER,), jnp.float32)
        inp['A_log'] = jnp.log(jnp.broadcast_to(jnp.arange(1, STATE + 1, dtype=jnp.float32), (INNER, STATE)))
        inp['xproj_w'] = jax.random.normal(ks[4], (INNER, DT_RANK + 2 * STATE), jnp.float32) * 0.02
        inp['dtproj_w'] = jax.random.normal(ks[5], (DT_RANK, INNER), jnp.float32) * 0.02
        inp['dtproj_b'] = jnp.zeros((INNER,), jnp.float32)
        inp['D_param'] = jnp.ones((INNER,), jnp.float32)
        inp['out_w'] = jax.random.normal(ks[6], (INNER, C), jnp.float32) * 0.02
        return inp
    _L2_conv_all = _L2_conv_setup()
    _L2_conv_in = {k: v for k, v in _L2_conv_all.items() if k in ('pe_w', 'pe_b', 'ln_g', 'ln_b', 'in_w', 'conv_w', 'conv_b', 'A_log', 'xproj_w', 'dtproj_w', 'dtproj_b', 'D_param', 'out_w', )}
    del _L2_conv_all

    def _L3_conv_setup():
        import jax, jax.numpy as jnp
        import numpy as np
        B_, C_IN, H_, W_ = (64, 2048, 24, 12)
        HID = 768
        INNER = 2 * HID
        N_STATE = 16
        DT_RANK = 48

        def _interp_axis(n_in, n_out):
            src = (jnp.arange(n_out, dtype=jnp.float32) + 0.5) * (n_in / n_out) - 0.5
            src = jnp.maximum(src, 0.0)
            i0 = jnp.minimum(jnp.floor(src).astype(jnp.int32), n_in - 1)
            i1 = jnp.minimum(i0 + 1, n_in - 1)
            w = src - i0.astype(jnp.float32)
            return (i0, i1, w)
        key = jax.random.key(seed)
        ks = jax.random.split(key, 8)
        s = 0.02
        return {'x': jax.random.normal(ks[0], (B_, C_IN, H_, W_), jnp.float32), 'pe_W': jax.random.normal(ks[1], (C_IN, HID), jnp.float32) * s, 'pe_b': jnp.zeros((HID,), jnp.float32), 'ln_g': jnp.ones((HID,), jnp.float32), 'ln_b': jnp.zeros((HID,), jnp.float32), 'in_W': jax.random.normal(ks[2], (HID, 2 * INNER), jnp.float32) * s, 'conv_w': jax.random.normal(ks[3], (INNER, 1, 3), jnp.float32) * s, 'conv_b': jnp.zeros((INNER,), jnp.float32), 'xproj_W': jax.random.normal(ks[4], (INNER, DT_RANK + 2 * N_STATE), jnp.float32) * s, 'dt_W': jax.random.normal(ks[5], (DT_RANK, INNER), jnp.float32) * s, 'dt_b': jnp.zeros((INNER,), jnp.float32), 'A_log': jnp.log(jnp.broadcast_to(jnp.arange(1, N_STATE + 1, dtype=jnp.float32), (INNER, N_STATE))), 'D_param': jnp.ones((INNER,), jnp.float32), 'out_W': jax.random.normal(ks[6], (INNER, C_IN), jnp.float32) * s}
    _L3_conv_all = _L3_conv_setup()
    _L3_conv_in = {k: v for k, v in _L3_conv_all.items() if k in ('pe_W', 'pe_b', 'ln_g', 'ln_b', 'in_W', 'conv_w', 'conv_b', 'xproj_W', 'dt_W', 'dt_b', 'A_log', 'D_param', 'out_W', )}
    del _L3_conv_all

    return {
        "x": x,
        "L0_conv_pe_w": _L0_conv_in["pe_w"],
        "L0_conv_pe_b": _L0_conv_in["pe_b"],
        "L0_conv_ln_g": _L0_conv_in["ln_g"],
        "L0_conv_ln_b": _L0_conv_in["ln_b"],
        "L0_conv_in_w": _L0_conv_in["in_w"],
        "L0_conv_conv_w": _L0_conv_in["conv_w"],
        "L0_conv_conv_b": _L0_conv_in["conv_b"],
        "L0_conv_A_log": _L0_conv_in["A_log"],
        "L0_conv_xproj_w": _L0_conv_in["xproj_w"],
        "L0_conv_dtproj_w": _L0_conv_in["dtproj_w"],
        "L0_conv_dtproj_b": _L0_conv_in["dtproj_b"],
        "L0_conv_D_param": _L0_conv_in["D_param"],
        "L0_conv_out_w": _L0_conv_in["out_w"],
        "L1_conv_pe_w": _L1_conv_in["pe_w"],
        "L1_conv_pe_b": _L1_conv_in["pe_b"],
        "L1_conv_ln_g": _L1_conv_in["ln_g"],
        "L1_conv_ln_b": _L1_conv_in["ln_b"],
        "L1_conv_in_w": _L1_conv_in["in_w"],
        "L1_conv_conv_w": _L1_conv_in["conv_w"],
        "L1_conv_conv_b": _L1_conv_in["conv_b"],
        "L1_conv_A_log": _L1_conv_in["A_log"],
        "L1_conv_xproj_w": _L1_conv_in["xproj_w"],
        "L1_conv_dtproj_w": _L1_conv_in["dtproj_w"],
        "L1_conv_dtproj_b": _L1_conv_in["dtproj_b"],
        "L1_conv_D_param": _L1_conv_in["D_param"],
        "L1_conv_out_w": _L1_conv_in["out_w"],
        "L2_conv_pe_w": _L2_conv_in["pe_w"],
        "L2_conv_pe_b": _L2_conv_in["pe_b"],
        "L2_conv_ln_g": _L2_conv_in["ln_g"],
        "L2_conv_ln_b": _L2_conv_in["ln_b"],
        "L2_conv_in_w": _L2_conv_in["in_w"],
        "L2_conv_conv_w": _L2_conv_in["conv_w"],
        "L2_conv_conv_b": _L2_conv_in["conv_b"],
        "L2_conv_A_log": _L2_conv_in["A_log"],
        "L2_conv_xproj_w": _L2_conv_in["xproj_w"],
        "L2_conv_dtproj_w": _L2_conv_in["dtproj_w"],
        "L2_conv_dtproj_b": _L2_conv_in["dtproj_b"],
        "L2_conv_D_param": _L2_conv_in["D_param"],
        "L2_conv_out_w": _L2_conv_in["out_w"],
        "L3_conv_pe_W": _L3_conv_in["pe_W"],
        "L3_conv_pe_b": _L3_conv_in["pe_b"],
        "L3_conv_ln_g": _L3_conv_in["ln_g"],
        "L3_conv_ln_b": _L3_conv_in["ln_b"],
        "L3_conv_in_W": _L3_conv_in["in_W"],
        "L3_conv_conv_w": _L3_conv_in["conv_w"],
        "L3_conv_conv_b": _L3_conv_in["conv_b"],
        "L3_conv_xproj_W": _L3_conv_in["xproj_W"],
        "L3_conv_dt_W": _L3_conv_in["dt_W"],
        "L3_conv_dt_b": _L3_conv_in["dt_b"],
        "L3_conv_A_log": _L3_conv_in["A_log"],
        "L3_conv_D_param": _L3_conv_in["D_param"],
        "L3_conv_out_W": _L3_conv_in["out_W"],
    }

def reference(x, L0_conv_pe_w, L0_conv_pe_b, L0_conv_ln_g, L0_conv_ln_b, L0_conv_in_w, L0_conv_conv_w, L0_conv_conv_b, L0_conv_A_log, L0_conv_xproj_w, L0_conv_dtproj_w, L0_conv_dtproj_b, L0_conv_D_param, L0_conv_out_w, L1_conv_pe_w, L1_conv_pe_b, L1_conv_ln_g, L1_conv_ln_b, L1_conv_in_w, L1_conv_conv_w, L1_conv_conv_b, L1_conv_A_log, L1_conv_xproj_w, L1_conv_dtproj_w, L1_conv_dtproj_b, L1_conv_D_param, L1_conv_out_w, L2_conv_pe_w, L2_conv_pe_b, L2_conv_ln_g, L2_conv_ln_b, L2_conv_in_w, L2_conv_conv_w, L2_conv_conv_b, L2_conv_A_log, L2_conv_xproj_w, L2_conv_dtproj_w, L2_conv_dtproj_b, L2_conv_D_param, L2_conv_out_w, L3_conv_pe_W, L3_conv_pe_b, L3_conv_ln_g, L3_conv_ln_b, L3_conv_in_W, L3_conv_conv_w, L3_conv_conv_b, L3_conv_xproj_W, L3_conv_dt_W, L3_conv_dt_b, L3_conv_A_log, L3_conv_D_param, L3_conv_out_W):
    import jax
    import jax.numpy as jnp
    def _L0_conv_ref(x, pe_w, pe_b, ln_g, ln_b, in_w, conv_w, conv_b, A_log, xproj_w, dtproj_w, dtproj_b, D_param, out_w):
        import jax, jax.numpy as jnp
        import numpy as np
        STATE = 16
        DT_RANK = 48
        INNER = 1536
        LN_EPS = 1e-05

        def _forward(x, pe_w, pe_b, ln_g, ln_b, in_w, conv_w, conv_b, A_log, xproj_w, dtproj_w, dtproj_b, D_param, out_w):
            B, C, H, W = x.shape
            xp = x.reshape(B, C, 3, H // 3, 3, W // 3).mean(axis=(3, 5))
            tok = xp.reshape(B, C, 9).transpose(0, 2, 1)
            tok = tok @ pe_w + pe_b
            mu = tok.mean(-1, keepdims=True)
            var = tok.var(-1, keepdims=True)
            h = (tok - mu) / jnp.sqrt(var + LN_EPS) * ln_g + ln_b
            xz = h @ in_w
            xs, z = (xz[..., :INNER], xz[..., INNER:])
            xc = jax.lax.conv_general_dilated(xs.transpose(0, 2, 1), conv_w, window_strides=(1,), padding=[(1, 1)], feature_group_count=INNER, dimension_numbers=('NCH', 'OIH', 'NCH'))
            xc = (xc + conv_b[None, :, None]).transpose(0, 2, 1)
            xc = jax.nn.silu(xc)
            A = -jnp.exp(A_log)
            dbc = xc @ xproj_w
            d_r = dbc[..., :DT_RANK]
            Bp = dbc[..., DT_RANK:DT_RANK + STATE]
            Cp = dbc[..., DT_RANK + STATE:]
            delta = jax.nn.softplus(d_r @ dtproj_w + dtproj_b)
            dA = jnp.exp(delta[..., None] * A)
            dBu = delta[..., None] * Bp[:, :, None, :] * xc[..., None]

            def step(s, t):
                dA_i, dBu_i, C_i = t
                s = dA_i * s + dBu_i
                y = jnp.einsum('bdn,bn->bd', s, C_i)
                return (s, y)
            s0 = jnp.zeros((B, INNER, STATE), xc.dtype)
            _, ys = jax.lax.scan(step, s0, (dA.transpose(1, 0, 2, 3), dBu.transpose(1, 0, 2, 3), Cp.transpose(1, 0, 2)))
            y = ys.transpose(1, 0, 2) + xc * D_param
            y = y * jax.nn.silu(z)
            out = y @ out_w
            out = out.transpose(0, 2, 1).reshape(B, C, 3, 3)
            out = jax.image.resize(out, (B, C, H, W), method='bilinear')
            return out
        return _forward(x, pe_w, pe_b, ln_g, ln_b, in_w, conv_w, conv_b, A_log, xproj_w, dtproj_w, dtproj_b, D_param, out_w)

    def _L1_conv_ref(x, pe_w, pe_b, ln_g, ln_b, in_w, conv_w, conv_b, A_log, xproj_w, dtproj_w, dtproj_b, D_param, out_w):
        import jax, jax.numpy as jnp
        import numpy as np
        STATE = 16
        DT_RANK = 48
        INNER = 1536
        LN_EPS = 1e-05

        def _forward(x, pe_w, pe_b, ln_g, ln_b, in_w, conv_w, conv_b, A_log, xproj_w, dtproj_w, dtproj_b, D_param, out_w):
            B, C, H, W = x.shape
            xp = x.reshape(B, C, 3, H // 3, 3, W // 3).mean(axis=(3, 5))
            tok = xp.reshape(B, C, 9).transpose(0, 2, 1)
            tok = tok @ pe_w + pe_b
            mu = tok.mean(-1, keepdims=True)
            var = tok.var(-1, keepdims=True)
            h = (tok - mu) / jnp.sqrt(var + LN_EPS) * ln_g + ln_b
            xz = h @ in_w
            xs, z = (xz[..., :INNER], xz[..., INNER:])
            xc = jax.lax.conv_general_dilated(xs.transpose(0, 2, 1), conv_w, window_strides=(1,), padding=[(1, 1)], feature_group_count=INNER, dimension_numbers=('NCH', 'OIH', 'NCH'))
            xc = (xc + conv_b[None, :, None]).transpose(0, 2, 1)
            xc = jax.nn.silu(xc)
            A = -jnp.exp(A_log)
            dbc = xc @ xproj_w
            d_r = dbc[..., :DT_RANK]
            Bp = dbc[..., DT_RANK:DT_RANK + STATE]
            Cp = dbc[..., DT_RANK + STATE:]
            delta = jax.nn.softplus(d_r @ dtproj_w + dtproj_b)
            dA = jnp.exp(delta[..., None] * A)
            dBu = delta[..., None] * Bp[:, :, None, :] * xc[..., None]

            def step(s, t):
                dA_i, dBu_i, C_i = t
                s = dA_i * s + dBu_i
                y = jnp.einsum('bdn,bn->bd', s, C_i)
                return (s, y)
            s0 = jnp.zeros((B, INNER, STATE), xc.dtype)
            _, ys = jax.lax.scan(step, s0, (dA.transpose(1, 0, 2, 3), dBu.transpose(1, 0, 2, 3), Cp.transpose(1, 0, 2)))
            y = ys.transpose(1, 0, 2) + xc * D_param
            y = y * jax.nn.silu(z)
            out = y @ out_w
            out = out.transpose(0, 2, 1).reshape(B, C, 3, 3)
            out = jax.image.resize(out, (B, C, H, W), method='bilinear')
            return out
        return _forward(x, pe_w, pe_b, ln_g, ln_b, in_w, conv_w, conv_b, A_log, xproj_w, dtproj_w, dtproj_b, D_param, out_w)

    def _L2_conv_ref(x, pe_w, pe_b, ln_g, ln_b, in_w, conv_w, conv_b, A_log, xproj_w, dtproj_w, dtproj_b, D_param, out_w):
        import jax, jax.numpy as jnp
        import numpy as np
        STATE = 16
        DT_RANK = 48
        INNER = 1536
        LN_EPS = 1e-05

        def _forward(x, pe_w, pe_b, ln_g, ln_b, in_w, conv_w, conv_b, A_log, xproj_w, dtproj_w, dtproj_b, D_param, out_w):
            B, C, H, W = x.shape
            xp = x.reshape(B, C, 3, H // 3, 3, W // 3).mean(axis=(3, 5))
            tok = xp.reshape(B, C, 9).transpose(0, 2, 1)
            tok = tok @ pe_w + pe_b
            mu = tok.mean(-1, keepdims=True)
            var = tok.var(-1, keepdims=True)
            h = (tok - mu) / jnp.sqrt(var + LN_EPS) * ln_g + ln_b
            xz = h @ in_w
            xs, z = (xz[..., :INNER], xz[..., INNER:])
            xc = jax.lax.conv_general_dilated(xs.transpose(0, 2, 1), conv_w, window_strides=(1,), padding=[(1, 1)], feature_group_count=INNER, dimension_numbers=('NCH', 'OIH', 'NCH'))
            xc = (xc + conv_b[None, :, None]).transpose(0, 2, 1)
            xc = jax.nn.silu(xc)
            A = -jnp.exp(A_log)
            dbc = xc @ xproj_w
            d_r = dbc[..., :DT_RANK]
            Bp = dbc[..., DT_RANK:DT_RANK + STATE]
            Cp = dbc[..., DT_RANK + STATE:]
            delta = jax.nn.softplus(d_r @ dtproj_w + dtproj_b)
            dA = jnp.exp(delta[..., None] * A)
            dBu = delta[..., None] * Bp[:, :, None, :] * xc[..., None]

            def step(s, t):
                dA_i, dBu_i, C_i = t
                s = dA_i * s + dBu_i
                y = jnp.einsum('bdn,bn->bd', s, C_i)
                return (s, y)
            s0 = jnp.zeros((B, INNER, STATE), xc.dtype)
            _, ys = jax.lax.scan(step, s0, (dA.transpose(1, 0, 2, 3), dBu.transpose(1, 0, 2, 3), Cp.transpose(1, 0, 2)))
            y = ys.transpose(1, 0, 2) + xc * D_param
            y = y * jax.nn.silu(z)
            out = y @ out_w
            out = out.transpose(0, 2, 1).reshape(B, C, 3, 3)
            out = jax.image.resize(out, (B, C, H, W), method='bilinear')
            return out
        return _forward(x, pe_w, pe_b, ln_g, ln_b, in_w, conv_w, conv_b, A_log, xproj_w, dtproj_w, dtproj_b, D_param, out_w)

    def _L3_conv_ref(x, pe_W, pe_b, ln_g, ln_b, in_W, conv_w, conv_b, xproj_W, dt_W, dt_b, A_log, D_param, out_W):
        import jax, jax.numpy as jnp
        import numpy as np
        B_, C_IN, H_, W_ = (64, 2048, 24, 12)
        HID = 768
        INNER = 2 * HID
        N_STATE = 16
        DT_RANK = 48

        def _interp_axis(n_in, n_out):
            src = (jnp.arange(n_out, dtype=jnp.float32) + 0.5) * (n_in / n_out) - 0.5
            src = jnp.maximum(src, 0.0)
            i0 = jnp.minimum(jnp.floor(src).astype(jnp.int32), n_in - 1)
            i1 = jnp.minimum(i0 + 1, n_in - 1)
            w = src - i0.astype(jnp.float32)
            return (i0, i1, w)
        B, C, H, W = x.shape
        D_in = conv_w.shape[0]
        dt_rank = dt_W.shape[0]
        nstate = A_log.shape[1]
        p = x.reshape(B, C, 3, H // 3, 3, W // 3).mean(axis=(3, 5))
        tok = p.reshape(B, C, 9).transpose(0, 2, 1) @ pe_W + pe_b
        mu = tok.mean(-1, keepdims=True)
        var = jnp.mean((tok - mu) ** 2, axis=-1, keepdims=True)
        t = (tok - mu) / jnp.sqrt(var + 1e-05) * ln_g + ln_b
        xz = t @ in_W
        xc, z = jnp.split(xz, [D_in], axis=-1)
        xdl = xc.transpose(0, 2, 1)
        xdl = jax.lax.conv_general_dilated(xdl, conv_w, (1,), [(1, 1)], dimension_numbers=('NCH', 'OIH', 'NCH'), feature_group_count=D_in) + conv_b[None, :, None]
        u = jax.nn.silu(xdl.transpose(0, 2, 1))
        A = -jnp.exp(A_log)
        dBC = u @ xproj_W
        dlt, Bp, Cp = jnp.split(dBC, [dt_rank, dt_rank + nstate], axis=-1)
        delta = jax.nn.softplus(dlt @ dt_W + dt_b)

        def step(state, inp):
            u_l, d_l, B_l, C_l = inp
            k1 = A[None] * state + B_l[:, None, :] * u_l[:, :, None]
            state = state + d_l[:, :, None] * k1
            y_l = jnp.einsum('bdn,bn->bd', state, C_l)
            return (state, y_l)
        st0 = jnp.zeros((B, D_in, nstate), u.dtype)
        _, ys = jax.lax.scan(step, st0, (u.transpose(1, 0, 2), delta.transpose(1, 0, 2), Bp.transpose(1, 0, 2), Cp.transpose(1, 0, 2)))
        y = ys.transpose(1, 0, 2) + u * D_param
        y = y * jax.nn.silu(z)
        out_tok = y @ out_W
        g = out_tok.transpose(0, 2, 1).reshape(B, out_W.shape[1], 3, 3)
        i0y, i1y, wy = _interp_axis(3, H)
        i0x, i1x, wx = _interp_axis(3, W)
        top = g[:, :, i0y, :]
        bot = g[:, :, i1y, :]
        v00 = top[:, :, :, i0x]
        v01 = top[:, :, :, i1x]
        v10 = bot[:, :, :, i0x]
        v11 = bot[:, :, :, i1x]
        wy_ = wy[None, None, :, None]
        wx_ = wx[None, None, None, :]
        out = (1 - wy_) * ((1 - wx_) * v00 + wx_ * v01) + wy_ * ((1 - wx_) * v10 + wx_ * v11)
        return out

    def _gn(v, G=32, eps=1e-5):
        B_, C_, H_, W_ = v.shape
        g = v.reshape(B_, G, C_ // G, H_, W_)
        m = jnp.mean(g, axis=(2, 3, 4), keepdims=True)
        s = jnp.var(g, axis=(2, 3, 4), keepdims=True)
        return ((g - m) / jnp.sqrt(s + eps)).reshape(v.shape)

    def _ln_c(v, eps=1e-6):
        m = jnp.mean(v, axis=1, keepdims=True)
        s = jnp.var(v, axis=1, keepdims=True)
        return (v - m) / jnp.sqrt(s + eps)

    def _ln_t(v, eps=1e-5):
        m = jnp.mean(v, axis=-1, keepdims=True)
        s = jnp.var(v, axis=-1, keepdims=True)
        return (v - m) / jnp.sqrt(s + eps)

    def _to_tokens(v):
        B_, C_, H_, W_ = v.shape
        return v.reshape(B_, C_, H_ * W_).transpose(0, 2, 1)
    def _from_tokens(t, like):
        B_, C_, H_, W_ = like.shape
        return t.transpose(0, 2, 1).reshape(B_, C_, H_, W_)

    x = x + _L0_conv_ref(_gn(x), L0_conv_pe_w, L0_conv_pe_b, L0_conv_ln_g, L0_conv_ln_b, L0_conv_in_w, L0_conv_conv_w, L0_conv_conv_b, L0_conv_A_log, L0_conv_xproj_w, L0_conv_dtproj_w, L0_conv_dtproj_b, L0_conv_D_param, L0_conv_out_w)
    x = x + _L1_conv_ref(_gn(x), L1_conv_pe_w, L1_conv_pe_b, L1_conv_ln_g, L1_conv_ln_b, L1_conv_in_w, L1_conv_conv_w, L1_conv_conv_b, L1_conv_A_log, L1_conv_xproj_w, L1_conv_dtproj_w, L1_conv_dtproj_b, L1_conv_D_param, L1_conv_out_w)
    x = x + _L2_conv_ref(_gn(x), L2_conv_pe_w, L2_conv_pe_b, L2_conv_ln_g, L2_conv_ln_b, L2_conv_in_w, L2_conv_conv_w, L2_conv_conv_b, L2_conv_A_log, L2_conv_xproj_w, L2_conv_dtproj_w, L2_conv_dtproj_b, L2_conv_D_param, L2_conv_out_w)
    x = x + _L3_conv_ref(_gn(x), L3_conv_pe_W, L3_conv_pe_b, L3_conv_ln_g, L3_conv_ln_b, L3_conv_in_W, L3_conv_conv_w, L3_conv_conv_b, L3_conv_xproj_W, L3_conv_dt_W, L3_conv_dt_b, L3_conv_A_log, L3_conv_D_param, L3_conv_out_W)
    return x


_drawn_inputs = setup_inputs


def setup_inputs(seed=0):
    import zlib

    import numpy as np

    out = dict(_drawn_inputs(seed))
    spreads = {'L0_conv_pe_b': (0.0, 0.1),
     'L0_conv_ln_g': (1.0, 0.6),
     'L0_conv_ln_b': (0.0, 0.8),
     'L0_conv_conv_b': (0.0, 0.1),
     'L0_conv_dtproj_b': (0.0, 0.8),
     'L0_conv_D_param': (1.0, 0.6),
     'L1_conv_pe_b': (0.0, 0.1),
     'L1_conv_ln_g': (1.0, 0.6),
     'L1_conv_ln_b': (0.0, 0.8),
     'L1_conv_conv_b': (0.0, 0.1),
     'L1_conv_dtproj_b': (0.0, 0.8),
     'L1_conv_D_param': (1.0, 0.6),
     'L2_conv_pe_b': (0.0, 0.1),
     'L2_conv_ln_g': (1.0, 0.6),
     'L2_conv_ln_b': (0.0, 0.786),
     'L2_conv_conv_b': (0.0, 0.1),
     'L2_conv_dtproj_b': (0.0, 0.8),
     'L2_conv_D_param': (1.0, 0.6),
     'L3_conv_pe_b': (0.0, 0.1),
     'L3_conv_ln_g': (1.0, 0.2),
     'L3_conv_ln_b': (0.0, 0.1),
     'L3_conv_conv_b': (0.0, 0.1),
     'L3_conv_dt_b': (0.0, 0.1),
     'L3_conv_D_param': (1.0, 0.6)}
    factors = {'L0_conv_A_log': 8.0,
     'L0_conv_xproj_w': 8.0,
     'L0_conv_dtproj_w': 8.0,
     'L1_conv_A_log': 8.0,
     'L1_conv_xproj_w': 8.0,
     'L1_conv_dtproj_w': 8.0,
     'L2_conv_A_log': 8.0,
     'L2_conv_xproj_w': 8.0,
     'L2_conv_dtproj_w': 8.0}
    for name, (base, spread) in spreads.items():
        noise = np.random.default_rng([zlib.crc32(name.encode()), seed]).standard_normal(out[name].shape)
        drawn = base * np.exp(spread * noise) if base else spread * noise
        out[name] = jnp.asarray(drawn.astype(out[name].dtype))
    for name, factor in factors.items():
        out[name] = (out[name] * factor).astype(out[name].dtype)
    return out
```

```python
from contextlib import ExitStack

import numpy as np

import concourse.bass as bass
from concourse import mybir

ALU = mybir.AluOpType
ACT = mybir.ActivationFunctionType
AX = mybir.AxisListType
F32 = mybir.dt.float32
BF16 = mybir.dt.bfloat16

P = 128
LAYERS = 4
B, C, H, W = 64, 2048, 24, 12
PIX = H * W
G3 = 3
T = G3 * G3
HID, INNER, STATE, RANK = 768, 1536, 16, 48
EPS = 1e-5
GN_GROUPS = 32
CJ = C // P
KH = HID // P
KI = INNER // P
DBC = RANK + 2 * STATE
HALVES = 2
HB = B // HALVES
TOK = HB * T
QB = 4
QG = B // QB
HG = HB // QB
CHUNKS = 4
JC = CJ // CHUNKS
CHUNK = JC * TOK
PACK = JC * QB * T
NQ = 2
NS = STATE // NQ
XB = QB

FREE = 1

V_PEB, V_G, V_B = 0, KH, 2 * KH
V_CW = 3 * KH
V_CB = V_CW + 3 * KI
V_DTB = V_CB + KI
V_D = V_DTB + KI
V_A = V_D + KI
NV = V_A + KI * STATE

C_ID, C_BLK, C_ONE = 0, P, 2 * P
C_RS, C_PS, C_LE, C_EN, C_IE = (3 * P + T * n for n in range(5))
NC = 3 * P + 5 * T


def interpolation(n_out):
    src = np.clip((np.arange(n_out) + 0.5) * (G3 / n_out) - 0.5, 0.0, G3 - 1.0)
    i0 = np.minimum(np.floor(src).astype(int), G3 - 1)
    i1 = np.minimum(i0 + 1, G3 - 1)
    r = np.zeros((n_out, G3))
    r[np.arange(n_out), i0] += 1 - (src - i0)
    r[np.arange(n_out), i1] += src - i0
    return r


def constants():
    u = np.array([[1.0, 1, 1], [1, 0, -1], [1, -2, 1]])
    n1 = (u * u).sum(1)
    ry, rx = interpolation(H), interpolation(W)
    gy = ((ry @ u.T) ** 2).sum(0)
    gx = ((rx @ u.T) ** 2).sum(0)
    py = np.kron(np.eye(G3), np.ones((1, H // G3))) / (H // G3)
    px = np.kron(np.eye(G3), np.ones((1, W // G3))) / (W // G3)
    ly = np.array([(py @ ry @ u[k]) @ u[k] / n1[k] for k in range(G3)])
    lx = np.array([(px @ rx @ u[k]) @ u[k] / n1[k] for k in range(G3)])
    e = np.sqrt(np.outer(gy, gx)).ravel()
    lam = np.outer(ly, lx).ravel()
    n = np.outer(n1, n1).ravel()
    con = np.zeros((P, NC), np.float32)
    con[:, C_ID:C_ID + P] = np.eye(P)
    lanes = P // GN_GROUPS
    con[:, C_BLK:C_BLK + P] = np.kron(np.eye(GN_GROUPS), np.ones((lanes, lanes)))
    con[:, C_ONE:C_ONE + P] = 1.0 / HID
    con[:, C_RS:C_RS + T] = 1 / e
    con[:, C_PS:C_PS + T] = e / (lam * n * (PIX // T))
    con[:, C_LE:C_LE + T] = lam / e
    con[:, C_EN:C_EN + T] = e / n
    con[:, C_IE:C_IE + T] = 1 / e
    rmat = np.kron(ry, rx).T
    spread = np.zeros((2 * QB * T, 2 * QB, PIX), np.float32)
    for i in range(2 * QB):
        spread[i * T:(i + 1) * T, i] = rmat
    return con, spread


class Order:

    def __init__(self, eng, sem):
        self.eng, self.sem, self.base, self.k = eng, sem, 0, 0

    def done(self, ins):
        ins.then_inc(self.sem, 1)
        self.k += 1

    def wait(self):
        self.eng.wait_ge(self.sem, self.base + self.k)

    def link(self, ins):
        self.done(ins)
        self.wait()

    def loop(self, start, end, per):
        return _OrderLoop(self, start, end, per)


class _OrderLoop:
    def __init__(self, order, start, end, per):
        self.o, self.start, self.end, self.per = order, start, end, per

    def __enter__(self):
        o = self.o
        self.base, self.k = o.base, o.k
        self.fori = o.eng.Fori(self.start, self.end)
        i = self.fori.__enter__()
        o.base, o.k = self.base + self.k + (i - self.start) * self.per, 0
        return i

    def __exit__(self, *e):
        o = self.o
        if e[0] is None:
            assert o.k == self.per, (o.k, self.per)
        self.fori.__exit__(*e)
        o.base, o.k = self.base, self.k + (self.end - self.start) * self.per


def functionals(dve, o, S, M, ct, out, tmp):
    a0, a1, a2, d0, d1, d2, m01, m23, a01, aw, dw, mdiff, msum = tmp
    for g, (a, d) in enumerate(((a0, d0), (a1, d1), (a2, d2))):
        o.done(dve.tensor_tensor(a, S[g], S[5 - g], ALU.add))
        o.done(dve.tensor_tensor(d, S[g], S[5 - g], ALU.subtract))
    o.done(dve.tensor_tensor(m01, M[0], M[1], ALU.add))
    o.done(dve.tensor_tensor(m23, M[2], M[3], ALU.add))
    o.wait()
    o.done(dve.tensor_tensor(a01, a0, a1, ALU.add))
    o.done(dve.scalar_tensor_tensor(aw, a1, 0.25, a0, ALU.mult, ALU.add))
    o.done(dve.tensor_tensor(out[3], d0, d1, ALU.add))
    o.done(dve.scalar_tensor_tensor(dw, d1, 0.75, d0, ALU.mult, ALU.add))
    o.done(dve.tensor_tensor(mdiff, m23, m01, ALU.subtract))
    o.done(dve.tensor_tensor(msum, m23, m01, ALU.add))
    o.wait()
    o.done(dve.tensor_tensor(out[0], a01, a2, ALU.add))
    o.done(dve.scalar_tensor_tensor(out[4], a2, -2.0, a01, ALU.mult, ALU.add))
    o.done(dve.scalar_tensor_tensor(a0, a2, -1.25, aw, ALU.mult, ALU.add))
    o.done(dve.scalar_tensor_tensor(d0, d2, 0.25, dw, ALU.mult, ALU.add))
    o.wait()
    o.done(dve.scalar_tensor_tensor(out[2], mdiff, 3 * ct, a0, ALU.mult, ALU.add))
    o.done(dve.scalar_tensor_tensor(out[1], msum, -ct, d0, ALU.mult, ALU.add))
    o.wait()


FUNCTIONALS = 20


def to_points(dve, o, src, dst):
    o.done(dve.tensor_tensor(dst(0), src(0), src(2), ALU.add))
    o.done(dve.scalar_tensor_tensor(dst(1), src(2), -2.0, src(0), ALU.mult, ALU.add))
    o.wait()
    o.link(dve.tensor_tensor(dst(2), dst(0), src(1), ALU.subtract))
    o.link(dve.tensor_tensor(dst(0), dst(0), src(1), ALU.add))


def to_modes(dve, o, src, dst):
    o.done(dve.tensor_tensor(dst(0), src(0), src(2), ALU.add))
    o.done(dve.tensor_tensor(dst(1), src(0), src(2), ALU.subtract))
    o.wait()
    o.link(dve.scalar_tensor_tensor(dst(2), src(1), -2.0, dst(0), ALU.mult, ALU.add))
    o.link(dve.tensor_tensor(dst(0), dst(0), src(1), ALU.add))


def along_x(buf, n):
    v = buf[:, 0:n * T].rearrange("p (r k) -> p r k", k=G3)
    return lambda k: v[:, :, k]


def along_y(buf, n):
    v = buf[:, 0:n * T].rearrange("p (r y x) -> p r y x", y=G3, x=G3)
    return lambda k: v[:, :, k, :]


def statistics(nc, sb, ps, sem, x, con_d, pr_d, s_d, cperp):
    xb = sb("xb", [P, XB, CJ * PIX], F32)
    junk = ps("junk", [P, 5 * 512], F32)
    con = sb("st_con", [P, NC], F32)
    row_a = sb("row_a", [P, 2, CJ * 6 * W], F32)
    row_b = sb("row_b", [P, 2, CJ * 4 * W], F32)
    ysum = sb("ysum", [P, QB, CJ * 6 * W], F32)
    ymom = sb("ymom", [P, QB, CJ * 4 * W], F32)
    ytmp = sb("ytmp", [P, 9, QB * CJ * W], F32)
    yout = sb("yout", [P, QB * CJ, 5, W], F32)
    rows = QB * CJ * 5
    xsum = ytmp[:, 0:3, :].rearrange("p a b -> p (a b)")[:, 0:rows * 6].rearrange("p (r g) -> p r g", g=6)
    xmom = ytmp[:, 3:5, :].rearrange("p a b -> p (a b)")[:, 0:rows * 4].rearrange("p (r g) -> p r g", g=4)
    xtmp = sb("xtmp", [P, 9, rows], F32)
    xout = sb("xout", [P, 5, rows], F32)
    stage = sb("stage", [P, 2, CJ, QB, T], F32)
    sq_r = sb("sq_r", [P, CJ * QB * T], F32)
    zero = sb("zero", [P, CHUNK], F32)
    sumsq = sb("sumsq", [P, B, 2], F32)
    esum = sb("esum", [P, QB], F32)
    etot = sb("etot", [P, QB], F32)

    x_full = [sem(f"x_full{i}") for i in range(XB)]
    con_full = sem("st_con_full")
    x_summed = sem("x_summed")
    x_squared = sem("x_squared")
    staged = sem("staged")
    r_squared = sem("r_squared")
    stored = sem("st_stored")
    stage_free = sem("stage_free")
    zero_set = sem("zero_set")
    zero_stored = sem("zero_stored")
    pool_steps = sem("st_pool_steps")
    own = sem("st_dve_own")
    xv = x.rearrange("b (p j) h w -> b p (j h w)", p=P)

    with nc.Block() as block:
        @block.sync
        def _(sp):
            sp.dma_start(con[:], con_d).then_inc(con_full, 16)

            def load(image, i):
                sp.dma_start(xb[:, i, :], xv[bass.ds(image, 1)].rearrange("o p n -> (o p) n")).then_inc(x_full[i], 16)
            for i in range(XB):
                load(i, i)
            with sp.Fori(0, QG - 1) as g:
                for i in range(XB):
                    sp.wait_ge(x_summed, g * QB + i + 1)
                    sp.wait_ge(x_squared, FREE + (g * QB + i + 1) * 2)
                    load((g + 1) * QB + i, i)

        @block.gpsimd
        def _(pool):
            pool.sem_inc(stage_free, FREE)
            pool.wait_ge(zero_set, 1)
            for h in range(HALVES):
                for c in range(CHUNKS):
                    pool.dma_start(s_d[h, c], zero[:]).then_inc(zero_stored, 16)
            with pool.Fori(0, QG) as g:
                pool.wait_ge(staged, g + 1)
                pool.sem_inc(pool_steps, 1)
                pool.dma_start(pr_d[bass.ds(g, 1)].rearrange("o p a n -> (o p) (a n)"),
                               stage[:].rearrange("p a j b k -> p (a j b k)")).then_inc(stored, 16)
                pool.wait_ge(stored, (g + 1) * 16)
                pool.sem_inc(stage_free, 1)
            pool.wait_ge(zero_stored, 16 * HALVES * CHUNKS)
            pool.wait_ge(stored, 16 * QG)

        @block.scalar
        def _(act):
            half = CJ * PIX // 2
            act.sem_inc(x_squared, FREE)
            with act.Fori(0, QG) as g:
                for i in range(QB):
                    act.wait_ge(x_full[i], (g + 1) * 16)
                    for n in range(2):
                        act.wait_ge(x_squared, FREE + (g * QB + i) * 2 + n)
                        act.activation(junk[:, 0:half], xb[:, i, n * half:(n + 1) * half], ACT.Square,
                                       accum_out=sumsq[:, bass.ds(g * QB + i, 1), n:n + 1]).then_inc(x_squared, 1)
                act.wait_ge(staged, g + 1)
                act.activation(sq_r[:], stage[:, 0].rearrange("p j b k -> p (j b k)"), ACT.Square).then_inc(r_squared, 1)

        @block.vector
        def _(dve):
            o = Order(dve, own)
            dve.memset(zero[:], 0.0).then_inc(zero_set, 1)
            dve.wait_ge(con_full, 16)

            def image(g, i):
                dve.wait_ge(x_full[i], (g + 1) * 16)
                v = xb[:, i, :].rearrange("p (jg k w) -> p jg k w", k=4, w=W)
                vm = xb[:, i, :].rearrange("p (j g k w) -> p j g k w", g=6, k=4, w=W)[:, :, 1:5]
                a = [row_a[:, n, :].rearrange("p (r w) -> p r w", w=W) for n in range(2)]
                bb = [row_b[:, n, :].rearrange("p (j g w) -> p j g w", g=4, w=W) for n in range(2)]
                o.done(dve.tensor_tensor(a[0], v[:, :, 0, :], v[:, :, 3, :], ALU.add))
                o.done(dve.tensor_tensor(a[1], v[:, :, 1, :], v[:, :, 2, :], ALU.add))
                o.done(dve.tensor_tensor(bb[0], vm[:, :, :, 3, :], vm[:, :, :, 0, :], ALU.subtract))
                dve.tensor_tensor(bb[1], vm[:, :, :, 2, :], vm[:, :, :, 1, :], ALU.subtract).then_inc(x_summed, 1)
                o.wait()
                dve.wait_ge(x_summed, g * QB + i + 1)
                o.done(dve.tensor_tensor(ysum[:, i, :], row_a[:, 0, :], row_a[:, 1, :], ALU.add))
                o.done(dve.scalar_tensor_tensor(ymom[:, i, :], row_b[:, 0, :], 3.0, row_b[:, 1, :], ALU.mult, ALU.add))
                o.wait()

            rest = row_a[:].rearrange("p a n -> p (a n)"), row_b[:, 0, :]

            def temps(n):
                own = ytmp if n == QB * CJ * W else xtmp
                return [own[:, i, :] for i in range(9)] + [rest[0][:, i * n:(i + 1) * n] for i in range(3)] + [rest[1][:, 0:n]]

            per = QB * 5 + 2 * FUNCTIONALS + 2 + 2
            with o.loop(0, QG, per) as g:
                for i in range(QB):
                    image(g, i)
                sv = ysum[:].rearrange("p b (j g w) -> p (b j) g w", g=6, w=W)
                mv = ymom[:].rearrange("p b (j g w) -> p (b j) g w", g=4, w=W)
                functionals(dve, o, [sv[:, :, n, :] for n in range(6)], [mv[:, :, n, :] for n in range(4)], 0.0625,
                            [yout[:, :, n, :] for n in range(5)],
                            [v.rearrange("p (r w) -> p r w", w=W) for v in temps(QB * CJ * W)])
                yr = yout[:].rearrange("p r f (g e) -> p (r f) g e", e=2)
                o.done(dve.tensor_tensor(xsum, yr[:, :, :, 0], yr[:, :, :, 1], ALU.add))
                o.done(dve.tensor_tensor(xmom, yr[:, :, 1:5, 1], yr[:, :, 1:5, 0], ALU.subtract))
                o.wait()
                functionals(dve, o, [xsum[:, :, n] for n in range(6)], [xmom[:, :, n] for n in range(4)], 0.125,
                            [xout[:, n, :] for n in range(5)], temps(rows))
                dve.wait_ge(stage_free, FREE + g)
                z = xout[:].rearrange("p f (b j y) -> p f b j y", j=CJ, y=5)
                st = stage[:].rearrange("p a j b (y x) -> p a b j y x", x=G3)
                rs = con[:, C_RS:C_RS + T].rearrange("p (y x) -> p y x", x=G3)
                pscale = con[:, C_PS:C_PS + T].rearrange("p (y x) -> p y x", x=G3)

                def spread(v, n):
                    return v.unsqueeze(1).unsqueeze(1).broadcast_to([P, QB, CJ, n])
                for kx in range(G3):
                    fx = (0, 3, 4)[kx]
                    dve.tensor_tensor(st[:, 0, :, :, :, kx], z[:, kx, :, :, 0:3], spread(rs[:, :, kx], 3), ALU.mult)
                    dve.tensor_tensor(st[:, 1, :, :, 0, kx], z[:, fx, :, :, 0],
                                      pscale[:, 0:1, kx].unsqueeze(1).broadcast_to([P, QB, CJ]), ALU.mult)
                    ins = dve.tensor_tensor(st[:, 1, :, :, 1:3, kx], z[:, fx, :, :, 3:5],
                                            spread(pscale[:, 1:3, kx], 2), ALU.mult)
                ins.then_inc(staged, 1)
                dve.wait_ge(r_squared, g + 1)
                o.done(dve.tensor_reduce(esum[:], sq_r[:].rearrange("p (j b k) -> p b j k", b=QB, k=T), AX.XY, ALU.add))
                dve.wait_ge(x_squared, FREE + (g + 1) * QB * 2)
                sv2 = sumsq[:, bass.ds(g * QB, QB), :]
                o.link(dve.tensor_tensor(etot[:], sv2[:, :, 0], sv2[:, :, 1], ALU.add))
                dve.tensor_tensor(cperp[:, bass.ds(g * QB, QB)], etot[:], esum[:], ALU.subtract)


def layers(nc, sb, ps, sem, con_d, vec_d, pe_d, in_d, xp_d, dt_d, out_d, pr_d, s_d, bc_d, cperp):
    con = sb("con", [P, NC], F32)
    vec = sb("vec", [P, NV], F32)
    half_cw = sb("half_cw", [P, 4 * KI], F32)
    neg_a = sb("neg_a", [P, KI * STATE], F32)
    xpw = sb("xpw", [P, KI * DBC], F32)
    dtw = sb("dtw", [RANK, INNER], F32)
    wring = sb("wring", [P, 2, CJ * P], F32)
    pbuf = sb("pbuf", [P, CHUNKS, CHUNK], F32)
    ldp = sb("ldp", [P, 2, CHUNK], F32)
    ldr = sb("ldr", [P, 2, CHUNK], F32)
    lds = sb("lds", [P, 2, CHUNK], F32)
    tok = sb("tok", [P, KH * TOK], F32)
    tok2 = sb("tok2", [P, KH * TOK], F32)
    u = sb("u", [P, KI * TOK], F32)
    delta = sb("delta", [P, KI * TOK], F32)
    zs = sb("zs", [P, KI * TOK], F32)
    zt = sb("zt", [P, 2, TOK], F32)
    dbc = sb("dbc", [DBC, TOK], F32)
    bc = sb("bc", [P, 2 * STATE, TOK], F32)
    dA = sb("dA", [P, NQ, NS * TOK], F32)
    st = sb("st", [P, NQ, NS * TOK], F32)
    wt = sb("wt", [P, TOK], F32)
    cgrp = sb("cgrp", [P, B], F32)
    small = sb("small", [P, 6, HB], F32)
    rexp = sb("rexp", [P, TOK], F32)
    softp = pbuf[:].rearrange("p c n -> p (c n)")[:, 0:KI * TOK]

    mm_ps = ps("mm_ps", [P, 2, 512], F32)
    y_ps = ps("y_ps", [P, 2, 512], F32)
    gm_ps = ps("gm_ps", [P, 512], F32)
    ge_ps = ps("ge_ps", [P, 512], F32)
    ln_ps = ps("ln_ps", [P, 512], F32)
    xp_ps = ps("xp_ps", [P, 512], F32)

    con_full = sem("con_full")
    par_full = sem("par_full")
    w_full = [sem(f"w_full{i}") for i in range(2)]
    ld_full = [sem(f"ld_full{i}") for i in range(2)]
    ks_full = [sem(f"ks_full{i}") for i in range(2)]
    ks_stored = [sem(f"ks_stored{i}") for i in range(2)]
    bc_stored = sem("bc_stored")
    bc_full = sem("bc_full")
    mm_free = [sem(f"mm_free{i}") for i in range(2)]
    p_sum = sem("p_sum")
    r_sum = sem("r_sum")
    r_sq = sem("r_sq")
    ge_done = sem("ge_done")
    gn_var, gn_std, ln_std = sem("gn_var"), sem("gn_std"), sem("ln_std")
    pn_ready = sem("pn_ready")
    mm_done = sem("mm_done")
    tok_points = sem("tok_points")
    tok_biased = sem("tok_biased")
    ln_sum = sem("ln_sum")
    tok_centred = sem("tok_centred")
    tok_sq = sem("tok_sq")
    tok_normed = sem("tok_normed")
    h_ready = sem("h_ready")
    xs_mid = sem("xs_mid")
    conv_tanh = sem("conv_tanh")
    u_ready = sem("u_ready")
    z_tanh = sem("z_tanh")
    z_ready = sem("z_ready")
    xp_done = sem("xp_done")
    dbc_ready = sem("dbc_ready")
    sp_ready = sem("sp_ready")
    delta_ready = sem("delta_ready")
    dA_zero = sem("dA_zero")
    dA_ready = sem("dA_ready")
    dA_free = [sem(f"dA_free{q}") for q in range(NQ)]
    cgrp_sum = sem("cgrp_sum")
    sc_ready = sem("sc_ready")
    sc_used = [sem(f"sc_used{q}") for q in range(NQ)]
    y_free = [sem(f"y_free{i}") for i in range(2)]
    yhat_ready = sem("yhat_ready")
    pool_steps = sem("pool_steps")
    own_d = sem("dve_own")
    own_a = sem("act_own")

    ident = con[:, C_ID:C_ID + P]
    MM_SLOT = KH + 2 * KI + KI + CJ
    W_SLOT = (KH + KI + CJ) // 2

    def chunk4(buf):
        return buf.rearrange("p (g j n) -> p g j n", j=JC, n=QB * T)

    with nc.Block() as block:
        @block.sync
        def _(sp):
            with sp.Fori(0, LAYERS) as l:
                with sp.Fori(0, HALVES) as h:
                    s = l * HALVES + h

                    def fetch(w_d, chunk, k, before):
                        sp.wait_ge(mm_done, FREE + s * MM_SLOT + before)
                        sp.dma_start(wring[:, k, 0:w_d.shape[-1]],
                                     w_d[bass.ds(l, 1), bass.ds(chunk, 1)].rearrange("a c p n -> (a c p) n")
                                     ).then_inc(w_full[k], 16)
                    for c in range(KH):
                        fetch(pe_d, c, c % 2, c - 1 if c >= 2 else 0)
                    with sp.Fori(0, KI // 2) as i:
                        for k in range(2):
                            fetch(in_d, i * 2 + k, k, KH - 1 + i * 4 + k)
                    with sp.Fori(0, CJ // 2) as i:
                        for k in range(2):
                            fetch(out_d, i * 2 + k, k, KH + 3 * KI - 1 + i * 2 + k)

        @block.gpsimd
        def _(pool):
            pool.dma_start(con[:], con_d).then_inc(con_full, 16)

            def move(dst, src):
                pool.sem_inc(pool_steps, 1)
                return pool.dma_start(dst, src)
            with pool.Fori(0, LAYERS) as l:
                with pool.Fori(0, HALVES) as h:
                    s = l * HALVES + h
                    pool.wait_ge(yhat_ready, FREE + s)
                    move(vec[:], vec_d[bass.ds(l, 1)].rearrange("a p n -> (a p) n")).then_inc(par_full, 16)
                    move(xpw[:], xp_d[bass.ds(l, 1)].rearrange("a p n -> (a p) n")).then_inc(par_full, 16)
                    move(dtw[:], dt_d[bass.ds(l, 1)].rearrange("a p n -> (a p) n")).then_inc(par_full, 16)
                    for c in range(CHUNKS):
                        k = c % 2
                        if c >= 2:
                            pool.wait_ge(r_sum, s * CHUNKS + c - 1)
                            pool.wait_ge(ge_done, s * CHUNKS + c - 1)
                        src = pr_d[bass.ds(h * HG, HG)]
                        for a, buf in ((1, ldp), (0, ldr)):
                            move(buf[:, k, :].rearrange("p (g n) -> p g n", n=PACK),
                                           src[:, :, a, c * PACK:(c + 1) * PACK].rearrange("g p n -> p g n")
                                           ).then_inc(ld_full[k], 16)
                        move(lds[:, k, :], s_d[bass.ds(h, 1), c].rearrange("o p n -> (o p) n")
                                       ).then_inc(ld_full[k], 16)
                    pool.wait_ge(dbc_ready, s + 1)
                    move(bc_d[0:32, :], dbc[RANK:DBC, :]).then_inc(bc_stored, 16)
                    pool.wait_ge(bc_stored, (s + 1) * 16)
                    move(bc[:], bc_d.unsqueeze(0).broadcast_to([P, 2 * STATE, TOK])).then_inc(bc_full, 16)
                    pool.wait_ge(r_sum, (s + 1) * CHUNKS)

                    def load(c):
                        move(lds[:, c % 2, :], s_d[bass.ds(h, 1), c].rearrange("o p n -> (o p) n")
                                       ).then_inc(ks_full[c % 2], 16)
                    load(0)
                    load(1)
                    for c in range(CHUNKS):
                        for k in range(2):
                            pool.wait_ge(mm_free[k], FREE + s * (MM_SLOT // 2) + (KH + 3 * KI) // 2 + (c + 1) * (JC // 2))
                        move(s_d[bass.ds(h, 1), c].rearrange("o p n -> (o p) n"), lds[:, c % 2, :]
                                       ).then_inc(ks_stored[c % 2], 16)
                        pool.wait_ge(ks_stored[c % 2], (s * 2 + c // 2 + 1) * 16)
                        if c + 2 < CHUNKS:
                            load(c + 2)

        @block.tensor
        def _(pe):
            pe.sem_inc(mm_done, FREE)
            for q in range(NQ):
                pe.sem_inc(sc_used[q], FREE)
            pe.wait_ge(con_full, 16)
            blk = con[:, C_BLK:C_BLK + P]
            one = con[:, C_ONE:C_ONE + P]

            def half_layer(l, h):
                s = l * HALVES + h

                def product(use, k, ksteps, lhs, rhs):
                    pe.wait_ge(mm_free[k], FREE + s * (MM_SLOT // 2) + use)
                    for n in range(ksteps):
                        ins = pe.matmul(mm_ps[:, k, 0:TOK], lhs(n), rhs(n), start=(n == 0), stop=(n == ksteps - 1))
                    ins.then_inc(mm_done, 1)

                for c in range(CHUNKS):
                    pe.wait_ge(p_sum, s * CHUNKS + c + 1)
                    pv = pbuf[:, c, :].rearrange("p (g j b k) -> p g j b k", j=JC, b=QB, k=T)
                    for j in range(JC):
                        pe.matmul(gm_ps[:, 0:HB], blk, pv[:, :, j, :, 0], start=(c == 0 and j == 0),
                                  stop=(c == CHUNKS - 1 and j == JC - 1))
                    pe.wait_ge(r_sq, s * CHUNKS + c + 1)
                    rv = chunk4(ldr[:, c % 2, :])
                    for j in range(JC):
                        ins = pe.matmul(ge_ps[:, 0:TOK], blk, rv[:, :, j, :], start=(c == 0 and j == 0),
                                        stop=(c == CHUNKS - 1 and j == JC - 1))
                    ins.then_inc(ge_done, 1)
                with pe.Fori(0, KH // 2) as i:
                    pe.wait_ge(pn_ready, s + 1)
                    for k in range(2):
                        pe.wait_ge(w_full[k], (s * W_SLOT + i + 1) * 16)
                        product(i, k, CJ, lambda n: wring[:, k, n * P:(n + 1) * P],
                                lambda n: chunk4(pbuf[:, n // JC, :])[:, :, n % JC, :])
                for src, there in ((tok, tok_biased), (tok2, tok_sq)):
                    pe.wait_ge(there, s + 1)
                    for m in range(KH):
                        ins = pe.matmul(ln_ps[:, 0:TOK], one, src[:, m * TOK:(m + 1) * TOK], start=(m == 0), stop=(m == KH - 1))
                    ins.then_inc(ln_sum, 1)
                with pe.Fori(0, KI // 2) as i:
                    pe.wait_ge(h_ready, s + 1)
                    for k in range(2):
                        pe.wait_ge(w_full[k], (s * W_SLOT + KH // 2 + i + 1) * 16)
                        for e in range(2):
                            product(KH // 2 + i * 2 + k, e, KH, lambda n: wring[:, k, (e * KH + n) * P:(e * KH + n + 1) * P],
                                    lambda n: tok[:, n * TOK:(n + 1) * TOK])
                pe.wait_ge(u_ready, s + 1)
                pe.wait_ge(par_full, (s + 1) * 48)
                for n in range(KI):
                    ins = pe.matmul(xp_ps[0:DBC, 0:TOK], xpw[:, n * DBC:(n + 1) * DBC], u[:, n * TOK:(n + 1) * TOK],
                                    start=(n == 0), stop=(n == KI - 1))
                ins.then_inc(xp_done, 1)
                pe.wait_ge(dbc_ready, s + 1)
                for m in range(KI):
                    product(KH // 2 + KI + m // 2, m % 2, 1, lambda n: dtw[:, m * P:(m + 1) * P], lambda n: dbc[0:RANK, :])
                with pe.Fori(0, KI // 2) as i:
                    for k in range(2):
                        pe.wait_ge(y_free[k], FREE + s * (KI // 2) + i)
                        for q in range(NQ):
                            pe.wait_ge(sc_ready, (s * KI + i * 2 + k) * NQ + q + 1)
                            for n in range(NS):
                                ins = pe.matmul(y_ps[:, k, 0:TOK], ident, st[:, q, n * TOK:(n + 1) * TOK],
                                                start=(q == 0 and n == 0), stop=(q == NQ - 1 and n == NS - 1))
                            ins.then_inc(sc_used[q], 1)
                with pe.Fori(0, CJ // 2) as i:
                    pe.wait_ge(yhat_ready, FREE + s + 1)
                    for k in range(2):
                        pe.wait_ge(w_full[k], (s * W_SLOT + (KH + KI) // 2 + i + 1) * 16)
                        product((KH + 3 * KI) // 2 + i, k, KI, lambda n: wring[:, k, n * P:(n + 1) * P],
                                lambda n: u[:, n * TOK:(n + 1) * TOK])

            pe.matmul(ln_ps[:, 0:B], blk, cperp[:], start=True, stop=True).then_inc(cgrp_sum, 1)
            with pe.Fori(0, LAYERS) as l:
                with pe.Fori(0, HALVES) as h:
                    half_layer(l, h)

        @block.scalar
        def _(act):
            o = Order(act, own_a)

            def half_layer(l, h):
                s = l * HALVES + h
                uses = s * (MM_SLOT // 2)
                act.wait_ge(par_full, (s + 1) * 48)
                o.done(act.activation(half_cw[:], vec[:, V_CW:V_CW + 4 * KI], ACT.Copy, scale=0.5))
                o.link(act.activation(neg_a[:], vec[:, V_A:V_A + KI * STATE], ACT.Exp))
                o.link(act.activation(neg_a[:], neg_a[:], ACT.Copy, scale=-1.0))
                for c in range(CHUNKS):
                    act.wait_ge(r_sum, s * CHUNKS + c + 1)
                    act.activation(ldr[:, c % 2, :], ldr[:, c % 2, :], ACT.Square).then_inc(r_sq, 1)
                act.wait_ge(gn_var, s + 1)
                act.activation(small[:, 3, :], small[:, 3, :], ACT.Sqrt).then_inc(gn_std, 1)
                act.wait_ge(tok_points, s + 1)
                for m in range(KH):
                    v = tok[:, m * TOK:(m + 1) * TOK]
                    ins = act.activation(v, v, ACT.Identity, bias=vec[:, V_PEB + m:V_PEB + m + 1])
                ins.then_inc(tok_biased, 1)
                act.wait_ge(tok_centred, s + 1)
                act.activation(tok2[:], tok[:], ACT.Square).then_inc(tok_sq, 1)
                act.wait_ge(ln_sum, 2 * s + 2)
                act.activation(rexp[:], ln_ps[:, 0:TOK], ACT.Sqrt, bias=EPS).then_inc(ln_std, 1)
                act.wait_ge(tok_normed, s + 1)
                for m in range(KH):
                    v = tok[:, m * TOK:(m + 1) * TOK]
                    ins = act.activation(v, v, ACT.Identity, scale=vec[:, V_G + m:V_G + m + 1],
                                         bias=vec[:, V_B + m:V_B + m + 1])
                ins.then_inc(h_ready, 1)
                with act.Fori(0, KI // 2) as i:
                    for k in range(2):
                        m = i * 2 + k
                        act.wait_ge(mm_done, FREE + s * MM_SLOT + KH + m + 1)
                        act.activation(u[:, bass.ds(m * TOK, TOK)], mm_ps[:, k, 0:TOK], ACT.Identity,
                                       scale=half_cw[:, bass.ds(m * 3 + 1, 1)], bias=half_cw[:, bass.ds(m + 3 * KI, 1)]
                                       ).then_inc(xs_mid, 1)
                for k in range(2):
                    act.wait_ge(mm_free[k], FREE + uses + (KH + KI) // 2)
                act.activation(delta[:], u[:], ACT.Tanh).then_inc(conv_tanh, 1)
                with act.Fori(0, KI // 2) as i:
                    for k in range(2):
                        act.wait_ge(mm_done, FREE + s * MM_SLOT + KH + KI + i * 2 + k + 1)
                        act.activation(zt[:, k, :], mm_ps[:, k, 0:TOK], ACT.Tanh, scale=0.5).then_inc(z_tanh, 1)
                act.wait_ge(xp_done, s + 1)
                act.activation(dbc[:], xp_ps[0:DBC, 0:TOK], ACT.Copy).then_inc(dbc_ready, 1)
                act.wait_ge(u_ready, s + 1)
                for m in range(KI):
                    k = m % 2
                    act.wait_ge(mm_done, FREE + s * MM_SLOT + KH + 2 * KI + m + 1)
                    bias = vec[:, V_DTB + m:V_DTB + m + 1]
                    o.done(act.activation(softp[:, m * TOK:(m + 1) * TOK], mm_ps[:, k, 0:TOK], ACT.Abs, bias=bias))
                    act.activation(delta[:, m * TOK:(m + 1) * TOK], mm_ps[:, k, 0:TOK], ACT.Relu, bias=bias
                                   ).then_inc(mm_free[k], 1)
                o.wait()
                o.link(act.activation(softp, softp, ACT.Exp, scale=-1.0))
                act.activation(softp, softp, ACT.Ln, bias=1.0).then_inc(sp_ready, 1)

                def factors(func, bias):
                    with act.Fori(0, KI) as m:
                        d = delta[:, bass.ds(m * TOK, TOK)].rearrange("p (b t) -> p b t", t=T)[:, :, 1:T]
                        for q in range(NQ):
                            act.wait_ge(dA_zero, 1)
                            act.wait_ge(delta_ready, s + 1)
                            act.wait_ge(dA_free[q], FREE + s * KI + m)
                            for n in range(NS):
                                v = dA[:, q, n * TOK:(n + 1) * TOK].rearrange("p (b t) -> p b t", t=T)[:, :, 1:T]
                                ins = act.activation(v, d, func, bias=bias, scale=neg_a[:, bass.ds(m * STATE + q * NS + n, 1)])
                            ins.then_inc(dA_ready, 1)
                with act.If(l < LAYERS - 1):
                    factors(ACT.Exp, 0.0)
                with act.Else():
                    factors(ACT.Identity, 1.0)

            with o.loop(0, LAYERS, HALVES * (4 + KI)) as l:
                with o.loop(0, HALVES, 4 + KI) as h:
                    half_layer(l, h)

        @block.vector
        def _(dve):
            o = Order(dve, own_d)
            dve.sem_inc(yhat_ready, FREE)
            for k in range(2):
                dve.sem_inc(mm_free[k], FREE)
                dve.sem_inc(y_free[k], FREE)
            for q in range(NQ):
                dve.sem_inc(dA_free[q], FREE)
            dve.memset(dA[:], 0.0).then_inc(dA_zero, 1)
            dve.wait_ge(con_full, 16)
            le = con[:, C_LE:C_LE + T].unsqueeze(1).broadcast_to([P, HB, T])
            en = con[:, C_EN:C_EN + T].unsqueeze(1).broadcast_to([P, KI * HB, T])

            def images(v):
                return v.rearrange("p (b t) -> p b t", t=T)

            def read_out(s, use):
                for k in range(2):
                    dve.wait_ge(mm_free[k], FREE + s * (MM_SLOT // 2) + use)

            def half_layer(l, h):
                s = l * HALVES + h
                for c in range(CHUNKS):
                    k = c % 2
                    dve.wait_ge(ld_full[k], (s * (CHUNKS // 2) + c // 2 + 1) * 48)
                    dve.tensor_tensor(pbuf[:, c, :], ldp[:, k, :], lds[:, k, :], ALU.add).then_inc(p_sum, 1)
                    dve.tensor_tensor(ldr[:, k, :], ldr[:, k, :], lds[:, k, :], ALU.add).then_inc(r_sum, 1)
                mean, esum, mm2, var, rstd = (small[:, n, :] for n in range(5))
                dve.wait_ge(ge_done, (s + 1) * CHUNKS)
                o.done(dve.tensor_scalar(mean, gm_ps[:, 0:HB], 1.0 / (C // GN_GROUPS), None, ALU.mult))
                o.done(dve.tensor_reduce(esum, ge_ps[:, 0:TOK].rearrange("p (b k) -> p b k", k=T), AX.X, ALU.add))
                o.wait()
                o.done(dve.tensor_tensor(esum, esum, cgrp[:, bass.ds(h * HB, HB)], ALU.add))
                o.done(dve.tensor_tensor(mm2, mean, mean, ALU.mult))
                o.wait()
                o.link(dve.scalar_tensor_tensor(var, mm2, -float(C // GN_GROUPS), esum, ALU.mult, ALU.add))
                dve.tensor_scalar(var, var, 1.0 / (C // GN_GROUPS * PIX), EPS, ALU.mult, ALU.add).then_inc(gn_var, 1)
                dve.wait_ge(gn_std, s + 1)
                o.link(dve.reciprocal(rstd, var))
                o.done(dve.tensor_scalar(images(rexp[:]), rstd.unsqueeze(2).broadcast_to([P, HB, T]), 1.0, None, ALU.mult))
                for c in range(CHUNKS):
                    v = pbuf[:, c, :].rearrange("p (g j b k) -> p g j b k", j=JC, b=QB, k=T)[:, :, :, :, 0]
                    mb = mean.rearrange("p (g b) -> p g b", b=QB).unsqueeze(2).broadcast_to([P, HG, JC, QB])
                    o.done(dve.tensor_tensor(v, v, mb, ALU.subtract))
                o.wait()
                for c in range(CHUNKS):
                    v = chunk4(pbuf[:, c, :])
                    rb = rexp[:].rearrange("p (g n) -> p g n", g=HG).unsqueeze(2).broadcast_to([P, HG, JC, QB * T])
                    ins = dve.tensor_tensor(v, v, rb, ALU.mult)
                ins.then_inc(pn_ready, 1)
                with dve.Fori(0, KH // 2) as i:
                    for k in range(2):
                        dve.wait_ge(mm_done, FREE + s * MM_SLOT + i * 2 + k + 1)
                        dve.tensor_tensor(images(tok[:, bass.ds((i * 2 + k) * TOK, TOK)]), images(mm_ps[:, k, 0:TOK]), le,
                                          ALU.mult).then_inc(mm_free[k], 1)
                read_out(s, KH // 2)
                to_points(dve, o, along_x(tok, KH * HB), along_x(tok2, KH * HB))
                yi, yo = along_y(tok2, KH * HB), along_y(tok, KH * HB)
                o.done(dve.tensor_tensor(yo(0), yi(0), yi(2), ALU.add))
                o.done(dve.scalar_tensor_tensor(yo(1), yi(2), -2.0, yi(0), ALU.mult, ALU.add))
                o.wait()
                o.link(dve.tensor_tensor(yo(2), yo(0), yi(1), ALU.subtract))
                dve.tensor_tensor(yo(0), yo(0), yi(1), ALU.add).then_inc(tok_points, 1)
                tk = tok[:].rearrange("p (m n) -> p m n", n=TOK)

                def over_m(v):
                    return v.unsqueeze(1).broadcast_to([P, KH, TOK])
                dve.wait_ge(ln_sum, 2 * s + 1)
                o.link(dve.tensor_scalar(rexp[:], ln_ps[:, 0:TOK], 1.0, None, ALU.mult))
                dve.tensor_tensor(tk, tk, over_m(rexp[:]), ALU.subtract).then_inc(tok_centred, 1)
                dve.wait_ge(ln_std, s + 1)
                o.link(dve.reciprocal(rexp[:], rexp[:]))
                dve.wait_ge(tok_centred, s + 1)
                dve.tensor_tensor(tk, tk, over_m(rexp[:]), ALU.mult).then_inc(tok_normed, 1)
                with o.loop(0, KI // 2, 2) as i:
                    for k in range(2):
                        m = i * 2 + k
                        dve.wait_ge(xs_mid, s * KI + m + 1)
                        uv, pv = images(u[:, bass.ds(m * TOK, TOK)]), images(mm_ps[:, k, 0:TOK])
                        o.link(dve.scalar_tensor_tensor(uv[:, :, 1:T], pv[:, :, 0:T - 1], half_cw[:, bass.ds(m * 3, 1)],
                                                        uv[:, :, 1:T], ALU.mult, ALU.add))
                        dve.scalar_tensor_tensor(uv[:, :, 0:T - 1], pv[:, :, 1:T], half_cw[:, bass.ds(m * 3 + 2, 1)],
                                                 uv[:, :, 0:T - 1], ALU.mult, ALU.add).then_inc(mm_free[k], 1)
                dve.wait_ge(conv_tanh, s + 1)
                read_out(s, (KH + KI) // 2)
                dve.scalar_tensor_tensor(u[:], delta[:], 1.0, u[:], ALU.add, ALU.mult).then_inc(u_ready, 1)
                with dve.Fori(0, KI // 2) as i:
                    for k in range(2):
                        m = i * 2 + k
                        dve.wait_ge(z_tanh, s * KI + m + 1)
                        dve.scalar_tensor_tensor(zs[:, bass.ds(m * TOK, TOK)], zt[:, k, :], 1.0, mm_ps[:, k, 0:TOK],
                                                 ALU.add, ALU.mult).then_inc(mm_free[k], 1)
                dve.wait_ge(sp_ready, s + 1)
                dve.tensor_tensor(delta[:], delta[:], softp, ALU.add).then_inc(delta_ready, 1)
                dve.wait_ge(delta_ready, s + 1)
                dve.wait_ge(u_ready, s + 1)
                read_out(s, KH // 2 + KI)
                dve.wait_ge(bc_full, (s + 1) * 16)

                def recurrence(m):
                    tile = bass.ds(m * TOK, TOK)
                    o.link(dve.tensor_tensor(wt[:], delta[:, tile], u[:, tile], ALU.mult))
                    for q in range(NQ):
                        v = st[:, q, :].rearrange("p (n t) -> p n t", t=TOK)
                        dve.wait_ge(sc_used[q], FREE + s * KI + m)
                        o.link(dve.tensor_tensor(v, bc[:, q * NS:(q + 1) * NS, :],
                                                 wt[:].unsqueeze(1).broadcast_to([P, NS, TOK]), ALU.mult))
                        dve.wait_ge(dA_ready, (s * KI + m) * NQ + q + 1)
                        dve.tensor_tensor_scan(st[:, q, :], dA[:, q, :], st[:, q, :], 0.0, ALU.mult, ALU.add
                                               ).then_inc(dA_free[q], 1)
                        dve.wait_ge(dA_free[q], FREE + s * KI + m + 1)
                        dve.tensor_tensor(v, v, bc[:, STATE + q * NS:STATE + (q + 1) * NS, :], ALU.mult
                                          ).then_inc(sc_ready, 1)

                def gated(m, k, pair):
                    tile = bass.ds(m * TOK, TOK)
                    for q in range(NQ):
                        dve.wait_ge(sc_used[q], FREE + s * KI + m + 1)
                    dve.scalar_tensor_tensor(u[:, tile], u[:, tile], vec[:, bass.ds(m + V_D, 1)], y_ps[:, k, 0:TOK],
                                             ALU.mult, ALU.add).then_inc(y_free[k], 1)
                    dve.wait_ge(y_free[k], FREE + s * (KI // 2) + pair + 1)
                    o.done(dve.scalar_tensor_tensor(u[:, tile], u[:, tile], 0.5, zs[:, tile], ALU.mult, ALU.mult))

                recurrence(0)
                with o.loop(0, KI // 2 - 1, 2 * (2 + NQ)) as i:
                    recurrence(i * 2 + 1)
                    gated(i * 2, 0, i)
                    recurrence(i * 2 + 2)
                    gated(i * 2 + 1, 1, i)
                recurrence(KI - 1)
                gated(KI - 2, 0, KI // 2 - 1)
                gated(KI - 1, 1, KI // 2 - 1)
                o.wait()
                to_modes(dve, o, along_x(u, KI * HB), along_x(delta, KI * HB))
                to_modes(dve, o, along_y(delta, KI * HB), along_y(u, KI * HB))
                dve.tensor_tensor(images(u[:]), images(u[:]), en, ALU.mult).then_inc(yhat_ready, 1)
                for c in range(CHUNKS):
                    dve.wait_ge(ks_full[c % 2], (s * (CHUNKS // 2) + c // 2 + 1) * 16)
                    for j in range(JC):
                        k = j % 2
                        dve.wait_ge(mm_done, FREE + s * MM_SLOT + KH + 3 * KI + c * JC + j + 1)
                        v = chunk4(lds[:, c % 2, :])[:, :, j, :]
                        dve.tensor_tensor(v, v, mm_ps[:, k, 0:TOK].rearrange("p (g n) -> p g n", g=HG), ALU.add
                                          ).then_inc(mm_free[k], 1)

            dve.wait_ge(cgrp_sum, 1)
            o.link(dve.tensor_scalar(cgrp[:], ln_ps[:, 0:B], 1.0, None, ALU.mult))
            per = 11 + 7 + 2 + KI + (2 + NQ) * KI + 8
            with o.loop(0, LAYERS, HALVES * per) as l:
                with o.loop(0, HALVES, per) as h:
                    half_layer(l, h)


def apply(nc, sb, ps, sem, x, con_d, spread_d, s_d, out):
    PB = 2 * QB
    RT = PB * T
    AB = 4
    con = sb("ap_con", [P, NC], F32)
    spread = sb("ap_spread", [RT, PB, PIX], F32)
    spreadb = sb("ap_spreadb", [RT, PB, PIX], BF16)
    xa = sb("xa", [P, AB, CJ, PIX], F32)
    modes = sb("modes", [P, 2, CJ * RT], F32)
    points = sb("points", [P, CJ * RT], F32)
    turned = sb("turned", [RT, 2, C // 2], F32)
    part = sb("part", [RT, 3, C], BF16)
    acc = ps("acc", [P, 2, 4, 512], F32)

    con_full = sem("ap_con_full")
    s_full = [sem(f"s_full{i}") for i in range(2)]
    x_full = [sem(f"xa_full{i}") for i in range(AB)]
    x_stored = [sem(f"xa_stored{i}") for i in range(AB)]
    spread_ready = sem("spread_ready")
    points_ready = sem("points_ready")
    turned_ps = sem("turned_ps")
    high_ready = sem("high_ready")
    acc_read = sem("acc_read")
    low_ready = sem("low_ready")
    resized = sem("resized")
    own = sem("ap_dve_own")
    xv = x.rearrange("b (p j) h w -> b p (j h w)", p=P)
    ov = out.rearrange("b (p j) h w -> b p (j h w)", p=P)
    GROUPS = B // PB
    QUADS = PB * CHUNKS + 2

    def image(v, b):
        return v[bass.ds(b, 1)].rearrange("o p n -> (o p) n")

    with nc.Block() as block:
        @block.sync
        def _(sp):
            for i in range(AB):
                sp.dma_start(xa[:, i].rearrange("p j n -> p (j n)"), image(xv, i)).then_inc(x_full[i], 16)
            with sp.Fori(0, B // AB - 1) as n:
                for i in range(AB):
                    sp.wait_ge(x_stored[i], (n + 1) * 16)
                    sp.dma_start(xa[:, i].rearrange("p j n -> p (j n)"), image(xv, (n + 1) * AB + i)).then_inc(x_full[i], 16)

        @block.gpsimd
        def _(pool):
            pool.dma_start(con[:], con_d).then_inc(con_full, 16)
            pool.dma_start(spread[:].rearrange("p b n -> p (b n)"), spread_d).then_inc(con_full, 16)

            def fetch(h, g, k):
                for gg in range(2):
                    src = s_d[h:h + 1].rearrange("o c p (g n) -> (o p) c g n", g=HG)[:, :, g * 2 + gg, :]
                    pool.dma_start(modes[:, k, :].rearrange("p (c g n) -> p c g n", c=CHUNKS, g=2)[:, :, gg, :],
                                   src).then_inc(s_full[k], 16)
            for g in range(GROUPS):
                if g >= 2:
                    pool.wait_ge(points_ready, g - 1)
                fetch(g // (GROUPS // HALVES), g % (GROUPS // HALVES), g % 2)

        @block.scalar
        def _(act):
            def store(b, i, uses):
                act.wait_ge(acc_read, uses)
                act.dma_start(image(ov, b), xa[:, i].rearrange("p j n -> p (j n)")).then_inc(x_stored[i], 16)
            with act.Fori(0, GROUPS) as g:
                for e in range(2):
                    act.wait_ge(acc_read, 2 * FREE + g * QUADS + e + 1)
                    act.wait_ge(resized, FREE + g * PB * CHUNKS)
                    act.activation(part[:, 0, e * (C // 2):(e + 1) * (C // 2)], turned[:, e, :], ACT.Copy).then_inc(high_ready, 1)
                for i in range(PB):
                    store(g * PB + i, i % AB, 2 * FREE + g * QUADS + 2 + (i + 1) * CHUNKS)
            for i in range(AB):
                act.wait_ge(x_stored[i], B // AB * 16)

        @block.tensor
        def _(pe):
            pe.sem_inc(resized, FREE)
            pe.wait_ge(con_full, 32)
            pe.wait_ge(spread_ready, 1)
            with pe.Fori(0, GROUPS) as g:
                pe.wait_ge(points_ready, g + 1)
                pv = points[:].rearrange("p (j n) -> p j n", j=CJ)
                for e in range(2):
                    pe.wait_ge(acc_read, 2 * FREE + g * QUADS + e - 1)
                    for j in range(CJ // 2):
                        jj = e * (CJ // 2) + j
                        dst = acc[0:RT, e].rearrange("p a n -> p (a n)")[:, j * P:(j + 1) * P]
                        ins = pe.matmul(dst, pv[:, jj, :], con[:, C_ID:C_ID + P], start=True, stop=True)
                    ins.then_inc(turned_ps, 1)
                pe.wait_ge(low_ready, g + 1)
                for i in range(PB):
                    for c in range(CHUNKS):
                        pe.wait_ge(acc_read, 2 * FREE + g * QUADS + 2 + i * CHUNKS + c - 1)
                        for j in range(JC):
                            for n in range(3):
                                ins = pe.matmul(acc[:, c % 2, j, 0:PIX], part[:, n, (c * JC + j) * P:(c * JC + j + 1) * P],
                                                spreadb[:, i, :], start=(n == 0), stop=(n == 2))
                        ins.then_inc(resized, 1)

        @block.vector
        def _(dve):
            o = Order(dve, own)
            dve.sem_inc(acc_read, 2 * FREE)
            dve.wait_ge(con_full, 32)
            dve.tensor_copy(spreadb[:], spread[:]).then_inc(spread_ready, 1)
            ie = con[:, C_IE:C_IE + T].unsqueeze(1).broadcast_to([P, CJ * PB, T])

            def group(g, k, uses):
                dve.wait_ge(s_full[k], uses * 32)
                m = modes[:, k, :]
                v = m.rearrange("p (r t) -> p r t", t=T)
                o.link(dve.tensor_tensor(v, v, ie, ALU.mult))
                to_points(dve, o, along_x(m, CJ * PB), along_x(points, CJ * PB))
                yi, yo = along_y(points, CJ * PB), along_y(m, CJ * PB)
                to_points(dve, o, yi, yo)
                pv = points[:].rearrange("p (c j g n) -> p c g j n", c=CHUNKS, j=JC, g=2)
                mv = m.rearrange("p (c g j n) -> p c g j n", c=CHUNKS, g=2, j=JC)
                for c in range(CHUNKS):
                    ins = dve.tensor_copy(pv[:, c], mv[:, c])
                ins.then_inc(points_ready, 1)
                for e in range(2):
                    dve.wait_ge(turned_ps, g * 2 + e + 1)
                    dve.tensor_scalar(turned[:, e, :], acc[0:RT, e].rearrange("p a n -> p (a n)")[:, 0:C // 2],
                                      1.0, None, ALU.mult).then_inc(acc_read, 1)
                    dve.wait_ge(acc_read, 2 * FREE + g * QUADS + e + 1)
                    dve.wait_ge(high_ready, g * 2 + e + 1)
                    cols = slice(e * (C // 2), (e + 1) * (C // 2))
                    o.link(dve.tensor_tensor(turned[:, e, :], turned[:, e, :], part[:, 0, cols], ALU.subtract))
                    o.link(dve.tensor_scalar(part[:, 1, cols], turned[:, e, :], 1.0, None, ALU.mult))
                    ins = dve.tensor_tensor(part[:, 2, cols], turned[:, e, :], part[:, 1, cols], ALU.subtract)
                ins.then_inc(low_ready, 1)
                for i in range(PB):
                    dve.wait_ge(x_full[i % AB], (g * (PB // AB) + i // AB + 1) * 16)
                    for c in range(CHUNKS):
                        dve.wait_ge(resized, FREE + (g * PB + i) * CHUNKS + c + 1)
                        v = xa[:, i % AB, c * JC:(c + 1) * JC, :]
                        dve.tensor_tensor(v, v, acc[:, c % 2, :, 0:PIX], ALU.add).then_inc(acc_read, 1)

            with o.loop(0, GROUPS // 2, 2 * (1 + 8 + 4)) as i:
                for k in range(2):
                    group(i * 2 + k, k, i + 1)


def program(nc, t, out):
    ctx = ExitStack()
    with ctx:
        cperp = ctx.enter_context(nc.sbuf_tensor("cperp", [P, B], F32))
        pr_d = nc.dram_tensor("pr_scratch", (QG, P, 2, CJ * QB * T), F32, kind="Internal").ap()
        s_d = nc.dram_tensor("s_scratch", (HALVES, CHUNKS, P, CHUNK), F32, kind="Internal").ap()
        bc_d = nc.dram_tensor("bc_scratch", (2 * STATE, TOK), F32, kind="Internal").ap()

        def phase(build, *args):
            with ExitStack() as own:
                build(nc, lambda n, shape, dt: own.enter_context(nc.sbuf_tensor(n, shape, dt)),
                      lambda n, shape, dt: own.enter_context(nc.psum_tensor(n, shape, dt)),
                      lambda n: ctx.enter_context(nc.semaphore(n)), *args)
        phase(statistics, t["x"], t["con"], pr_d, s_d, cperp)
        phase(layers, t["con"], t["vec"], t["pe"], t["inp"], t["xp"], t["dt"], t["outw"], pr_d, s_d, bc_d, cperp)
        phase(apply, t["x"], t["con"], t["spread"], s_d, out)


def kernel(**inputs):
    import concourse.bacc as _bacc
    from concourse.bass_utils import run_bass_kernel_spmd as _run

    def layer(l):
        new = {"pe_W": "pe_w", "in_W": "in_w", "xproj_W": "xproj_w", "dt_W": "dtproj_w", "dt_b": "dtproj_b", "out_W": "out_w"}
        pre = f"L{l}_conv_"
        return {new.get(n[len(pre):], n[len(pre):]): np.asarray(v) for n, v in inputs.items() if n.startswith(pre)}

    ls = [layer(l) for l in range(LAYERS)]

    def cols(v, n):
        return v.reshape(n, P, -1).transpose(1, 0, 2).reshape(P, -1)

    con, spread = constants()
    arrays = {
        "x": np.asarray(inputs["x"]),
        "con": con,
        "spread": spread.reshape(2 * QB * T, -1),
        "vec": np.stack([np.concatenate([cols(w["pe_b"], KH), cols(w["ln_g"], KH), cols(w["ln_b"], KH),
                                         cols(w["conv_w"], KI), cols(w["conv_b"], KI), cols(w["dtproj_b"], KI),
                                         cols(w["D_param"], KI), cols(w["A_log"], KI)], axis=1) for w in ls]),
        "pe": np.stack([w["pe_w"].reshape(P, CJ, KH, P).transpose(2, 0, 1, 3).reshape(KH, P, CJ * P) for w in ls]),
        "inp": np.stack([w["in_w"].reshape(KH, P, KI, 2, P).transpose(2, 1, 3, 0, 4).reshape(KI, P, 2 * KH * P) for w in ls]),
        "xp": np.stack([w["xproj_w"].reshape(KI, P, DBC).transpose(1, 0, 2).reshape(P, KI * DBC) for w in ls]),
        "dt": np.stack([w["dtproj_w"] for w in ls]),
        "outw": np.stack([w["out_w"].reshape(KI, P, P, CJ).transpose(3, 1, 0, 2).reshape(CJ, P, KI * P) for w in ls]),
    }
    nc = _bacc.Bacc("TRN2", target_bir_lowering=False, num_devices=1)
    t = {n: nc.dram_tensor(f"{n}_dram", a.shape, mybir.dt.from_np(a.dtype), kind="ExternalInput").ap() for n, a in arrays.items()}
    out = nc.dram_tensor("out_dram", (B, C, H, W), F32, kind="ExternalOutput").ap()
    program(nc, t, out)
    r = _run(nc, [{f"{n}_dram": np.ascontiguousarray(a) for n, a in arrays.items()}], core_ids=[0])
    return r.results[0]["out_dram"]
```

```python
from contextlib import ExitStack

import numpy as np

import concourse.bass as bass
from concourse import mybir

ALU = mybir.AluOpType
ACT = mybir.ActivationFunctionType
AX = mybir.AxisListType
F32 = mybir.dt.float32
BF16 = mybir.dt.bfloat16

P = 128
LAYERS = 4
B, C, H, W = 64, 2048, 24, 12
PIX = H * W
G3 = 3
T = G3 * G3
HID, INNER, STATE, RANK = 768, 1536, 16, 48
EPS = 1e-5
GN_GROUPS = 32
CJ = C // P
KH = HID // P
KI = INNER // P
DBC = RANK + 2 * STATE
HALVES = 2
HB = B // HALVES
TOK = HB * T
QB = 4
QG = B // QB
HG = HB // QB
CHUNKS = 4
JC = CJ // CHUNKS
CHUNK = JC * TOK
PACK = JC * QB * T
NQ = 4
NS = STATE // NQ
NDA, NST = 2, 3
STEPS = KI * NQ
MT = 4
XB = QB

FREE = 1

V_PEB, V_G, V_B = 0, KH, 2 * KH
V_CW = 3 * KH
V_CB = V_CW + 3 * KI
V_DTB = V_CB + KI
V_D = V_DTB + KI
V_A = V_D + KI
NV = V_A + KI * STATE

C_ID, C_BLK, C_ONE = 0, P, 2 * P
C_RS, C_PS, C_LE, C_EN, C_IE = (3 * P + T * n for n in range(5))
NC = 3 * P + 5 * T


def interpolation(n_out):
    src = np.clip((np.arange(n_out) + 0.5) * (G3 / n_out) - 0.5, 0.0, G3 - 1.0)
    i0 = np.minimum(np.floor(src).astype(int), G3 - 1)
    i1 = np.minimum(i0 + 1, G3 - 1)
    r = np.zeros((n_out, G3))
    r[np.arange(n_out), i0] += 1 - (src - i0)
    r[np.arange(n_out), i1] += src - i0
    return r


def constants():
    u = np.array([[1.0, 1, 1], [1, 0, -1], [1, -2, 1]])
    n1 = (u * u).sum(1)
    ry, rx = interpolation(H), interpolation(W)
    gy = ((ry @ u.T) ** 2).sum(0)
    gx = ((rx @ u.T) ** 2).sum(0)
    py = np.kron(np.eye(G3), np.ones((1, H // G3))) / (H // G3)
    px = np.kron(np.eye(G3), np.ones((1, W // G3))) / (W // G3)
    ly = np.array([(py @ ry @ u[k]) @ u[k] / n1[k] for k in range(G3)])
    lx = np.array([(px @ rx @ u[k]) @ u[k] / n1[k] for k in range(G3)])
    e = np.sqrt(np.outer(gy, gx)).ravel()
    lam = np.outer(ly, lx).ravel()
    n = np.outer(n1, n1).ravel()
    con = np.zeros((P, NC), np.float32)
    con[:, C_ID:C_ID + P] = np.eye(P)
    lanes = P // GN_GROUPS
    con[:, C_BLK:C_BLK + P] = np.kron(np.eye(GN_GROUPS), np.ones((lanes, lanes)))
    con[:, C_ONE:C_ONE + P] = 1.0 / HID
    con[:, C_RS:C_RS + T] = 1 / e
    con[:, C_PS:C_PS + T] = e / (lam * n * (PIX // T))
    con[:, C_LE:C_LE + T] = lam / e
    con[:, C_EN:C_EN + T] = e / n
    con[:, C_IE:C_IE + T] = 1 / e
    rmat = np.kron(ry, rx).T
    spread = np.zeros((2 * QB * T, 2 * QB, PIX), np.float32)
    for i in range(2 * QB):
        spread[i * T:(i + 1) * T, i] = rmat
    return con, spread


BACK_STEP = [j * 9 // 8 for j in range(CJ)]
CHUNK_STEP = [BACK_STEP[c * JC + JC - 1] for c in range(CHUNKS)]
SUM_STEP = [n + 2 for n in CHUNK_STEP]
GN_STEP = SUM_STEP[-1] + 1
VEC_STEP = GN_STEP
PE_STEP = [GN_STEP + 1 + m * 3 // 2 for m in range(KH)]
LN_STEP = PE_STEP[-1] + 1
IN_STEP = [LN_STEP + 3 + i * 13 // 24 for i in range(2 * KI)]
TANH_STEP = IN_STEP[KI - 1] + 1
XP_STEP = TANH_STEP + 2
XP_CHUNK = (len([i for i in IN_STEP if i <= XP_STEP]) + 1) // 2
IN_PLACE = [KH + c + (c >= XP_CHUNK) for c in range(KI)]
XP_PLACE, DT_PLACE = KH + XP_CHUNK, KH + KI + 1
DT_STEP = [STEPS - 4 + m // 4 for m in range(KI)]
FRONT = KH + 3 * KI
W_FRONT, W_BACK = (KH + KI + 2) // 2, CJ // 2


def on(n, steps):
    return [i for i, at in enumerate(steps) if at == n]


class Order:

    def __init__(self, eng, sem):
        self.eng, self.sem, self.base, self.k = eng, sem, 0, 0

    def done(self, ins):
        ins.then_inc(self.sem, 1)
        self.k += 1

    def wait(self):
        self.eng.wait_ge(self.sem, self.base + self.k)

    def link(self, ins):
        self.done(ins)
        self.wait()

    def loop(self, start, end, per):
        return _OrderLoop(self, start, end, per)


class _OrderLoop:
    def __init__(self, order, start, end, per):
        self.o, self.start, self.end, self.per = order, start, end, per

    def __enter__(self):
        o = self.o
        self.base, self.k = o.base, o.k
        self.fori = o.eng.Fori(self.start, self.end)
        i = self.fori.__enter__()
        o.base, o.k = self.base + self.k + (i - self.start) * self.per, 0
        return i

    def __exit__(self, *e):
        o = self.o
        if e[0] is None:
            assert o.k == self.per, (o.k, self.per)
        self.fori.__exit__(*e)
        o.base, o.k = self.base, self.k + (self.end - self.start) * self.per


def functionals(dve, o, S, M, ct, out, tmp):
    a0, a1, a2, d0, d1, d2, m01, m23, a01, aw, dw, mdiff, msum = tmp
    for g, (a, d) in enumerate(((a0, d0), (a1, d1), (a2, d2))):
        o.done(dve.tensor_tensor(a, S[g], S[5 - g], ALU.add))
        o.done(dve.tensor_tensor(d, S[g], S[5 - g], ALU.subtract))
    o.done(dve.tensor_tensor(m01, M[0], M[1], ALU.add))
    o.done(dve.tensor_tensor(m23, M[2], M[3], ALU.add))
    o.wait()
    o.done(dve.tensor_tensor(a01, a0, a1, ALU.add))
    o.done(dve.scalar_tensor_tensor(aw, a1, 0.25, a0, ALU.mult, ALU.add))
    o.done(dve.tensor_tensor(out[3], d0, d1, ALU.add))
    o.done(dve.scalar_tensor_tensor(dw, d1, 0.75, d0, ALU.mult, ALU.add))
    o.done(dve.tensor_tensor(mdiff, m23, m01, ALU.subtract))
    o.done(dve.tensor_tensor(msum, m23, m01, ALU.add))
    o.wait()
    o.done(dve.tensor_tensor(out[0], a01, a2, ALU.add))
    o.done(dve.scalar_tensor_tensor(out[4], a2, -2.0, a01, ALU.mult, ALU.add))
    o.done(dve.scalar_tensor_tensor(a0, a2, -1.25, aw, ALU.mult, ALU.add))
    o.done(dve.scalar_tensor_tensor(d0, d2, 0.25, dw, ALU.mult, ALU.add))
    o.wait()
    o.done(dve.scalar_tensor_tensor(out[2], mdiff, 3 * ct, a0, ALU.mult, ALU.add))
    o.done(dve.scalar_tensor_tensor(out[1], msum, -ct, d0, ALU.mult, ALU.add))
    o.wait()


FUNCTIONALS = 20


def to_points(dve, o, src, dst):
    o.done(dve.tensor_tensor(dst(0), src(0), src(2), ALU.add))
    o.done(dve.scalar_tensor_tensor(dst(1), src(2), -2.0, src(0), ALU.mult, ALU.add))
    o.wait()
    o.link(dve.tensor_tensor(dst(2), dst(0), src(1), ALU.subtract))
    o.link(dve.tensor_tensor(dst(0), dst(0), src(1), ALU.add))


def to_modes(dve, o, src, dst):
    o.done(dve.tensor_tensor(dst(0), src(0), src(2), ALU.add))
    o.done(dve.tensor_tensor(dst(1), src(0), src(2), ALU.subtract))
    o.wait()
    o.link(dve.scalar_tensor_tensor(dst(2), src(1), -2.0, dst(0), ALU.mult, ALU.add))
    o.link(dve.tensor_tensor(dst(0), dst(0), src(1), ALU.add))


def along_x(buf, n):
    v = buf[:, 0:n * T].rearrange("p (r k) -> p r k", k=G3)
    return lambda k: v[:, :, k]


def along_y(buf, n):
    v = buf[:, 0:n * T].rearrange("p (r y x) -> p r y x", y=G3, x=G3)
    return lambda k: v[:, :, k, :]


def statistics(nc, sb, ps, sem, x, con_d, pr_d, s_d, cperp):
    xb = sb("xb", [P, XB, CJ * PIX], F32)
    junk = ps("junk", [P, 5 * 512], F32)
    con = sb("st_con", [P, NC], F32)
    row_a = sb("row_a", [P, 2, CJ * 6 * W], F32)
    row_b = sb("row_b", [P, 2, CJ * 4 * W], F32)
    ysum = sb("ysum", [P, QB, CJ * 6 * W], F32)
    ymom = sb("ymom", [P, QB, CJ * 4 * W], F32)
    ytmp = sb("ytmp", [P, 9, QB * CJ * W], F32)
    yout = sb("yout", [P, QB * CJ, 5, W], F32)
    rows = QB * CJ * 5
    xsum = ytmp[:, 0:3, :].rearrange("p a b -> p (a b)")[:, 0:rows * 6].rearrange("p (r g) -> p r g", g=6)
    xmom = ytmp[:, 3:5, :].rearrange("p a b -> p (a b)")[:, 0:rows * 4].rearrange("p (r g) -> p r g", g=4)
    xtmp = sb("xtmp", [P, 9, rows], F32)
    xout = sb("xout", [P, 5, rows], F32)
    stage = sb("stage", [P, 2, CJ, QB, T], F32)
    sq_r = sb("sq_r", [P, CJ * QB * T], F32)
    zero = sb("zero", [P, CHUNK], F32)
    sumsq = sb("sumsq", [P, B, 2], F32)
    esum = sb("esum", [P, QB], F32)
    etot = sb("etot", [P, QB], F32)

    x_full = [sem(f"x_full{i}") for i in range(XB)]
    con_full = sem("st_con_full")
    x_summed = sem("x_summed")
    x_squared = sem("x_squared")
    staged = sem("staged")
    r_squared = sem("r_squared")
    stored = sem("st_stored")
    stage_free = sem("stage_free")
    zero_set = sem("zero_set")
    zero_stored = sem("zero_stored")
    pool_steps = sem("st_pool_steps")
    own = sem("st_dve_own")
    xv = x.rearrange("b (p j) h w -> b p (j h w)", p=P)

    with nc.Block() as block:
        @block.sync
        def _(sp):
            sp.dma_start(con[:], con_d).then_inc(con_full, 16)

            def load(image, i):
                sp.dma_start(xb[:, i, :], xv[bass.ds(image, 1)].rearrange("o p n -> (o p) n")).then_inc(x_full[i], 16)
            for i in range(XB):
                load(i, i)
            with sp.Fori(0, QG - 1) as g:
                for i in range(XB):
                    sp.wait_ge(x_summed, g * QB + i + 1)
                    sp.wait_ge(x_squared, FREE + (g * QB + i + 1) * 2)
                    load((g + 1) * QB + i, i)

        @block.gpsimd
        def _(pool):
            pool.sem_inc(stage_free, FREE)
            pool.wait_ge(zero_set, 1)
            for h in range(HALVES):
                for c in range(CHUNKS):
                    pool.dma_start(s_d[h, c], zero[:]).then_inc(zero_stored, 16)
            with pool.Fori(0, QG) as g:
                pool.wait_ge(staged, g + 1)
                pool.sem_inc(pool_steps, 1)
                pool.dma_start(pr_d[bass.ds(g, 1)].rearrange("o p a n -> (o p) (a n)"),
                               stage[:].rearrange("p a j b k -> p (a j b k)")).then_inc(stored, 16)
                pool.wait_ge(stored, (g + 1) * 16)
                pool.sem_inc(stage_free, 1)
            pool.wait_ge(zero_stored, 16 * HALVES * CHUNKS)
            pool.wait_ge(stored, 16 * QG)

        @block.scalar
        def _(act):
            half = CJ * PIX // 2
            act.sem_inc(x_squared, FREE)
            with act.Fori(0, QG) as g:
                for i in range(QB):
                    act.wait_ge(x_full[i], (g + 1) * 16)
                    for n in range(2):
                        act.wait_ge(x_squared, FREE + (g * QB + i) * 2 + n)
                        act.activation(junk[:, 0:half], xb[:, i, n * half:(n + 1) * half], ACT.Square,
                                       accum_out=sumsq[:, bass.ds(g * QB + i, 1), n:n + 1]).then_inc(x_squared, 1)
                act.wait_ge(staged, g + 1)
                act.activation(sq_r[:], stage[:, 0].rearrange("p j b k -> p (j b k)"), ACT.Square).then_inc(r_squared, 1)

        @block.vector
        def _(dve):
            o = Order(dve, own)
            dve.memset(zero[:], 0.0).then_inc(zero_set, 1)
            dve.wait_ge(con_full, 16)

            def image(g, i):
                dve.wait_ge(x_full[i], (g + 1) * 16)
                v = xb[:, i, :].rearrange("p (jg k w) -> p jg k w", k=4, w=W)
                vm = xb[:, i, :].rearrange("p (j g k w) -> p j g k w", g=6, k=4, w=W)[:, :, 1:5]
                a = [row_a[:, n, :].rearrange("p (r w) -> p r w", w=W) for n in range(2)]
                bb = [row_b[:, n, :].rearrange("p (j g w) -> p j g w", g=4, w=W) for n in range(2)]
                o.done(dve.tensor_tensor(a[0], v[:, :, 0, :], v[:, :, 3, :], ALU.add))
                o.done(dve.tensor_tensor(a[1], v[:, :, 1, :], v[:, :, 2, :], ALU.add))
                o.done(dve.tensor_tensor(bb[0], vm[:, :, :, 3, :], vm[:, :, :, 0, :], ALU.subtract))
                dve.tensor_tensor(bb[1], vm[:, :, :, 2, :], vm[:, :, :, 1, :], ALU.subtract).then_inc(x_summed, 1)
                o.wait()
                dve.wait_ge(x_summed, g * QB + i + 1)
                o.done(dve.tensor_tensor(ysum[:, i, :], row_a[:, 0, :], row_a[:, 1, :], ALU.add))
                o.done(dve.scalar_tensor_tensor(ymom[:, i, :], row_b[:, 0, :], 3.0, row_b[:, 1, :], ALU.mult, ALU.add))
                o.wait()

            rest = row_a[:].rearrange("p a n -> p (a n)"), row_b[:, 0, :]

            def temps(n):
                own = ytmp if n == QB * CJ * W else xtmp
                return [own[:, i, :] for i in range(9)] + [rest[0][:, i * n:(i + 1) * n] for i in range(3)] + [rest[1][:, 0:n]]

            per = QB * 5 + 2 * FUNCTIONALS + 2 + 2
            with o.loop(0, QG, per) as g:
                for i in range(QB):
                    image(g, i)
                sv = ysum[:].rearrange("p b (j g w) -> p (b j) g w", g=6, w=W)
                mv = ymom[:].rearrange("p b (j g w) -> p (b j) g w", g=4, w=W)
                functionals(dve, o, [sv[:, :, n, :] for n in range(6)], [mv[:, :, n, :] for n in range(4)], 0.0625,
                            [yout[:, :, n, :] for n in range(5)],
                            [v.rearrange("p (r w) -> p r w", w=W) for v in temps(QB * CJ * W)])
                yr = yout[:].rearrange("p r f (g e) -> p (r f) g e", e=2)
                o.done(dve.tensor_tensor(xsum, yr[:, :, :, 0], yr[:, :, :, 1], ALU.add))
                o.done(dve.tensor_tensor(xmom, yr[:, :, 1:5, 1], yr[:, :, 1:5, 0], ALU.subtract))
                o.wait()
                functionals(dve, o, [xsum[:, :, n] for n in range(6)], [xmom[:, :, n] for n in range(4)], 0.125,
                            [xout[:, n, :] for n in range(5)], temps(rows))
                dve.wait_ge(stage_free, FREE + g)
                z = xout[:].rearrange("p f (b j y) -> p f b j y", j=CJ, y=5)
                st = stage[:].rearrange("p a j b (y x) -> p a b j y x", x=G3)
                rs = con[:, C_RS:C_RS + T].rearrange("p (y x) -> p y x", x=G3)
                pscale = con[:, C_PS:C_PS + T].rearrange("p (y x) -> p y x", x=G3)

                def spread(v, n):
                    return v.unsqueeze(1).unsqueeze(1).broadcast_to([P, QB, CJ, n])
                for kx in range(G3):
                    fx = (0, 3, 4)[kx]
                    dve.tensor_tensor(st[:, 0, :, :, :, kx], z[:, kx, :, :, 0:3], spread(rs[:, :, kx], 3), ALU.mult)
                    dve.tensor_tensor(st[:, 1, :, :, 0, kx], z[:, fx, :, :, 0],
                                      pscale[:, 0:1, kx].unsqueeze(1).broadcast_to([P, QB, CJ]), ALU.mult)
                    ins = dve.tensor_tensor(st[:, 1, :, :, 1:3, kx], z[:, fx, :, :, 3:5],
                                            spread(pscale[:, 1:3, kx], 2), ALU.mult)
                ins.then_inc(staged, 1)
                dve.wait_ge(r_squared, g + 1)
                o.done(dve.tensor_reduce(esum[:], sq_r[:].rearrange("p (j b k) -> p b j k", b=QB, k=T), AX.XY, ALU.add))
                dve.wait_ge(x_squared, FREE + (g + 1) * QB * 2)
                sv2 = sumsq[:, bass.ds(g * QB, QB), :]
                o.link(dve.tensor_tensor(etot[:], sv2[:, :, 0], sv2[:, :, 1], ALU.add))
                dve.tensor_tensor(cperp[:, bass.ds(g * QB, QB)], etot[:], esum[:], ALU.subtract)


def layers(nc, sb, ps, sem, con_d, vec_d, pe_d, in_d, xp_d, dt_d, out_d, pr_d, s_d, bc_d, cperp):
    con = sb("con", [P, NC], F32)
    vec = sb("vec", [P, 2, NV], F32)
    half_cw = sb("half_cw", [P, 4 * KI], F32)
    neg_a = sb("neg_a", [P, 2, KI * STATE], F32)
    wring = sb("wring", [P, 2, CJ * P], F32)
    xy = sb("xy", [P, 2, CHUNKS * CHUNK], F32)
    ld = sb("ld", [P, 4 * CHUNK], F32)
    lds = sb("lds", [P, 2, CHUNK], F32)
    us = sb("us", [P, 2, KI * TOK], F32)
    zss = sb("zss", [P, 2, KI * TOK], F32)
    zt = sb("zt", [P, 2, TOK], F32)
    dbc = sb("dbc", [DBC, TOK], F32)
    bc = sb("bc", [P, 2 * STATE, TOK], F32)
    dA = sb("dA", [P, NDA, NS * TOK], F32)
    st = sb("st", [P, NST, NS * TOK], F32)
    wt = sb("wt", [P, TOK], F32)
    cgrp = sb("cgrp", [P, B], F32)
    small = sb("small", [P, 5, HB], F32)
    rexp = sb("rexp", [P, TOK], F32)
    ldp = [ld[:, k * CHUNK:(k + 1) * CHUNK] for k in range(2)]
    ldr = [ld[:, (2 + k) * CHUNK:(3 + k) * CHUNK] for k in range(2)]
    tok = ld[:, 0:KH * TOK]
    tok2 = ld[:, 2 * CHUNK:2 * CHUNK + KH * TOK]
    softp = ld[:, 0:KI * TOK]

    mm_ps = ps("mm_ps", [P, 2, 512], F32)
    y_ps = ps("y_ps", [P, 2, 512], F32)
    gm_ps = ps("gm_ps", [P, 512], F32)
    ge_ps = ps("ge_ps", [P, 512], F32)
    ln_ps = ps("ln_ps", [P, 512], F32)
    xp_ps = ps("xp_ps", [P, 512], F32)

    con_full = sem("con_full")
    vec_full = sem("vec_full")
    w_full = [sem(f"w_full{i}") for i in range(2)]
    pr_full = [sem(f"pr_full{i}") for i in range(2)]
    s_full = [sem(f"s_full{i}") for i in range(2)]
    s_stored = [sem(f"s_stored{i}") for i in range(2)]
    bc_stored = sem("bc_stored")
    bc_full = [sem(f"bc_full{q}") for q in range(NQ)]
    mm_done = sem("mm_done")
    mm_free = [sem(f"mm_free{i}") for i in range(2)]
    p_sum, r_sum, r_sq = sem("p_sum"), sem("r_sum"), sem("r_sq")
    ge_done = sem("ge_done")
    gn_var, gn_std = sem("gn_var"), sem("gn_std")
    pn_ready = sem("pn_ready")
    tok_points, tok_biased = sem("tok_points"), sem("tok_biased")
    ln_sum, ln_std = sem("ln_sum"), sem("ln_std")
    tok_centred, tok_sq, tok_normed = sem("tok_centred"), sem("tok_sq"), sem("tok_normed")
    h_ready = sem("h_ready")
    xs_mid, conv_tanh, u_ready, z_tanh = sem("xs_mid"), sem("conv_tanh"), sem("u_ready"), sem("z_tanh")
    xp_done, dbc_ready = sem("xp_done"), sem("dbc_ready")
    dt_out, sp_ready, delta_ready = sem("dt_out"), sem("sp_ready"), sem("delta_ready")
    dA_zero, dA_ready = sem("dA_zero"), sem("dA_ready")
    dA_free = [sem(f"dA_free{q}") for q in range(NDA)]
    sc_ready = sem("sc_ready")
    sc_used = [sem(f"sc_used{q}") for q in range(NST)]
    y_free = [sem(f"y_free{i}") for i in range(2)]
    yhat_ready = sem("yhat_ready")
    cgrp_sum = sem("cgrp_sum")
    pool_steps = sem("pool_steps")
    own_d, own_a = sem("dve_own"), sem("act_own")

    ident = con[:, C_ID:C_ID + P]
    LAST = LAYERS * HALVES - 1

    def chunk4(buf):
        return buf.rearrange("p (g j n) -> p g j n", j=JC, n=QB * T)

    def front_at(s):
        if isinstance(s, int) and s == 0:
            return 0, 0, 0
        return s * (FRONT + CJ) - CJ, s * ((FRONT + CJ) // 2) - CJ // 2, s * (W_FRONT + W_BACK) - W_BACK

    def back_at(s):
        if isinstance(s, int) and s == LAST:
            return tuple(n + d for n, d in zip(back_at(s - 1), (CJ, CJ // 2, W_BACK)))
        return (2 * FRONT + s * (FRONT + CJ), FRONT + s * ((FRONT + CJ) // 2), 2 * W_FRONT + s * (W_FRONT + W_BACK))

    def each_slot(eng, front, slot, back, loop):
        front(0, 0, 0)
        slot(0, 0, 0, None, (0, 1))
        with loop(0, LAYERS - 1) as l:
            slot(l * 2 + 1, l, 1, (l, 0), (l + 1, 0))
            slot(l * 2 + 2, l + 1, 0, (l, 1), (l + 1, 1))
        slot(LAST, LAYERS - 1, 1, (LAYERS - 1, 0), None)
        back(LAST, LAYERS - 1, 1)

    with nc.Block() as block:
        @block.sync
        def _(sp):
            def fetch(w_d, l, chunk, k, before, products=mm_done):
                if not isinstance(before, int) or before > 0:
                    sp.wait_ge(products, before)
                src = w_d[l] if isinstance(l, int) else w_d[bass.ds(l, 1)].rearrange("a c p n -> (a c) p n")
                src = src[chunk] if isinstance(chunk, int) else src[bass.ds(chunk, 1)].rearrange("a p n -> (a p) n")
                sp.dma_start(wring[0:src.shape[0], k, 0:src.shape[1]], src).then_inc(w_full[k], 16)

            def front(s, l, h):
                at = front_at(s)[0]
                for c in range(KH):
                    fetch(pe_d, l, c, c % 2, at + c - 1)
                for c in range(KI):
                    if c == XP_CHUNK:
                        fetch(xp_d, l, 0, XP_PLACE % 2, at + KH + 2 * (c - 1))
                    done = KH + 2 * (c - (c != XP_CHUNK)) if c >= 2 else KH + c - 1
                    if c == XP_CHUNK + 1:
                        fetch(in_d, l, c, IN_PLACE[c] % 2, s + 1, xp_done)
                    else:
                        fetch(in_d, l, c, IN_PLACE[c] % 2, at + done)
                fetch(dt_d, l, 0, DT_PLACE % 2, at + KH + 2 * (KI - 1))

            def back(s, l, h):
                at = back_at(s)[0]
                for c in range(CJ):
                    fetch(out_d, l, c, c % 2, at + c - 1)

            def slot(s, l, h, kk, ff):
                if kk:
                    back(s - 1, *kk)
                if ff:
                    front(s + 1, *ff)
            each_slot(sp, front, slot, back, sp.Fori)

        @block.gpsimd
        def _(pool):
            pool.dma_start(con[:], con_d).then_inc(con_full, 16)

            def move(dst, src):
                pool.sem_inc(pool_steps, 1)
                return pool.dma_start(dst, src)

            def load_s(h, c):
                move(lds[:, c % 2, :], s_d[h, c]).then_inc(s_full[c % 2], 16)

            def load_pr(h, c):
                for a, buf in ((1, ldp[c % 2]), (0, ldr[c % 2])):
                    move(buf.rearrange("p (g n) -> p g n", n=PACK),
                         pr_d[h * HG:(h + 1) * HG, :, a, c * PACK:(c + 1) * PACK].rearrange("g p n -> p g n")
                         ).then_inc(pr_full[c % 2], 16)

            def state(s, h, back, front, l_front):
                if front:
                    if back:
                        pool.wait_ge(yhat_ready, FREE + s - 1)
                    src = vec_d[l_front] if isinstance(l_front, int) else vec_d[bass.ds(l_front, 1)].rearrange("a p n -> (a p) n")
                    move(vec[:, h, :], src).then_inc(vec_full, 16)
                load_s(h, 0)
                load_s(h, 1)
                if front:
                    if not isinstance(s, int) or s > 0:
                        pool.wait_ge(delta_ready, s)
                    load_pr(h, 0)
                    load_pr(h, 1)
                for c in range(CHUNKS):
                    if back:
                        for k in range(2):
                            pool.wait_ge(mm_free[k], FREE + back_at(s - 2)[1] + (c + 1) * (JC // 2))
                        move(s_d[h, c], lds[:, c % 2, :]).then_inc(s_stored[c % 2], 16)
                        pool.wait_ge(s_stored[c % 2], ((s - 2) * 2 + c // 2 + 1) * 16)
                    if front:
                        pool.wait_ge(r_sum, s * CHUNKS + c + 1)
                        pool.wait_ge(ge_done, s * CHUNKS + c + 1)
                    if c + 2 < CHUNKS:
                        load_s(h, c + 2)
                        if front:
                            load_pr(h, c + 2)

            def spread(s, h):
                pool.wait_ge(dbc_ready, s + 1)
                move(bc_d[h], dbc[RANK:DBC, :]).then_inc(bc_stored, 16)
                pool.wait_ge(bc_stored, (s + 1) * 16)
                for q in range(NQ):
                    if not isinstance(s, int) or s > 0:
                        pool.wait_ge(sc_ready, s * STEPS - NQ + q + 1)
                    for a in range(2):
                        r = slice(a * STATE + q * NS, a * STATE + (q + 1) * NS)
                        move(bc[:, r, :], bc_d[h, r, :].unsqueeze(0).broadcast_to([P, NS, TOK])).then_inc(bc_full[q], 16)

            def front(s, l, h):
                state(s, h, False, True, l)
                spread(s, h)

            def back(s, l, h):
                state(s + 2, h, True, False, None)

            def slot(s, l, h, kk, ff):
                state(s + 1, 1 - h, kk is not None, ff is not None, ff[0] if ff else None)
                if ff:
                    spread(s + 1, 1 - h)
            each_slot(pool, front, slot, back, pool.Fori)

        @block.tensor
        def _(pe):
            for q in range(NST):
                pe.sem_inc(sc_used[q], FREE)
            pe.wait_ge(con_full, 16)
            blk = con[:, C_BLK:C_BLK + P]
            one = con[:, C_ONE:C_ONE + P]
            pe.matmul(ln_ps[:, 0:B], blk, cperp[:], start=True, stop=True).then_inc(cgrp_sum, 1)

            def product(at, use, k, ksteps, lhs, rhs):
                pe.wait_ge(mm_free[k], FREE + at[1] + use)
                for n in range(ksteps):
                    ins = pe.matmul(mm_ps[:, k, 0:TOK], lhs(n), rhs(n), start=(n == 0), stop=(n == ksteps - 1))
                ins.then_inc(mm_done, 1)

            def back_step(s, h, n):
                at = back_at(s)
                for j in on(n, BACK_STEP):
                    if j == 0:
                        pe.wait_ge(yhat_ready, FREE + s + 1)
                    pe.wait_ge(w_full[j % 2], (at[2] + j // 2 + 1) * 16)
                    product(at, j // 2, j % 2, KI, lambda i: wring[:, j % 2, i * P:(i + 1) * P],
                            lambda i: us[:, h, i * TOK:(i + 1) * TOK])

            def front_step(s, h, n):
                at = front_at(s)
                for c in on(n, SUM_STEP):
                    pe.wait_ge(p_sum, s * CHUNKS + c + 1)
                    pv = xy[:, h, c * CHUNK:(c + 1) * CHUNK].rearrange("p (g j b k) -> p g j b k", j=JC, b=QB, k=T)
                    for j in range(JC):
                        pe.matmul(gm_ps[:, 0:HB], blk, pv[:, :, j, :, 0], start=(c == 0 and j == 0),
                                  stop=(c == CHUNKS - 1 and j == JC - 1))
                    pe.wait_ge(r_sq, s * CHUNKS + c + 1)
                    rv = chunk4(ldr[c % 2])
                    for j in range(JC):
                        ins = pe.matmul(ge_ps[:, 0:TOK], blk, rv[:, :, j, :], start=(c == 0 and j == 0),
                                        stop=(c == CHUNKS - 1 and j == JC - 1))
                    ins.then_inc(ge_done, 1)
                for m in on(n, PE_STEP):
                    if m == 0:
                        pe.wait_ge(pn_ready, s + 1)
                    pe.wait_ge(w_full[m % 2], (at[2] + m // 2 + 1) * 16)
                    product(at, m // 2, m % 2, CJ, lambda i: wring[:, m % 2, i * P:(i + 1) * P],
                            lambda i: chunk4(xy[:, h, i // JC * CHUNK:(i // JC + 1) * CHUNK])[:, :, i % JC, :])
                for when, src, there in ((LN_STEP + 1, tok, tok_biased), (LN_STEP + 2, tok2, tok_sq)):
                    if n == when:
                        pe.wait_ge(there, s + 1)
                        for m in range(KH):
                            ins = pe.matmul(ln_ps[:, 0:TOK], one, src[:, m * TOK:(m + 1) * TOK], start=(m == 0),
                                            stop=(m == KH - 1))
                        ins.then_inc(ln_sum, 1)
                for i in on(n, IN_STEP):
                    c, e = i // 2, i % 2
                    if i == 0:
                        pe.wait_ge(h_ready, s + 1)
                    k = IN_PLACE[c] % 2
                    if e == 0:
                        pe.wait_ge(w_full[k], (at[2] + IN_PLACE[c] // 2 + 1) * 16)
                    product(at, (KH + i) // 2, e, KH, lambda t: wring[:, k, (e * KH + t) * P:(e * KH + t + 1) * P],
                            lambda t: tok[:, t * TOK:(t + 1) * TOK])
                if n == XP_STEP:
                    pe.wait_ge(u_ready, s + 1)
                    pe.wait_ge(w_full[XP_PLACE % 2], (at[2] + XP_PLACE // 2 + 1) * 16)
                    for t in range(KI):
                        ins = pe.matmul(xp_ps[0:DBC, 0:TOK], wring[:, XP_PLACE % 2, t * DBC:(t + 1) * DBC],
                                        us[:, h, t * TOK:(t + 1) * TOK], start=(t == 0), stop=(t == KI - 1))
                    ins.then_inc(xp_done, 1)
                for m in on(n, DT_STEP):
                    if m == 0:
                        pe.wait_ge(dbc_ready, s + 1)
                        pe.wait_ge(w_full[DT_PLACE % 2], (at[2] + DT_PLACE // 2 + 1) * 16)
                    product(at, KH // 2 + KI + m // 2, m % 2, 1, lambda t: wring[0:RANK, DT_PLACE % 2, m * P:(m + 1) * P],
                            lambda t: dbc[0:RANK, :])

            def state_sum(s, n):
                m, q = n // NQ, n % NQ
                if q == 0:
                    pe.wait_ge(y_free[m % 2], FREE + s * (KI // 2) + m // 2)
                pe.wait_ge(sc_ready, s * STEPS + n + 1)
                for t in range(NS // 2):
                    ins = pe.matmul(y_ps[:, m % 2, 0:TOK], ident, st[:, n % NST, t * TOK:(t + 1) * TOK],
                                    start=(q == 0 and t == 0), stop=(q == NQ - 1 and t == NS // 2 - 1))
                ins.then_inc(sc_used[n % NST], 1)

            def front(s, l, h):
                for n in range(STEPS):
                    front_step(s, h, n)

            def back(s, l, h):
                for n in range(STEPS):
                    back_step(s, h, n)

            def slot(s, l, h, kk, ff):
                for n in range(STEPS):
                    if kk:
                        back_step(s - 1, 1 - h, n)
                    if ff:
                        front_step(s + 1, 1 - h, n)
                    state_sum(s, n)
            each_slot(pe, front, slot, back, pe.Fori)

        @block.scalar
        def _(act):
            o = Order(act, own_a)

            def front_step(s, h, n):
                at = front_at(s)
                if n == VEC_STEP:
                    act.wait_ge(vec_full, (s + 1) * 16)
                    o.done(act.activation(half_cw[:], vec[:, h, V_CW:V_CW + 4 * KI], ACT.Copy, scale=0.5))
                    o.link(act.activation(neg_a[:, h, :], vec[:, h, V_A:V_A + KI * STATE], ACT.Exp))
                    o.link(act.activation(neg_a[:, h, :], neg_a[:, h, :], ACT.Copy, scale=-1.0))
                for c in on(n, CHUNK_STEP):
                    act.wait_ge(r_sum, s * CHUNKS + c + 1)
                    act.activation(ldr[c % 2], ldr[c % 2], ACT.Square).then_inc(r_sq, 1)
                if n == GN_STEP:
                    act.wait_ge(gn_var, s + 1)
                    act.activation(small[:, 3, :], small[:, 3, :], ACT.Sqrt).then_inc(gn_std, 1)
                if n == LN_STEP:
                    act.wait_ge(tok_points, s + 1)
                    for m in range(KH):
                        v = tok[:, m * TOK:(m + 1) * TOK]
                        ins = act.activation(v, v, ACT.Identity, bias=vec[:, h, V_PEB + m:V_PEB + m + 1])
                    ins.then_inc(tok_biased, 1)
                if n == LN_STEP + 1:
                    act.wait_ge(tok_centred, s + 1)
                    act.activation(tok2, tok, ACT.Square).then_inc(tok_sq, 1)
                if n == LN_STEP + 2:
                    act.wait_ge(ln_sum, 2 * s + 2)
                    act.activation(rexp[:], ln_ps[:, 0:TOK], ACT.Sqrt, bias=EPS).then_inc(ln_std, 1)
                    act.wait_ge(tok_normed, s + 1)
                    for m in range(KH):
                        v = tok[:, m * TOK:(m + 1) * TOK]
                        ins = act.activation(v, v, ACT.Identity, scale=vec[:, h, V_G + m:V_G + m + 1],
                                             bias=vec[:, h, V_B + m:V_B + m + 1])
                    ins.then_inc(h_ready, 1)
                for i in on(n, IN_STEP):
                    act.wait_ge(mm_done, at[0] + KH + i + 1)
                    if i < KI:
                        act.activation(us[:, h, i * TOK:(i + 1) * TOK], mm_ps[:, i % 2, 0:TOK], ACT.Identity,
                                       scale=half_cw[:, i * 3 + 1:i * 3 + 2],
                                       bias=half_cw[:, i + 3 * KI:i + 3 * KI + 1]).then_inc(xs_mid, 1)
                    else:
                        act.activation(zt[:, i % 2, :], mm_ps[:, i % 2, 0:TOK], ACT.Tanh, scale=0.5).then_inc(z_tanh, 1)
                if n == TANH_STEP:
                    for k in range(2):
                        act.wait_ge(mm_free[k], FREE + at[1] + (KH + KI) // 2)
                    act.activation(xy[:, h, 0:KI * TOK], us[:, h, :], ACT.Tanh).then_inc(conv_tanh, 1)
                if n == XP_STEP:
                    act.wait_ge(xp_done, s + 1)
                    act.activation(dbc[:], xp_ps[0:DBC, 0:TOK], ACT.Copy).then_inc(dbc_ready, 1)
                for m in on(n, DT_STEP):
                    act.wait_ge(u_ready, s + 1)
                    act.wait_ge(mm_done, at[0] + KH + 2 * KI + m + 1)
                    act.activation(xy[:, h, m * TOK:(m + 1) * TOK], mm_ps[:, m % 2, 0:TOK], ACT.Identity,
                                   bias=vec[:, h, V_DTB + m:V_DTB + m + 1]).then_inc(mm_free[m % 2], 1)
                if n == STEPS - 1:
                    for k in range(2):
                        act.wait_ge(mm_free[k], FREE + at[1] + FRONT // 2)
                    o.link(act.activation(softp, xy[:, h, 0:KI * TOK], ACT.Abs))
                    o.link(act.activation(softp, softp, ACT.Exp, scale=-1.0))
                    act.activation(softp, softp, ACT.Ln, bias=1.0).then_inc(sp_ready, 1)

            def factors(s, h, n, func, bias):
                m, q = n // NQ, n % NQ
                if n == 0:
                    act.wait_ge(dA_zero, 1)
                    act.wait_ge(delta_ready, s + 1)
                act.wait_ge(dA_free[n % NDA], FREE + s * (STEPS // NDA) + n // NDA)
                d = xy[:, h, m * TOK:(m + 1) * TOK].rearrange("p (b t) -> p b t", t=T)[:, :, 1:T]
                for t in range(NS):
                    v = dA[:, n % NDA, t * TOK:(t + 1) * TOK].rearrange("p (b t) -> p b t", t=T)[:, :, 1:T]
                    a = m * STATE + q * NS + t
                    ins = act.activation(v, d, func, bias=bias, scale=neg_a[:, h, a:a + 1])
                ins.then_inc(dA_ready, 1)

            def slot(s, l, h, kk, ff):
                def ahead(n):
                    if isinstance(l, int):
                        factors(s, h, n, *((ACT.Exp, 0.0) if l < LAYERS - 1 else (ACT.Identity, 1.0)))
                    elif h == 1:
                        factors(s, h, n, ACT.Exp, 0.0)
                    else:
                        with act.If(l < LAYERS - 1):
                            factors(s, h, n, ACT.Exp, 0.0)
                        with act.Else():
                            factors(s, h, n, ACT.Identity, 1.0)
                ahead(0)
                for n in range(STEPS):
                    if n + 1 < STEPS:
                        ahead(n + 1)
                    if ff:
                        front_step(s + 1, 1 - h, n)

            def front(s, l, h):
                for n in range(STEPS):
                    front_step(s, h, n)
            each_slot(act, front, slot, lambda *a: None, lambda a, b: o.loop(a, b, HALVES * 5))

        @block.vector
        def _(dve):
            o = Order(dve, own_d)
            for k in range(2):
                dve.sem_inc(mm_free[k], FREE)
                dve.sem_inc(y_free[k], FREE)
            dve.sem_inc(yhat_ready, FREE)
            for q in range(NDA):
                dve.sem_inc(dA_free[q], FREE)
            dve.memset(dA[:], 0.0).then_inc(dA_zero, 1)
            dve.wait_ge(con_full, 16)
            le = con[:, C_LE:C_LE + T].unsqueeze(1).broadcast_to([P, HB, T])
            en = con[:, C_EN:C_EN + T].unsqueeze(1).broadcast_to([P, MT * HB, T])
            dve.wait_ge(cgrp_sum, 1)
            o.link(dve.tensor_scalar(cgrp[:], ln_ps[:, 0:B], 1.0, None, ALU.mult))

            def images(v):
                return v.rearrange("p (b t) -> p b t", t=T)

            def read_out(at, use):
                for k in range(2):
                    dve.wait_ge(mm_free[k], FREE + at[1] + use)

            def back_step(s, h, n):
                at = back_at(s)
                for j in on(n, BACK_STEP):
                    c, k = j // JC, j % 2
                    if j % JC == 0:
                        dve.wait_ge(s_full[c % 2], ((s + 2) * (CHUNKS // 2) + c // 2 + 1) * 16)
                    dve.wait_ge(mm_done, at[0] + j + 1)
                    v = chunk4(lds[:, c % 2, :])[:, :, j % JC, :]
                    dve.tensor_tensor(v, v, mm_ps[:, k, 0:TOK].rearrange("p (g n) -> p g n", g=HG), ALU.add
                                      ).then_inc(mm_free[k], 1)

            def front_step(s, h, n, back=None):
                at = front_at(s)
                mean, esum, mm2, var, rstd = (small[:, i, :] for i in range(5))
                for c in on(n, CHUNK_STEP):
                    k = c % 2
                    dve.wait_ge(pr_full[k], (s * (CHUNKS // 2) + c // 2 + 1) * 32)
                    dve.wait_ge(s_full[k], (s * (CHUNKS // 2) + c // 2 + 1) * 16)
                    if back:
                        read_out(back, (c + 1) * (JC // 2))
                    dve.tensor_tensor(xy[:, h, c * CHUNK:(c + 1) * CHUNK], ldp[k], lds[:, k, :], ALU.add).then_inc(p_sum, 1)
                    dve.tensor_tensor(ldr[k], ldr[k], lds[:, k, :], ALU.add).then_inc(r_sum, 1)
                if n == GN_STEP:
                    dve.wait_ge(ge_done, (s + 1) * CHUNKS)
                    o.done(dve.tensor_scalar(mean, gm_ps[:, 0:HB], 1.0 / (C // GN_GROUPS), None, ALU.mult))
                    o.done(dve.tensor_reduce(esum, ge_ps[:, 0:TOK].rearrange("p (b k) -> p b k", k=T), AX.X, ALU.add))
                    o.wait()
                    o.done(dve.tensor_tensor(esum, esum, cgrp[:, h * HB:(h + 1) * HB], ALU.add))
                    o.done(dve.tensor_tensor(mm2, mean, mean, ALU.mult))
                    o.wait()
                    o.link(dve.scalar_tensor_tensor(var, mm2, -float(C // GN_GROUPS), esum, ALU.mult, ALU.add))
                    dve.tensor_scalar(var, var, 1.0 / (C // GN_GROUPS * PIX), EPS, ALU.mult, ALU.add).then_inc(gn_var, 1)
                    for c in range(CHUNKS):
                        v = xy[:, h, c * CHUNK:(c + 1) * CHUNK].rearrange("p (g j b k) -> p g j b k", j=JC, b=QB, k=T)[:, :, :, :, 0]
                        mb = mean.rearrange("p (g b) -> p g b", b=QB).unsqueeze(2).broadcast_to([P, HG, JC, QB])
                        o.done(dve.tensor_tensor(v, v, mb, ALU.subtract))
                    dve.wait_ge(gn_std, s + 1)
                    o.link(dve.reciprocal(rstd, var))
                    o.link(dve.tensor_scalar(images(rexp[:]), rstd.unsqueeze(2).broadcast_to([P, HB, T]), 1.0, None, ALU.mult))
                    for c in range(CHUNKS):
                        v = chunk4(xy[:, h, c * CHUNK:(c + 1) * CHUNK])
                        rb = rexp[:].rearrange("p (g n) -> p g n", g=HG).unsqueeze(2).broadcast_to([P, HG, JC, QB * T])
                        ins = dve.tensor_tensor(v, v, rb, ALU.mult)
                    ins.then_inc(pn_ready, 1)
                for m in on(n, PE_STEP):
                    dve.wait_ge(mm_done, at[0] + m + 1)
                    dve.tensor_tensor(images(tok[:, m * TOK:(m + 1) * TOK]), images(mm_ps[:, m % 2, 0:TOK]), le,
                                      ALU.mult).then_inc(mm_free[m % 2], 1)
                tk = tok.rearrange("p (m n) -> p m n", n=TOK)

                def over_m(v):
                    return v.unsqueeze(1).broadcast_to([P, KH, TOK])
                if n == LN_STEP:
                    read_out(at, KH // 2)
                    to_points(dve, o, along_x(tok, KH * HB), along_x(tok2, KH * HB))
                    yi, yo = along_y(tok2, KH * HB), along_y(tok, KH * HB)
                    o.done(dve.tensor_tensor(yo(0), yi(0), yi(2), ALU.add))
                    o.done(dve.scalar_tensor_tensor(yo(1), yi(2), -2.0, yi(0), ALU.mult, ALU.add))
                    o.wait()
                    o.link(dve.tensor_tensor(yo(2), yo(0), yi(1), ALU.subtract))
                    dve.tensor_tensor(yo(0), yo(0), yi(1), ALU.add).then_inc(tok_points, 1)
                if n == LN_STEP + 1:
                    dve.wait_ge(ln_sum, 2 * s + 1)
                    o.link(dve.tensor_scalar(rexp[:], ln_ps[:, 0:TOK], 1.0, None, ALU.mult))
                    dve.tensor_tensor(tk, tk, over_m(rexp[:]), ALU.subtract).then_inc(tok_centred, 1)
                if n == LN_STEP + 2:
                    dve.wait_ge(ln_std, s + 1)
                    o.link(dve.reciprocal(rexp[:], rexp[:]))
                    dve.wait_ge(tok_centred, s + 1)
                    dve.tensor_tensor(tk, tk, over_m(rexp[:]), ALU.mult).then_inc(tok_normed, 1)
                for i in on(n, IN_STEP):
                    k = i % 2
                    if i < KI:
                        dve.wait_ge(xs_mid, s * KI + i + 1)
                        uv, pv = images(us[:, h, i * TOK:(i + 1) * TOK]), images(mm_ps[:, k, 0:TOK])
                        o.link(dve.scalar_tensor_tensor(uv[:, :, 1:T], pv[:, :, 0:T - 1], half_cw[:, i * 3:i * 3 + 1],
                                                        uv[:, :, 1:T], ALU.mult, ALU.add))
                        dve.scalar_tensor_tensor(uv[:, :, 0:T - 1], pv[:, :, 1:T], half_cw[:, i * 3 + 2:i * 3 + 3],
                                                 uv[:, :, 0:T - 1], ALU.mult, ALU.add).then_inc(mm_free[k], 1)
                    else:
                        m = i - KI
                        dve.wait_ge(z_tanh, s * KI + m + 1)
                        dve.scalar_tensor_tensor(zss[:, h, m * TOK:(m + 1) * TOK], zt[:, k, :], 1.0, mm_ps[:, k, 0:TOK],
                                                 ALU.add, ALU.mult).then_inc(mm_free[k], 1)
                if n == TANH_STEP:
                    dve.wait_ge(conv_tanh, s + 1)
                    read_out(at, (KH + KI) // 2)
                    dve.scalar_tensor_tensor(us[:, h, :], xy[:, h, 0:KI * TOK], 1.0, us[:, h, :], ALU.add, ALU.mult
                                             ).then_inc(u_ready, 1)
                if n == STEPS - 1:
                    dve.wait_ge(sp_ready, s + 1)
                    v = xy[:, h, 0:KI * TOK]
                    dve.scalar_tensor_tensor(v, v, 0.0, softp, ALU.max, ALU.add).then_inc(delta_ready, 1)

            def recurrence(s, h, n):
                m, q = n // NQ, n % NQ
                tile = slice(m * TOK, (m + 1) * TOK)
                u, delta = us[:, h, :], xy[:, h, :]
                if n == 0:
                    dve.wait_ge(delta_ready, s + 1)
                    dve.wait_ge(u_ready, s + 1)
                    read_out(front_at(s), KH // 2 + KI)
                if m == 0:
                    dve.wait_ge(bc_full[q], (s + 1) * 32)
                if q == 0:
                    o.link(dve.tensor_tensor(wt[:], delta[:, tile], u[:, tile], ALU.mult))
                buf = st[:, n % NST, :]
                v = buf.rearrange("p (n t) -> p n t", t=TOK)
                dve.wait_ge(sc_used[n % NST], FREE + s * (STEPS // NST) + n // NST)
                o.link(dve.tensor_tensor(v, bc[:, q * NS:(q + 1) * NS, :],
                                         wt[:].unsqueeze(1).broadcast_to([P, NS, TOK]), ALU.mult))
                dve.wait_ge(dA_ready, s * STEPS + n + 1)
                dve.tensor_tensor_scan(buf, dA[:, n % NDA, :], buf, 0.0, ALU.mult, ALU.add).then_inc(dA_free[n % NDA], 1)
                dve.wait_ge(dA_free[n % NDA], FREE + s * (STEPS // NDA) + n // NDA + 1)
                o.link(dve.tensor_tensor(v, v, bc[:, STATE + q * NS:STATE + (q + 1) * NS, :], ALU.mult))
                dve.tensor_tensor(v[:, 0:NS // 2], v[:, 0:NS // 2], v[:, NS // 2:NS], ALU.add).then_inc(sc_ready, 1)

            def gated(s, h, m):
                tile = slice(m * TOK, (m + 1) * TOK)
                u = us[:, h, :]
                last = m * NQ + NQ - 1
                dve.wait_ge(sc_used[last % NST], FREE + s * (STEPS // NST) + last // NST + 1)
                dve.scalar_tensor_tensor(u[:, tile], u[:, tile], vec[:, h, V_D + m:V_D + m + 1], y_ps[:, m % 2, 0:TOK],
                                         ALU.mult, ALU.add).then_inc(y_free[m % 2], 1)
                dve.wait_ge(y_free[m % 2], FREE + s * (KI // 2) + m // 2 + 1)
                o.link(dve.scalar_tensor_tensor(u[:, tile], u[:, tile], 0.5, zss[:, h, tile], ALU.mult, ALU.mult))
                if m % MT == MT - 1:
                    some = slice((m + 1 - MT) * TOK, (m + 1) * TOK)
                    uv, tmp = u[:, some], xy[:, h, some]
                    to_modes(dve, o, along_x(uv, MT * HB), along_x(tmp, MT * HB))
                    to_modes(dve, o, along_y(tmp, MT * HB), along_y(uv, MT * HB))
                    if m == KI - 1:
                        dve.tensor_tensor(images(uv), images(uv), en, ALU.mult).then_inc(yhat_ready, 1)
                    else:
                        o.done(dve.tensor_tensor(images(uv), images(uv), en, ALU.mult))

            def slot(s, l, h, kk, ff):
                for n in range(STEPS):
                    recurrence(s, h, n)
                    if n % NQ == 1 and n > NQ:
                        gated(s, h, n // NQ - 1)
                    if kk:
                        back_step(s - 1, 1 - h, n)
                    if ff:
                        front_step(s + 1, 1 - h, n, back_at(s - 1) if kk else None)
                gated(s, h, KI - 1)

            def front(s, l, h):
                for n in range(STEPS):
                    front_step(s, h, n)

            def back(s, l, h):
                for n in range(STEPS):
                    back_step(s, h, n)
            per = 5 + 4 + 2 + 7 + 2 + KI + KI + 2 * STEPS + KI + 9 * (KI // MT) - 1
            each_slot(dve, front, slot, back, lambda a, b: o.loop(a, b, HALVES * per))


def apply(nc, sb, ps, sem, x, con_d, spread_d, s_d, out):
    PB = 2 * QB
    RT = PB * T
    AB = 4
    con = sb("ap_con", [P, NC], F32)
    spread = sb("ap_spread", [RT, PB, PIX], F32)
    spreadb = sb("ap_spreadb", [RT, PB, PIX], BF16)
    xa = sb("xa", [P, AB, CJ, PIX], F32)
    modes = sb("modes", [P, 2, CJ * RT], F32)
    points = sb("points", [P, CJ * RT], F32)
    turned = sb("turned", [RT, 2, C // 2], F32)
    part = sb("part", [RT, 3, C], BF16)
    acc = ps("acc", [P, 2, 4, 512], F32)

    con_full = sem("ap_con_full")
    s_full = [sem(f"ap_s_full{i}") for i in range(2)]
    x_full = [sem(f"xa_full{i}") for i in range(AB)]
    x_stored = [sem(f"xa_stored{i}") for i in range(AB)]
    spread_ready = sem("spread_ready")
    points_ready = sem("points_ready")
    turned_ps = sem("turned_ps")
    high_ready = sem("high_ready")
    acc_read = sem("acc_read")
    low_ready = sem("low_ready")
    resized = sem("resized")
    own = sem("ap_dve_own")
    xv = x.rearrange("b (p j) h w -> b p (j h w)", p=P)
    ov = out.rearrange("b (p j) h w -> b p (j h w)", p=P)
    GROUPS = B // PB
    QUADS = PB * CHUNKS + 2

    def image(v, b):
        return v[bass.ds(b, 1)].rearrange("o p n -> (o p) n")

    with nc.Block() as block:
        @block.sync
        def _(sp):
            for i in range(AB):
                sp.dma_start(xa[:, i].rearrange("p j n -> p (j n)"), image(xv, i)).then_inc(x_full[i], 16)
            with sp.Fori(0, B // AB - 1) as n:
                for i in range(AB):
                    sp.wait_ge(x_stored[i], (n + 1) * 16)
                    sp.dma_start(xa[:, i].rearrange("p j n -> p (j n)"), image(xv, (n + 1) * AB + i)).then_inc(x_full[i], 16)

        @block.gpsimd
        def _(pool):
            pool.dma_start(con[:], con_d).then_inc(con_full, 16)
            pool.dma_start(spread[:].rearrange("p b n -> p (b n)"), spread_d).then_inc(con_full, 16)

            def fetch(h, g, k):
                for gg in range(2):
                    src = s_d[h:h + 1].rearrange("o c p (g n) -> (o p) c g n", g=HG)[:, :, g * 2 + gg, :]
                    pool.dma_start(modes[:, k, :].rearrange("p (c g n) -> p c g n", c=CHUNKS, g=2)[:, :, gg, :],
                                   src).then_inc(s_full[k], 16)
            for g in range(GROUPS):
                if g >= 2:
                    pool.wait_ge(points_ready, g - 1)
                fetch(g // (GROUPS // HALVES), g % (GROUPS // HALVES), g % 2)

        @block.scalar
        def _(act):
            def store(b, i, uses):
                act.wait_ge(acc_read, uses)
                act.dma_start(image(ov, b), xa[:, i].rearrange("p j n -> p (j n)")).then_inc(x_stored[i], 16)
            with act.Fori(0, GROUPS) as g:
                for e in range(2):
                    act.wait_ge(acc_read, 2 * FREE + g * QUADS + e + 1)
                    act.wait_ge(resized, FREE + g * PB * CHUNKS)
                    act.activation(part[:, 0, e * (C // 2):(e + 1) * (C // 2)], turned[:, e, :], ACT.Copy).then_inc(high_ready, 1)
                for i in range(PB):
                    store(g * PB + i, i % AB, 2 * FREE + g * QUADS + 2 + (i + 1) * CHUNKS)
            for i in range(AB):
                act.wait_ge(x_stored[i], B // AB * 16)

        @block.tensor
        def _(pe):
            pe.sem_inc(resized, FREE)
            pe.wait_ge(con_full, 32)
            pe.wait_ge(spread_ready, 1)
            with pe.Fori(0, GROUPS) as g:
                pe.wait_ge(points_ready, g + 1)
                pv = points[:].rearrange("p (j n) -> p j n", j=CJ)
                for e in range(2):
                    pe.wait_ge(acc_read, 2 * FREE + g * QUADS + e - 1)
                    for j in range(CJ // 2):
                        jj = e * (CJ // 2) + j
                        dst = acc[0:RT, e].rearrange("p a n -> p (a n)")[:, j * P:(j + 1) * P]
                        ins = pe.matmul(dst, pv[:, jj, :], con[:, C_ID:C_ID + P], start=True, stop=True)
                    ins.then_inc(turned_ps, 1)
                pe.wait_ge(low_ready, g + 1)
                for i in range(PB):
                    for c in range(CHUNKS):
                        pe.wait_ge(acc_read, 2 * FREE + g * QUADS + 2 + i * CHUNKS + c - 1)
                        for j in range(JC):
                            for n in range(3):
                                ins = pe.matmul(acc[:, c % 2, j, 0:PIX], part[:, n, (c * JC + j) * P:(c * JC + j + 1) * P],
                                                spreadb[:, i, :], start=(n == 0), stop=(n == 2))
                        ins.then_inc(resized, 1)

        @block.vector
        def _(dve):
            o = Order(dve, own)
            dve.sem_inc(acc_read, 2 * FREE)
            dve.wait_ge(con_full, 32)
            dve.tensor_copy(spreadb[:], spread[:]).then_inc(spread_ready, 1)
            ie = con[:, C_IE:C_IE + T].unsqueeze(1).broadcast_to([P, CJ * PB, T])

            def group(g, k, uses):
                dve.wait_ge(s_full[k], uses * 32)
                m = modes[:, k, :]
                v = m.rearrange("p (r t) -> p r t", t=T)
                o.link(dve.tensor_tensor(v, v, ie, ALU.mult))
                to_points(dve, o, along_x(m, CJ * PB), along_x(points, CJ * PB))
                yi, yo = along_y(points, CJ * PB), along_y(m, CJ * PB)
                to_points(dve, o, yi, yo)
                pv = points[:].rearrange("p (c j g n) -> p c g j n", c=CHUNKS, j=JC, g=2)
                mv = m.rearrange("p (c g j n) -> p c g j n", c=CHUNKS, g=2, j=JC)
                for c in range(CHUNKS):
                    ins = dve.tensor_copy(pv[:, c], mv[:, c])
                ins.then_inc(points_ready, 1)
                for e in range(2):
                    dve.wait_ge(turned_ps, g * 2 + e + 1)
                    dve.tensor_scalar(turned[:, e, :], acc[0:RT, e].rearrange("p a n -> p (a n)")[:, 0:C // 2],
                                      1.0, None, ALU.mult).then_inc(acc_read, 1)
                    dve.wait_ge(acc_read, 2 * FREE + g * QUADS + e + 1)
                    dve.wait_ge(high_ready, g * 2 + e + 1)
                    cols = slice(e * (C // 2), (e + 1) * (C // 2))
                    o.link(dve.tensor_tensor(turned[:, e, :], turned[:, e, :], part[:, 0, cols], ALU.subtract))
                    o.link(dve.tensor_scalar(part[:, 1, cols], turned[:, e, :], 1.0, None, ALU.mult))
                    ins = dve.tensor_tensor(part[:, 2, cols], turned[:, e, :], part[:, 1, cols], ALU.subtract)
                ins.then_inc(low_ready, 1)
                for i in range(PB):
                    dve.wait_ge(x_full[i % AB], (g * (PB // AB) + i // AB + 1) * 16)
                    for c in range(CHUNKS):
                        dve.wait_ge(resized, FREE + (g * PB + i) * CHUNKS + c + 1)
                        v = xa[:, i % AB, c * JC:(c + 1) * JC, :]
                        dve.tensor_tensor(v, v, acc[:, c % 2, :, 0:PIX], ALU.add).then_inc(acc_read, 1)

            with o.loop(0, GROUPS // 2, 2 * (1 + 8 + 4)) as i:
                for k in range(2):
                    group(i * 2 + k, k, i + 1)


def program(nc, t, out):
    ctx = ExitStack()
    with ctx:
        cperp = ctx.enter_context(nc.sbuf_tensor("cperp", [P, B], F32))
        pr_d = nc.dram_tensor("pr_scratch", (QG, P, 2, CJ * QB * T), F32, kind="Internal").ap()
        s_d = nc.dram_tensor("s_scratch", (HALVES, CHUNKS, P, CHUNK), F32, kind="Internal").ap()
        bc_d = nc.dram_tensor("bc_scratch", (HALVES, 2 * STATE, TOK), F32, kind="Internal").ap()

        def phase(build, *args):
            with ExitStack() as own:
                build(nc, lambda n, shape, dt: own.enter_context(nc.sbuf_tensor(n, shape, dt)),
                      lambda n, shape, dt: own.enter_context(nc.psum_tensor(n, shape, dt)),
                      lambda n: ctx.enter_context(nc.semaphore(n)), *args)
        phase(statistics, t["x"], t["con"], pr_d, s_d, cperp)
        phase(layers, t["con"], t["vec"], t["pe"], t["inp"], t["xp"], t["dt"], t["outw"], pr_d, s_d, bc_d, cperp)
        phase(apply, t["x"], t["con"], t["spread"], s_d, out)


def kernel(**inputs):
    import concourse.bacc as _bacc
    from concourse.bass_utils import run_bass_kernel_spmd as _run

    def layer(l):
        new = {"pe_W": "pe_w", "in_W": "in_w", "xproj_W": "xproj_w", "dt_W": "dtproj_w", "dt_b": "dtproj_b", "out_W": "out_w"}
        pre = f"L{l}_conv_"
        return {new.get(n[len(pre):], n[len(pre):]): np.asarray(v) for n, v in inputs.items() if n.startswith(pre)}

    ls = [layer(l) for l in range(LAYERS)]

    def cols(v, n):
        return v.reshape(n, P, -1).transpose(1, 0, 2).reshape(P, -1)

    con, spread = constants()
    arrays = {
        "x": np.asarray(inputs["x"]),
        "con": con,
        "spread": spread.reshape(2 * QB * T, -1),
        "vec": np.stack([np.concatenate([cols(w["pe_b"], KH), cols(w["ln_g"], KH), cols(w["ln_b"], KH),
                                         cols(w["conv_w"], KI), cols(w["conv_b"], KI), cols(w["dtproj_b"], KI),
                                         cols(w["D_param"], KI), cols(w["A_log"], KI)], axis=1) for w in ls]),
        "pe": np.stack([w["pe_w"].reshape(P, CJ, KH, P).transpose(2, 0, 1, 3).reshape(KH, P, CJ * P) for w in ls]),
        "inp": np.stack([w["in_w"].reshape(KH, P, KI, 2, P).transpose(2, 1, 3, 0, 4).reshape(KI, P, 2 * KH * P) for w in ls]),
        "xp": np.stack([w["xproj_w"].reshape(KI, P, DBC).transpose(1, 0, 2).reshape(1, P, KI * DBC) for w in ls]),
        "dt": np.stack([w["dtproj_w"][None] for w in ls]),
        "outw": np.stack([w["out_w"].reshape(KI, P, P, CJ).transpose(3, 1, 0, 2).reshape(CJ, P, KI * P) for w in ls]),
    }
    nc = _bacc.Bacc("TRN2", target_bir_lowering=False, num_devices=1)
    t = {n: nc.dram_tensor(f"{n}_dram", a.shape, mybir.dt.from_np(a.dtype), kind="ExternalInput").ap() for n, a in arrays.items()}
    out = nc.dram_tensor("out_dram", (B, C, H, W), F32, kind="ExternalOutput").ap()
    program(nc, t, out)
    r = _run(nc, [{f"{n}_dram": np.ascontiguousarray(a) for n, a in arrays.items()}], core_ids=[0])
    return r.results[0]["out_dram"]
```

```python
from contextlib import ExitStack

import numpy as np

import concourse.bass as bass
from concourse import mybir

ALU = mybir.AluOpType
ACT = mybir.ActivationFunctionType
AX = mybir.AxisListType
F32 = mybir.dt.float32

P = 128
LAYERS = 4
B, C, H, W = 64, 2048, 24, 12
PIX = H * W
G3 = 3
T = G3 * G3
HID, INNER, STATE, RANK = 768, 1536, 16, 48
EPS = 1e-5
GN_GROUPS = 32
CJ = C // P
KH = HID // P
KI = INNER // P
DBC = RANK + 2 * STATE
HALVES = 2
HB = B // HALVES
TOK = HB * T
QB = 4
QG = B // QB
HG = HB // QB
CHUNKS = 4
JC = CJ // CHUNKS
CHUNK = JC * TOK
PACK = JC * QB * T
NQ = 4
NS = STATE // NQ
NDA, NST = 2, 4
STEPS = KI * NQ
MB = 4
NZ = 4
MT = 4
XB = QB

FREE = 1

V_PEB, V_G, V_B = 0, KH, 2 * KH
V_CW = 3 * KH
V_CB = V_CW + 3 * KI
V_DTB = V_CB + KI
V_D = V_DTB + KI
V_A = V_D + KI
NV = V_A + KI * STATE

C_ID, C_BLK, C_ONE = 0, P, 2 * P
C_RS, C_PS, C_LE, C_EN, C_IE = (3 * P + T * n for n in range(5))
NC = 3 * P + 5 * T


def interpolation(n_out):
    src = np.clip((np.arange(n_out) + 0.5) * (G3 / n_out) - 0.5, 0.0, G3 - 1.0)
    i0 = np.minimum(np.floor(src).astype(int), G3 - 1)
    i1 = np.minimum(i0 + 1, G3 - 1)
    r = np.zeros((n_out, G3))
    r[np.arange(n_out), i0] += 1 - (src - i0)
    r[np.arange(n_out), i1] += src - i0
    return r


def constants():
    u = np.array([[1.0, 1, 1], [1, 0, -1], [1, -2, 1]])
    n1 = (u * u).sum(1)
    ry, rx = interpolation(H), interpolation(W)
    gy = ((ry @ u.T) ** 2).sum(0)
    gx = ((rx @ u.T) ** 2).sum(0)
    py = np.kron(np.eye(G3), np.ones((1, H // G3))) / (H // G3)
    px = np.kron(np.eye(G3), np.ones((1, W // G3))) / (W // G3)
    ly = np.array([(py @ ry @ u[k]) @ u[k] / n1[k] for k in range(G3)])
    lx = np.array([(px @ rx @ u[k]) @ u[k] / n1[k] for k in range(G3)])
    e = np.sqrt(np.outer(gy, gx)).ravel()
    lam = np.outer(ly, lx).ravel()
    n = np.outer(n1, n1).ravel()
    con = np.zeros((P, NC), np.float32)
    con[:, C_ID:C_ID + P] = np.eye(P)
    lanes = P // GN_GROUPS
    con[:, C_BLK:C_BLK + P] = np.kron(np.eye(GN_GROUPS), np.ones((lanes, lanes)))
    con[:, C_ONE:C_ONE + P] = 1.0 / HID
    con[:, C_RS:C_RS + T] = 1 / e
    con[:, C_PS:C_PS + T] = e / (lam * n * (PIX // T))
    con[:, C_LE:C_LE + T] = lam / e
    con[:, C_EN:C_EN + T] = e / n
    con[:, C_IE:C_IE + T] = 1 / e
    rmat = np.kron(ry, rx).T
    spread = np.zeros((2 * QB * T, 2 * QB, PIX), np.float32)
    for i in range(2 * QB):
        spread[i * T:(i + 1) * T, i] = rmat
    return con, spread


BACK_STEP = [0, 1, 2, 4, 5, 6, 7, 9, 10, 11, 12, 13, 14, 15, 17, 18]
CHUNK_STEP = [BACK_STEP[c * JC + JC - 1] + 1 for c in range(CHUNKS)]
SUM_STEP = [n + 1 for n in CHUNK_STEP]
GN_STEP = SUM_STEP[-1] + 1
VEC_STEP = GN_STEP
PE_STEP = [GN_STEP + n for n in (2, 3, 5, 6, 8, 9)]
LN_STEP = PE_STEP[-1] + 1
IN_STEP = [LN_STEP + n for n in (3, 4, 5, 5, 6, 8, 9, 10, 10, 11, 11, 12)]
TANH_STEP = IN_STEP[-1] + 1
XP_STEP = TANH_STEP + 1
DT_STEP = [[XP_STEP + 1, 6, 19][m // MT] for m in range(KI)]
Z_STEP = [n for n in (3, 8, 16, GN_STEP + 1, GN_STEP + 7, LN_STEP + 7) for _ in range(2)]
assert DT_STEP[0] < STEPS - 1
GATE_STEP = 2
assert all((m - NZ + 1) * NQ + GATE_STEP < n < (m + 1) * NQ + GATE_STEP - 2 for m, n in enumerate(Z_STEP))


def on(n, steps):
    return [i for i, at in enumerate(steps) if at == n]


class Plan:

    def __init__(self, back, here, front):
        self.steps = []
        for n in range(STEPS):
            todo = []
            if back:
                todo += [("out", j) for j in on(n, BACK_STEP)]
            if here:
                todo += [("dt", m) for m in on(n, DT_STEP) if m >= MT]
            if front:
                todo += [("pe", m) for m in on(n, PE_STEP)]
                todo += [("in", i) for i in on(n, IN_STEP)]
                todo += [("xp", i) for i in range(2) if n == XP_STEP]
                todo += [("dt", m) for m in on(n, DT_STEP) if m < MT]
            if here:
                todo += [("z", m) for m in on(n, Z_STEP)]
            self.steps.append(todo)
        every = [e for todo in self.steps for e in todo]
        self.product = {e: i for i, e in enumerate(e for e in every if e[0] != "xp")}
        self.chunks = [e for e in every if e[0] in ("out", "pe", "xp") or (e[0] in ("in", "z") and e[1] % 2 == 0)]
        self.chunk = {e: i for i, e in enumerate(self.chunks)}
        assert len(self.chunks) % 2 == 0


FIRST, SLOT_0, MIDDLE, SLOT_LAST, ENDING = (Plan(*which) for which in (
    (False, False, True), (False, True, True), (True, True, True), (True, True, False), (True, False, False)))
ROUND = 2 * len(MIDDLE.product), 2 * len(MIDDLE.chunks)
assert ROUND[0] % MB == 0


class Order:

    def __init__(self, eng, sem):
        self.eng, self.sem, self.base, self.k = eng, sem, 0, 0

    def done(self, ins):
        ins.then_inc(self.sem, 1)
        self.k += 1

    def wait(self):
        self.eng.wait_ge(self.sem, self.base + self.k)

    def link(self, ins):
        self.done(ins)
        self.wait()

    def loop(self, start, end, per):
        return _OrderLoop(self, start, end, per)


class _OrderLoop:
    def __init__(self, order, start, end, per):
        self.o, self.start, self.end, self.per = order, start, end, per

    def __enter__(self):
        o = self.o
        self.base, self.k = o.base, o.k
        self.fori = o.eng.Fori(self.start, self.end)
        i = self.fori.__enter__()
        o.base, o.k = self.base + self.k + (i - self.start) * self.per, 0
        return i

    def __exit__(self, *e):
        o = self.o
        if e[0] is None:
            assert o.k == self.per, (o.k, self.per)
        self.fori.__exit__(*e)
        o.base, o.k = self.base, self.k + (self.end - self.start) * self.per


def functionals(dve, o, S, M, ct, out, tmp, freed=None):
    a0, a1, a2, d0, d1, d2, m01, m23, a01, aw, dw, mdiff, msum = tmp
    for g, (a, d) in enumerate(((a0, d0), (a1, d1), (a2, d2))):
        o.done(dve.tensor_tensor(a, S[g], S[5 - g], ALU.add))
        o.done(dve.tensor_tensor(d, S[g], S[5 - g], ALU.subtract))
    o.done(dve.tensor_tensor(m01, M[0], M[1], ALU.add))
    o.done(dve.tensor_tensor(m23, M[2], M[3], ALU.add))
    o.wait()
    ins = dve.tensor_tensor(a01, a0, a1, ALU.add)
    if freed:
        ins.then_inc(freed[0], 1)
    else:
        o.done(ins)
    o.done(dve.scalar_tensor_tensor(aw, a1, 0.25, a0, ALU.mult, ALU.add))
    o.done(dve.tensor_tensor(out[3], d0, d1, ALU.add))
    o.done(dve.scalar_tensor_tensor(dw, d1, 0.75, d0, ALU.mult, ALU.add))
    o.done(dve.tensor_tensor(mdiff, m23, m01, ALU.subtract))
    o.done(dve.tensor_tensor(msum, m23, m01, ALU.add))
    o.wait()
    if freed:
        dve.wait_ge(*freed)
    o.done(dve.tensor_tensor(out[0], a01, a2, ALU.add))
    o.done(dve.scalar_tensor_tensor(out[4], a2, -2.0, a01, ALU.mult, ALU.add))
    o.done(dve.scalar_tensor_tensor(a0, a2, -1.25, aw, ALU.mult, ALU.add))
    o.done(dve.scalar_tensor_tensor(d0, d2, 0.25, dw, ALU.mult, ALU.add))
    o.wait()
    o.done(dve.scalar_tensor_tensor(out[2], mdiff, 3 * ct, a0, ALU.mult, ALU.add))
    o.done(dve.scalar_tensor_tensor(out[1], msum, -ct, d0, ALU.mult, ALU.add))
    o.wait()


FUNCTIONALS = 20


def to_points(dve, o, src, dst):
    o.done(dve.tensor_tensor(dst(0), src(0), src(2), ALU.add))
    o.done(dve.scalar_tensor_tensor(dst(1), src(2), -2.0, src(0), ALU.mult, ALU.add))
    o.wait()
    o.link(dve.tensor_tensor(dst(2), dst(0), src(1), ALU.subtract))
    o.link(dve.tensor_tensor(dst(0), dst(0), src(1), ALU.add))


def to_modes(dve, o, src, dst):
    o.done(dve.tensor_tensor(dst(0), src(0), src(2), ALU.add))
    o.done(dve.tensor_tensor(dst(1), src(0), src(2), ALU.subtract))
    o.wait()
    o.link(dve.scalar_tensor_tensor(dst(2), src(1), -2.0, dst(0), ALU.mult, ALU.add))
    o.link(dve.tensor_tensor(dst(0), dst(0), src(1), ALU.add))


def along_x(buf, n):
    v = buf[:, 0:n * T].rearrange("p (r k) -> p r k", k=G3)
    return lambda k: v[:, :, k]


def along_y(buf, n):
    v = buf[:, 0:n * T].rearrange("p (r y x) -> p r y x", y=G3, x=G3)
    return lambda k: v[:, :, k, :]


def statistics(nc, sb, ps, sem, x, con_d, pr_d, s_d, cperp):
    xb = sb("xb", [P, XB, CJ * PIX], F32)
    junk = sb("junk", [P, CJ * PIX // 2], F32)
    sums = ps("sums", [P, 2, CHUNKS, 512], F32)
    con = sb("st_con", [P, NC], F32)
    row_b = sb("row_b", [P, 2, CJ * 4 * W], F32)
    ysum = sb("ysum", [P, 2, QB, CJ * 6 * W], F32)
    ymom = sb("ymom", [P, QB, CJ * 4 * W], F32)
    ytmp = sb("ytmp", [P, 9, QB * CJ * W], F32)
    yout = sb("yout", [P, QB * CJ, 5, W], F32)
    rows = QB * CJ * 5
    xsum = ytmp[:, 0:3, :].rearrange("p a b -> p (a b)")[:, 0:rows * 6].rearrange("p (r g) -> p r g", g=6)
    xmom = ytmp[:, 3:5, :].rearrange("p a b -> p (a b)")[:, 0:rows * 4].rearrange("p (r g) -> p r g", g=4)
    xtmp = sb("xtmp", [P, 9, rows], F32)
    xout = sb("xout", [P, 5, rows], F32)
    stage = sb("stage", [P, 2, CJ, QB, T], F32)
    sq_r = sb("sq_r", [P, CJ * QB * T], F32)
    zero = sb("zero", [P, CHUNK // 2], F32)
    sumsq = sb("sumsq", [P, B, 2], F32)
    esum = sb("esum", [P, QB], F32)
    etot = sb("etot", [P, QB], F32)

    x_full = [sem(f"x_full{i}") for i in range(XB)]
    con_full = sem("st_con_full")
    x_moments = sem("x_moments")
    x_squared = sem("x_squared")
    x_summed = sem("x_summed")
    ysum_full = sem("ysum_full")
    ysum_free = sem("ysum_free")
    staged = sem("staged")
    r_squared = sem("r_squared")
    stored = sem("st_stored")
    stage_free = sem("stage_free")
    zero_set = sem("zero_set")
    zero_stored = sem("zero_stored")
    pool_steps = sem("st_pool_steps")
    own = sem("st_dve_own")
    xv = x.rearrange("b (p j) h w -> b p (j h w)", p=P)

    with nc.Block() as block:
        @block.sync
        def _(sp):
            sp.dma_start(con[:], con_d).then_inc(con_full, 16)

            def load(image, i):
                sp.dma_start(xb[:, i, :], xv[bass.ds(image, 1)].rearrange("o p n -> (o p) n")).then_inc(x_full[i], 16)
            for i in range(XB):
                load(i, i)
            with sp.Fori(0, QG - 1) as g:
                for i in range(XB):
                    read = 2 * FREE + g * QB + i + 1
                    sp.wait_ge(x_moments, read)
                    sp.wait_ge(ysum_full, read)
                    load((g + 1) * QB + i, i)

        @block.gpsimd
        def _(pool):
            pool.sem_inc(stage_free, FREE)
            pool.wait_ge(zero_set, 1)
            for h in range(HALVES):
                for c in range(CHUNKS):
                    for part in range(2):
                        pool.dma_start(s_d[h, c, :, part * (CHUNK // 2):(part + 1) * (CHUNK // 2)], zero[:]).then_inc(zero_stored, 16)
            with pool.Fori(0, QG) as g:
                pool.wait_ge(staged, g + 1)
                pool.sem_inc(pool_steps, 1)
                pool.dma_start(pr_d[bass.ds(g, 1)].rearrange("o p a n -> (o p) (a n)"),
                               stage[:].rearrange("p a j b k -> p (a j b k)")).then_inc(stored, 16)
                pool.wait_ge(stored, (g + 1) * 16)
                pool.sem_inc(stage_free, 1)
            pool.wait_ge(zero_stored, 16 * HALVES * CHUNKS * 2)
            pool.wait_ge(stored, 16 * QG)

        @block.tensor
        def _(pe):
            pe.wait_ge(con_full, 16)
            with pe.Fori(0, QG) as g:
                for i in range(QB):
                    pe.wait_ge(x_full[i], (g + 1) * 16)
                    pe.wait_ge(ysum_full, 2 * FREE + g * QB + i - 1)
                    v = xb[:, i, :].rearrange("p (c jg k w) -> p c jg k w", c=CHUNKS, k=4, w=W)
                    for c in range(CHUNKS):
                        for k in range(4):
                            ins = pe.matmul(sums[:, i % 2, c, 0:JC * 6 * W], con[:, C_ID:C_ID + P], v[:, c, :, k, :],
                                            start=(k == 0), stop=(k == 3))
                    ins.then_inc(x_summed, 1)

        @block.scalar
        def _(act):
            half = CJ * PIX // 2
            act.sem_inc(x_squared, FREE)
            act.sem_inc(ysum_full, 2 * FREE)
            def images(g, k):
                for i in range(QB):
                    act.wait_ge(x_full[i], (g + 1) * 16)
                    for n in range(2):
                        act.wait_ge(x_squared, FREE + (g * QB + i) * 2 + n)
                        act.activation(junk[:, 0:half], xb[:, i, n * half:(n + 1) * half], ACT.Square,
                                       accum_out=sumsq[:, bass.ds(g * QB + i, 1), n:n + 1]).then_inc(x_squared, 1)
                    act.wait_ge(x_squared, FREE + (g * QB + i + 1) * 2)
                    if i == 0:
                        act.wait_ge(ysum_free, FREE + g)
                    act.wait_ge(x_summed, g * QB + i + 1)
                    act.activation(ysum[:, k, i, :].rearrange("p (c n) -> p c n", c=CHUNKS), sums[:, i % 2, :, 0:JC * 6 * W],
                                   ACT.Copy).then_inc(ysum_full, 1)

            def square(g):
                act.wait_ge(staged, g + 1)
                act.activation(sq_r[:], stage[:, 0].rearrange("p j b k -> p (j b k)"), ACT.Square).then_inc(r_squared, 1)

            images(0, 0)
            with act.Fori(0, QG // 2 - 1) as n:
                for k in range(2):
                    images(n * 2 + k + 1, 1 - k)
                    square(n * 2 + k)
            images(QG - 1, 1)
            square(QG - 2)
            square(QG - 1)

        @block.vector
        def _(dve):
            o = Order(dve, own)
            dve.memset(zero[:], 0.0).then_inc(zero_set, 1)
            dve.wait_ge(con_full, 16)

            def image(g, i):
                dve.wait_ge(x_full[i], (g + 1) * 16)
                vm = xb[:, i, :].rearrange("p (j g k w) -> p j g k w", g=6, k=4, w=W)[:, :, 1:5]
                bb = [row_b[:, n, :].rearrange("p (j g w) -> p j g w", g=4, w=W) for n in range(2)]
                o.done(dve.tensor_tensor(bb[0], vm[:, :, :, 3, :], vm[:, :, :, 0, :], ALU.subtract))
                dve.tensor_tensor(bb[1], vm[:, :, :, 2, :], vm[:, :, :, 1, :], ALU.subtract).then_inc(x_moments, 1)
                o.wait()
                dve.wait_ge(x_moments, 2 * FREE + g * QB + i + 1)
                o.done(dve.scalar_tensor_tensor(ymom[:, i, :], row_b[:, 0, :], 3.0, row_b[:, 1, :], ALU.mult, ALU.add))
                o.wait()

            def temps(buf, moments, n):
                v = [buf[:, i, :] for i in range(9)] + [row_b[:, 0, 0:n]] + [moments[:, i * n:(i + 1) * n] for i in range(3)]
                return v[0:8] + v[10:13] + v[8:10]

            xmom_flat = ytmp[:, 3:5, :].rearrange("p a b -> p (a b)")

            per = QB * 2 + 2 * FUNCTIONALS - 1 + 2 + 2
            dve.sem_inc(ysum_free, 2 * FREE)
            dve.sem_inc(x_moments, 2 * FREE)

            def group(g, k, following):
                dve.wait_ge(ysum_full, 2 * FREE + (g + 1) * QB)
                sv = ysum[:, k].rearrange("p b (j g w) -> p (b j) g w", g=6, w=W)
                mv = ymom[:].rearrange("p b (j g w) -> p (b j) g w", g=4, w=W)
                functionals(dve, o, [sv[:, :, n, :] for n in range(6)], [mv[:, :, n, :] for n in range(4)], 0.0625,
                            [yout[:, :, n, :] for n in range(5)],
                            [v.rearrange("p (r w) -> p r w", w=W)
                             for v in temps(ytmp, ymom[:].rearrange("p b n -> p (b n)"), QB * CJ * W)],
                            (ysum_free, 2 * FREE + g + 1))
                yr = yout[:].rearrange("p r f (g e) -> p (r f) g e", e=2)
                o.done(dve.tensor_tensor(xsum, yr[:, :, :, 0], yr[:, :, :, 1], ALU.add))
                o.done(dve.tensor_tensor(xmom, yr[:, :, 1:5, 1], yr[:, :, 1:5, 0], ALU.subtract))
                o.wait()
                functionals(dve, o, [xsum[:, :, n] for n in range(6)], [xmom[:, :, n] for n in range(4)], 0.125,
                            [xout[:, n, :] for n in range(5)], temps(xtmp, xmom_flat, rows))
                dve.wait_ge(stage_free, FREE + g)
                z = xout[:].rearrange("p f (b j y) -> p f b j y", j=CJ, y=5)
                st = stage[:].rearrange("p a j b (y x) -> p a b j y x", x=G3)
                rs = con[:, C_RS:C_RS + T].rearrange("p (y x) -> p y x", x=G3)
                pscale = con[:, C_PS:C_PS + T].rearrange("p (y x) -> p y x", x=G3)

                def spread(v, n):
                    return v.unsqueeze(1).unsqueeze(1).broadcast_to([P, QB, CJ, n])
                for kx in range(G3):
                    fx = (0, 3, 4)[kx]
                    dve.tensor_tensor(st[:, 0, :, :, :, kx], z[:, kx, :, :, 0:3], spread(rs[:, :, kx], 3), ALU.mult)
                    dve.tensor_tensor(st[:, 1, :, :, 0, kx], z[:, fx, :, :, 0],
                                      pscale[:, 0:1, kx].unsqueeze(1).broadcast_to([P, QB, CJ]), ALU.mult)
                    ins = dve.tensor_tensor(st[:, 1, :, :, 1:3, kx], z[:, fx, :, :, 3:5],
                                            spread(pscale[:, 1:3, kx], 2), ALU.mult)
                ins.then_inc(staged, 1)
                if following:
                    for i in range(QB):
                        image(g + 1, i)
                dve.wait_ge(r_squared, g + 1)
                o.done(dve.tensor_reduce(esum[:], sq_r[:].rearrange("p (j b k) -> p b j k", b=QB, k=T), AX.XY, ALU.add))
                dve.wait_ge(x_squared, FREE + (g + 1) * QB * 2)
                sv2 = sumsq[:, bass.ds(g * QB, QB), :]
                o.link(dve.tensor_tensor(etot[:], sv2[:, :, 0], sv2[:, :, 1], ALU.add))
                dve.tensor_tensor(cperp[:, bass.ds(g * QB, QB)], etot[:], esum[:], ALU.subtract)

            for i in range(QB):
                image(0, i)
            with o.loop(0, QG // 2 - 1, 2 * per) as n:
                for k in range(2):
                    group(n * 2 + k, k, True)
            group(QG - 2, 0, True)
            group(QG - 1, 1, False)


def layers(nc, sb, ps, sem, con_d, vec_d, pe_d, in_d, xp_d, dt_d, out_d, pr_d, s_d, bc_d, cperp):
    con = sb("con", [P, NC], F32)
    vec = sb("vec", [P, 2, NV], F32)
    half_cw = sb("half_cw", [P, 4 * KI], F32)
    neg_a = sb("neg_a", [P, 2, KI * STATE], F32)
    wring = sb("wring", [P, 2, CJ * P], F32)
    dtw = sb("dtw", [RANK, INNER], F32)
    xy = sb("xy", [P, 2, CHUNKS * CHUNK], F32)
    ld = sb("ld", [P, 4 * CHUNK], F32)
    lds = sb("lds", [P, 2, CHUNK], F32)
    us = sb("us", [P, 2, KI * TOK], F32)
    hid = sb("hid", [P, 2, KH * TOK], F32)
    zs = sb("zs", [P, NZ, TOK], F32)
    dbc = sb("dbc", [DBC, TOK], F32)
    softp = sb("softp", [P, MT * TOK], F32)
    bc = sb("bc", [P, 2 * STATE, TOK], F32)
    dA = sb("dA", [P, NDA, NS * TOK], F32)
    st = sb("st", [P, NST, NS * TOK], F32)
    wt = sb("wt", [P, TOK], F32)
    cgrp = sb("cgrp", [P, B], F32)
    small = sb("small", [P, 5, HB], F32)
    rexp = sb("rexp", [P, TOK], F32)
    ldp = [ld[:, k * CHUNK:(k + 1) * CHUNK] for k in range(2)]
    ldr = [ld[:, (2 + k) * CHUNK:(3 + k) * CHUNK] for k in range(2)]
    tok = ld[:, 0:KH * TOK]
    tok2 = ld[:, 2 * CHUNK:2 * CHUNK + KH * TOK]

    mm_ps = ps("mm_ps", [P, MB, 512], F32)
    y_ps = ps("y_ps", [P, 2, 512], F32)
    gm_ps = ps("gm_ps", [P, 512], F32)[:, 0:HB]
    ln_ps = ps("ln_ps", [P, 512], F32)
    ge_ps = ln_ps[:, 0:TOK]
    xp_ps = ln_ps

    con_full = sem("con_full")
    vec_full = sem("vec_full")
    w_full = [sem(f"w_full{i}") for i in range(2)]
    pr_full = [sem(f"pr_full{i}") for i in range(2)]
    s_full = [sem(f"s_full{i}") for i in range(2)]
    s_stored = [sem(f"s_stored{i}") for i in range(2)]
    bc_stored = sem("bc_stored")
    bc_full = [sem(f"bc_full{q}") for q in range(NQ)]
    mm_done = sem("mm_done")
    mm_free = [sem(f"mm_free{i}") for i in range(MB)]
    p_sum, r_sum, r_sq = sem("p_sum"), sem("r_sum"), sem("r_sq")
    ge_done = sem("ge_done")
    gn_var, gn_std = sem("gn_var"), sem("gn_std")
    pn_ready = sem("pn_ready")
    tok_points, tok_biased = sem("tok_points"), sem("tok_biased")
    ln_sum, ln_std = sem("ln_sum"), sem("ln_std")
    tok_centred, tok_sq, tok_normed = sem("tok_centred"), sem("tok_sq"), sem("tok_normed")
    h_ready = sem("h_ready")
    xs_mid, conv_tanh, u_ready = sem("xs_mid"), sem("conv_tanh"), sem("u_ready")
    z_tanh = sem("z_tanh")
    xp_done, dbc_ready = sem("xp_done"), sem("dbc_ready")
    dtw_full = sem("dtw_full")
    sp_ready, delta_ready = sem("sp_ready"), sem("delta_ready")
    dA_zero, dA_ready = sem("dA_zero"), sem("dA_ready")
    dA_free = [sem(f"dA_free{q}") for q in range(NDA)]
    driven = sem("driven")
    sc_ready = sem("sc_ready")
    sc_used = [sem(f"sc_used{q}") for q in range(NST)]
    y_free = [sem(f"y_free{i}") for i in range(2)]
    yhat_ready = sem("yhat_ready")
    cgrp_sum = sem("cgrp_sum")
    pool_steps = sem("pool_steps")
    own_d, own_a = sem("dve_own"), sem("act_own")

    ident = con[:, C_ID:C_ID + P]
    LAST = LAYERS * HALVES - 1
    GROUPS = KI // MT

    def chunk4(buf):
        return buf.rearrange("p (g j n) -> p g j n", j=JC, n=QB * T)

    class Slot:

        def __init__(self, plan, s, l, h, before, rounds, back, here, front):
            self.plan, self.s, self.l, self.h = plan, s, l, h
            self.products, self.chunks = before[0], before[1] // 2 + rounds * ROUND[1] // 2
            self.rounds, self.uses = rounds * ROUND[0], rounds * (ROUND[0] // MB)
            self.back, self.here, self.front = back, here, front

        def made(self, *e):
            return self.rounds + self.products + self.plan.product[e] + 1

        def bank(self, *e):
            n = self.products + self.plan.product[e]
            return n % MB, self.uses + n // MB

        def used(self, *e):
            n = self.products + self.plan.product[e]
            return [self.uses + (n + MB - k) // MB for k in range(MB)]

        def weights(self, *e):
            n = self.plan.chunk[e]
            return n % 2, self.chunks + n // 2 + 1

    def each_slot(run, loop):
        def after(*plans):
            return sum(len(p.product) for p in plans), sum(len(p.chunks) for p in plans)
        start = (FIRST, SLOT_0)
        run(Slot(FIRST, -1, None, 1, (0, 0), 0, None, None, 0))
        run(Slot(SLOT_0, 0, 0, 0, after(FIRST), 0, None, 0, 0))
        with loop(0, LAYERS - 1) as l:
            run(Slot(MIDDLE, l * 2 + 1, l, 1, after(*start), l, l, l, l + 1))
            run(Slot(MIDDLE, l * 2 + 2, l + 1, 0, after(*start, MIDDLE), l, l, l + 1, l + 1))
        run(Slot(SLOT_LAST, LAST, LAYERS - 1, 1, after(*start), LAYERS - 1, LAYERS - 1, LAYERS - 1, None))
        run(Slot(ENDING, LAST + 1, None, 0, after(*start, SLOT_LAST), LAYERS - 1, LAYERS - 1, None, None))

    def row(w, l, chunk):
        w = w[l] if isinstance(l, int) else w[bass.ds(l, 1)].rearrange("a c p n -> (a c) p n")
        return w[chunk]

    with nc.Block() as block:
        @block.sync
        def _(sp):
            def finished(t, e):
                kind, i = e
                if kind == "xp":
                    return xp_done, 2 * (t.s + 1) + i + 1
                return mm_done, t.made(kind, i + (kind in ("in", "z")))

            def run(t):
                plan = t.plan
                for n, e in enumerate(plan.chunks):
                    kind, i = e
                    if e == ("xp", 0):
                        if t.here is not None:
                            sp.wait_ge(mm_done, t.made("dt", KI - 1))
                        sp.dma_start(dtw[:], row(dt_d, t.front, 0)).then_inc(dtw_full, 16)
                    if n >= 2:
                        sp.wait_ge(*finished(t, plan.chunks[n - 2]))
                    elif plan is ENDING:
                        sp.wait_ge(mm_done, t.products + t.rounds - 2 * (1 - n))
                    elif plan is not FIRST:
                        sp.wait_ge(xp_done, 2 * t.s + n + 1)
                    w_d, l, c = {"out": (out_d, t.back, i), "pe": (pe_d, t.front, i), "in": (in_d, t.front, i // 2),
                                 "xp": (xp_d, t.front, i), "z": (in_d, t.here, KI // 2 + i // 2)}[kind]
                    src = row(w_d, l, c)
                    sp.dma_start(wring[:, n % 2, 0:src.shape[1]], src).then_inc(w_full[n % 2], 16)
            each_slot(run, sp.Fori)

        @block.gpsimd
        def _(pool):
            pool.dma_start(con[:], con_d).then_inc(con_full, 16)

            def move(dst, src):
                pool.sem_inc(pool_steps, 1)
                return pool.dma_start(dst, src)

            def load_s(h, c):
                move(lds[:, c % 2, :], s_d[h, c]).then_inc(s_full[c % 2], 16)

            def load_pr(h, c):
                for a, buf in ((1, ldp[c % 2]), (0, ldr[c % 2])):
                    move(buf.rearrange("p (g n) -> p g n", n=PACK),
                         pr_d[h * HG:(h + 1) * HG, :, a, c * PACK:(c + 1) * PACK].rearrange("g p n -> p g n")
                         ).then_inc(pr_full[c % 2], 16)

            def state(t, s, h):
                front = t.front is not None
                if front:
                    if t.back is not None:
                        pool.wait_ge(yhat_ready, FREE + s - 1)
                    src = vec_d[t.front] if isinstance(t.front, int) else vec_d[bass.ds(t.front, 1)].rearrange("a p n -> (a p) n")
                    move(vec[:, h, :], src).then_inc(vec_full, 16)
                load_s(h, 0)
                load_s(h, 1)
                if front:
                    if t.here is not None:
                        pool.wait_ge(h_ready, s)
                    load_pr(h, 0)
                    load_pr(h, 1)
                for c in range(CHUNKS):
                    if t.back is not None:
                        for k, uses in enumerate(t.used("out", c * JC + JC - 1)):
                            pool.wait_ge(mm_free[k], FREE + uses)
                        move(s_d[h, c], lds[:, c % 2, :]).then_inc(s_stored[c % 2], 16)
                        pool.wait_ge(s_stored[c % 2], ((s - 2) * 2 + c // 2 + 1) * 16)
                    if front:
                        pool.wait_ge(r_sum, s * CHUNKS + c + 1)
                        pool.wait_ge(ge_done, s * CHUNKS + c + 1)
                    if c + 2 < CHUNKS:
                        load_s(h, c + 2)
                        if front:
                            load_pr(h, c + 2)

            def spread(s, h):
                pool.wait_ge(dbc_ready, s + 1)
                move(bc_d[h], dbc[RANK:DBC, :]).then_inc(bc_stored, 16)
                pool.wait_ge(bc_stored, (s + 1) * 16)
                for q in range(NQ):
                    if not isinstance(s, int) or s > 0:
                        pool.wait_ge(sc_ready, s * STEPS - NQ + q + 1)
                    for a in range(2):
                        r = slice(a * STATE + q * NS, a * STATE + (q + 1) * NS)
                        move(bc[:, r, :], bc_d[h, r, :].unsqueeze(0).broadcast_to([P, NS, TOK])).then_inc(bc_full[q], 16)

            def run(t):
                state(t, t.s + 1, 1 - t.h)
                if t.front is not None:
                    spread(t.s + 1, 1 - t.h)
            each_slot(run, pool.Fori)

        @block.tensor
        def _(pe):
            for q in range(NST):
                pe.sem_inc(sc_used[q], FREE)
            pe.wait_ge(con_full, 16)
            blk = con[:, C_BLK:C_BLK + P]
            one = con[:, C_ONE:C_ONE + P]
            pe.matmul(ln_ps[:, 0:B], blk, cperp[:], start=True, stop=True).then_inc(cgrp_sum, 1)

            def product(t, e, ksteps, lhs, rhs):
                k, uses = t.bank(*e)
                pe.wait_ge(mm_free[k], FREE + uses)
                for n in range(ksteps):
                    ins = pe.matmul(mm_ps[:, k, 0:TOK], lhs(n), rhs(n), start=(n == 0), stop=(n == ksteps - 1))
                ins.then_inc(mm_done, 1)

            def weights(t, *e):
                k, uses = t.weights(*e)
                pe.wait_ge(w_full[k], uses * 16)
                return wring[:, k, :]

            def project(t, e):
                (kind, i), s, h, f, hf = e, t.s, t.h, t.s + 1, 1 - t.h
                if kind == "out":
                    if i == 0:
                        pe.wait_ge(yhat_ready, FREE + s)
                    w = weights(t, kind, i)
                    product(t, e, KI, lambda n: w[:, n * P:(n + 1) * P], lambda n: us[:, hf, n * TOK:(n + 1) * TOK])
                if kind == "pe":
                    if i == 0:
                        pe.wait_ge(pn_ready, f + 1)
                    w = weights(t, kind, i)
                    product(t, e, CJ, lambda n: w[:, n * P:(n + 1) * P],
                            lambda n: chunk4(xy[:, hf, n // JC * CHUNK:(n // JC + 1) * CHUNK])[:, :, n % JC, :])
                if kind == "in":
                    if i == 0:
                        pe.wait_ge(h_ready, f + 1)
                    w = weights(t, kind, i - i % 2)[:, i % 2 * KH * P:]
                    product(t, e, KH, lambda n: w[:, n * P:(n + 1) * P], lambda n: hid[:, hf, n * TOK:(n + 1) * TOK])
                if kind == "xp":
                    if i == 0:
                        pe.wait_ge(u_ready, f + 1)
                    w = weights(t, kind, i)
                    for n in range(KI // 2):
                        m = i * (KI // 2) + n
                        ins = pe.matmul(xp_ps[0:DBC, 0:TOK], w[:, n * DBC:(n + 1) * DBC],
                                        us[:, hf, m * TOK:(m + 1) * TOK], start=(m == 0), stop=(m == KI - 1))
                    ins.then_inc(xp_done, 1)
                if kind == "dt":
                    if i == 0:
                        pe.wait_ge(dbc_ready, f + 1)
                        pe.wait_ge(dtw_full, (f + 1) * 16)
                    product(t, e, 1, lambda n: dtw[:, i * P:(i + 1) * P], lambda n: dbc[0:RANK, :])
                if kind == "z":
                    w = weights(t, kind, i - i % 2)[:, i % 2 * KH * P:]
                    product(t, e, KH, lambda n: w[:, n * P:(n + 1) * P], lambda n: hid[:, h, n * TOK:(n + 1) * TOK])

            def norm_sums(s, h, n):
                for c in on(n, SUM_STEP):
                    pe.wait_ge(p_sum, s * CHUNKS + c + 1)
                    pv = xy[:, h, c * CHUNK:(c + 1) * CHUNK].rearrange("p (g j b k) -> p g j b k", j=JC, b=QB, k=T)
                    for j in range(JC):
                        pe.matmul(gm_ps, blk, pv[:, :, j, :, 0], start=(c == 0 and j == 0),
                                  stop=(c == CHUNKS - 1 and j == JC - 1))
                    pe.wait_ge(r_sq, s * CHUNKS + c + 1)
                    rv = chunk4(ldr[c % 2])
                    for j in range(JC):
                        ins = pe.matmul(ge_ps, blk, rv[:, :, j, :], start=(c == 0 and j == 0),
                                        stop=(c == CHUNKS - 1 and j == JC - 1))
                    ins.then_inc(ge_done, 1)
                for when, src, there in ((LN_STEP + 1, tok, tok_biased), (LN_STEP + 2, tok2, tok_sq)):
                    if n == when:
                        pe.wait_ge(there, s + 1)
                        for m in range(KH):
                            ins = pe.matmul(ln_ps[:, 0:TOK], one, src[:, m * TOK:(m + 1) * TOK], start=(m == 0),
                                            stop=(m == KH - 1))
                        ins.then_inc(ln_sum, 1)

            def state_sum(s, n):
                m, q = n // NQ, n % NQ
                if q == 0:
                    pe.wait_ge(y_free[m % 2], FREE + s * (KI // 2) + m // 2)
                pe.wait_ge(sc_ready, s * STEPS + n + 1)
                for t in range(NS // 2):
                    ins = pe.matmul(y_ps[:, m % 2, 0:TOK], ident, st[:, n % NST, t * TOK:(t + 1) * TOK],
                                    start=(q == 0 and t == 0), stop=(q == NQ - 1 and t == NS // 2 - 1))
                ins.then_inc(sc_used[n % NST], 1)

            def run(t):
                for n in range(STEPS):
                    if t.front is not None:
                        norm_sums(t.s + 1, 1 - t.h, n)
                    for e in t.plan.steps[n]:
                        project(t, e)
                    if t.here is not None and n > 0:
                        state_sum(t.s, n - 1)
                if t.here is not None:
                    state_sum(t.s, STEPS - 1)
            each_slot(run, pe.Fori)

        @block.scalar
        def _(act):
            o = Order(act, own_a)

            def step_sizes(t, s, h, g):
                if g == 0:
                    act.wait_ge(u_ready, s + 1)
                for m in range(g * MT, (g + 1) * MT):
                    k = t.bank("dt", m)[0]
                    act.wait_ge(mm_done, t.made("dt", m))
                    act.activation(xy[:, h, m * TOK:(m + 1) * TOK], mm_ps[:, k, 0:TOK], ACT.Identity,
                                   bias=vec[:, h, V_DTB + m:V_DTB + m + 1]).then_inc(mm_free[k], 1)
                for k, uses in enumerate(t.used("dt", (g + 1) * MT - 1)):
                    act.wait_ge(mm_free[k], FREE + uses)
                act.wait_ge(delta_ready, FREE + s * GROUPS + g)
                o.link(act.activation(softp[:], xy[:, h, g * MT * TOK:(g + 1) * MT * TOK], ACT.Abs))
                o.link(act.activation(softp[:], softp[:], ACT.Exp, scale=-1.0))
                act.activation(softp[:], softp[:], ACT.Ln, bias=1.0).then_inc(sp_ready, 1)

            def front_step(t, s, h, n):
                if n == VEC_STEP:
                    act.wait_ge(vec_full, (s + 1) * 16)
                    o.done(act.activation(half_cw[:], vec[:, h, V_CW:V_CW + 4 * KI], ACT.Copy, scale=0.5))
                    o.link(act.activation(neg_a[:, h, :], vec[:, h, V_A:V_A + KI * STATE], ACT.Exp))
                    o.link(act.activation(neg_a[:, h, :], neg_a[:, h, :], ACT.Copy, scale=-1.0))
                for c in on(n, CHUNK_STEP):
                    act.wait_ge(r_sum, s * CHUNKS + c + 1)
                    act.activation(ldr[c % 2], ldr[c % 2], ACT.Square).then_inc(r_sq, 1)
                if n == GN_STEP:
                    act.wait_ge(gn_var, s + 1)
                    act.activation(small[:, 3, :], small[:, 3, :], ACT.Sqrt).then_inc(gn_std, 1)
                if n == LN_STEP:
                    act.wait_ge(tok_points, s + 1)
                    for m in range(KH):
                        v = tok[:, m * TOK:(m + 1) * TOK]
                        ins = act.activation(v, v, ACT.Identity, bias=vec[:, h, V_PEB + m:V_PEB + m + 1])
                    ins.then_inc(tok_biased, 1)
                if n == LN_STEP + 1:
                    act.wait_ge(tok_centred, s + 1)
                    act.activation(tok2, tok, ACT.Square).then_inc(tok_sq, 1)
                if n == LN_STEP + 2:
                    act.wait_ge(ln_sum, 2 * s + 2)
                    act.activation(rexp[:], ln_ps[:, 0:TOK], ACT.Sqrt, bias=EPS).then_inc(ln_std, 1)
                    act.wait_ge(tok_normed, s + 1)
                    for m in range(KH):
                        v = slice(m * TOK, (m + 1) * TOK)
                        ins = act.activation(hid[:, h, v], tok[:, v], ACT.Identity, scale=vec[:, h, V_G + m:V_G + m + 1],
                                             bias=vec[:, h, V_B + m:V_B + m + 1])
                    ins.then_inc(h_ready, 1)
                for i in on(n, IN_STEP):
                    act.wait_ge(mm_done, t.made("in", i))
                    act.activation(us[:, h, i * TOK:(i + 1) * TOK], mm_ps[:, t.bank("in", i)[0], 0:TOK], ACT.Identity,
                                   scale=half_cw[:, i * 3 + 1:i * 3 + 2],
                                   bias=half_cw[:, i + 3 * KI:i + 3 * KI + 1]).then_inc(xs_mid, 1)
                if n == TANH_STEP:
                    for k, uses in enumerate(t.used("in", KI - 1)):
                        act.wait_ge(mm_free[k], FREE + uses)
                    act.activation(xy[:, h, 0:KI * TOK], us[:, h, :], ACT.Tanh).then_inc(conv_tanh, 1)
                if n == XP_STEP:
                    act.wait_ge(xp_done, 2 * s + 2)
                    act.activation(dbc[:], xp_ps[0:DBC, 0:TOK], ACT.Copy).then_inc(dbc_ready, 1)
                if n == DT_STEP[0]:
                    step_sizes(t, s, h, 0)

            def factors(s, h, n, func, bias):
                m, q = n // NQ, n % NQ
                if n == 0:
                    act.wait_ge(dA_zero, 1)
                if n % (MT * NQ) == 0:
                    act.wait_ge(delta_ready, FREE + s * GROUPS + n // (MT * NQ) + 1)
                act.wait_ge(dA_free[n % NDA], FREE + s * (STEPS // NDA) + n // NDA)
                d = xy[:, h, m * TOK:(m + 1) * TOK].rearrange("p (b t) -> p b t", t=T)[:, :, 1:T]
                for t in range(NS):
                    v = dA[:, n % NDA, t * TOK:(t + 1) * TOK].rearrange("p (b t) -> p b t", t=T)[:, :, 1:T]
                    a = m * STATE + q * NS + t
                    ins = act.activation(v, d, func, bias=bias, scale=neg_a[:, h, a:a + 1])
                ins.then_inc(dA_ready, 1)

            def ahead(s, l, h, n):
                if isinstance(l, int):
                    factors(s, h, n, *((ACT.Exp, 0.0) if l < LAYERS - 1 else (ACT.Identity, 1.0)))
                elif h == 1:
                    factors(s, h, n, ACT.Exp, 0.0)
                else:
                    with act.If(l < LAYERS - 1):
                        factors(s, h, n, ACT.Exp, 0.0)
                    with act.Else():
                        factors(s, h, n, ACT.Identity, 1.0)

            def run(t):
                here = t.here is not None
                if here:
                    ahead(t.s, t.l, t.h, 0)
                for n in range(STEPS):
                    if here and n + 1 < STEPS:
                        ahead(t.s, t.l, t.h, n + 1)
                    if here:
                        for g in range(1, GROUPS):
                            if n == DT_STEP[g * MT] + 1:
                                step_sizes(t, t.s, t.h, g)
                    if t.front is not None:
                        front_step(t, t.s + 1, 1 - t.h, n)
                    if here:
                        for m in on(n - 1, Z_STEP):
                            act.wait_ge(mm_done, t.made("z", m))
                            if m >= NZ:
                                act.wait_ge(sc_ready, t.s * STEPS + (m - NZ + 1) * NQ + GATE_STEP + 2)
                            act.activation(zs[:, m % NZ, :], mm_ps[:, t.bank("z", m)[0], 0:TOK], ACT.Tanh,
                                           scale=0.5).then_inc(z_tanh, 1)
            each_slot(run, lambda a, b: o.loop(a, b, HALVES * (3 + 2 * GROUPS)))

        @block.vector
        def _(dve):
            o = Order(dve, own_d)
            for k in range(MB):
                dve.sem_inc(mm_free[k], FREE)
            for k in range(2):
                dve.sem_inc(y_free[k], FREE)
            dve.sem_inc(yhat_ready, FREE)
            dve.sem_inc(delta_ready, FREE)
            for q in range(NDA):
                dve.sem_inc(dA_free[q], FREE)
            dve.memset(dA[:], 0.0).then_inc(dA_zero, 1)
            dve.wait_ge(con_full, 16)
            le = con[:, C_LE:C_LE + T].unsqueeze(1).broadcast_to([P, HB, T])
            en = con[:, C_EN:C_EN + T].unsqueeze(1).broadcast_to([P, MT * HB, T])
            dve.wait_ge(cgrp_sum, 1)
            o.link(dve.tensor_scalar(cgrp[:], ln_ps[:, 0:B], 1.0, None, ALU.mult))

            def images(v):
                return v.rearrange("p (b t) -> p b t", t=T)

            def read_out(t, *e):
                for k, uses in enumerate(t.used(*e)):
                    dve.wait_ge(mm_free[k], FREE + uses)

            def back_step(t, s, h, n):
                for j in on(n - 1, BACK_STEP):
                    c, k = j // JC, t.bank("out", j)[0]
                    if j % JC == 0:
                        dve.wait_ge(s_full[c % 2], ((s + 2) * (CHUNKS // 2) + c // 2 + 1) * 16)
                    dve.wait_ge(mm_done, t.made("out", j))
                    v = chunk4(lds[:, c % 2, :])[:, :, j % JC, :]
                    dve.tensor_tensor(v, v, mm_ps[:, k, 0:TOK].rearrange("p (g n) -> p g n", g=HG), ALU.add
                                      ).then_inc(mm_free[k], 1)

            def step_sizes(s, h, g):
                dve.wait_ge(sp_ready, s * GROUPS + g + 1)
                v = xy[:, h, g * MT * TOK:(g + 1) * MT * TOK]
                dve.scalar_tensor_tensor(v, v, 0.0, softp[:], ALU.max, ALU.add).then_inc(delta_ready, 1)

            def front_step(t, s, h, n):
                mean, esum, mm2, var, rstd = (small[:, i, :] for i in range(5))
                for c in on(n, CHUNK_STEP):
                    k = c % 2
                    dve.wait_ge(pr_full[k], (s * (CHUNKS // 2) + c // 2 + 1) * 32)
                    dve.wait_ge(s_full[k], (s * (CHUNKS // 2) + c // 2 + 1) * 16)
                    if t.back is not None:
                        read_out(t, "out", c * JC + JC - 1)
                    dve.tensor_tensor(xy[:, h, c * CHUNK:(c + 1) * CHUNK], ldp[k], lds[:, k, :], ALU.add).then_inc(p_sum, 1)
                    dve.tensor_tensor(ldr[k], ldr[k], lds[:, k, :], ALU.add).then_inc(r_sum, 1)
                if n == GN_STEP:
                    dve.wait_ge(ge_done, (s + 1) * CHUNKS)
                    o.done(dve.tensor_scalar(mean, gm_ps, 1.0 / (C // GN_GROUPS), None, ALU.mult))
                    o.done(dve.tensor_reduce(esum, ge_ps.rearrange("p (b k) -> p b k", k=T), AX.X, ALU.add))
                    o.wait()
                    o.done(dve.tensor_tensor(esum, esum, cgrp[:, h * HB:(h + 1) * HB], ALU.add))
                    o.done(dve.tensor_tensor(mm2, mean, mean, ALU.mult))
                    o.wait()
                    o.link(dve.scalar_tensor_tensor(var, mm2, -float(C // GN_GROUPS), esum, ALU.mult, ALU.add))
                    dve.tensor_scalar(var, var, 1.0 / (C // GN_GROUPS * PIX), EPS, ALU.mult, ALU.add).then_inc(gn_var, 1)
                    for c in range(CHUNKS):
                        v = xy[:, h, c * CHUNK:(c + 1) * CHUNK].rearrange("p (g j b k) -> p g j b k", j=JC, b=QB, k=T)[:, :, :, :, 0]
                        mb = mean.rearrange("p (g b) -> p g b", b=QB).unsqueeze(2).broadcast_to([P, HG, JC, QB])
                        o.done(dve.tensor_tensor(v, v, mb, ALU.subtract))
                if n == GN_STEP + 1:
                    dve.wait_ge(gn_std, s + 1)
                    o.link(dve.reciprocal(rstd, var))
                    o.link(dve.tensor_scalar(images(rexp[:]), rstd.unsqueeze(2).broadcast_to([P, HB, T]), 1.0, None, ALU.mult))
                    for c in range(CHUNKS):
                        v = chunk4(xy[:, h, c * CHUNK:(c + 1) * CHUNK])
                        rb = rexp[:].rearrange("p (g n) -> p g n", g=HG).unsqueeze(2).broadcast_to([P, HG, JC, QB * T])
                        ins = dve.tensor_tensor(v, v, rb, ALU.mult)
                    ins.then_inc(pn_ready, 1)
                for m in on(n - 1, PE_STEP):
                    k = t.bank("pe", m)[0]
                    dve.wait_ge(mm_done, t.made("pe", m))
                    dve.tensor_tensor(images(tok[:, m * TOK:(m + 1) * TOK]), images(mm_ps[:, k, 0:TOK]), le,
                                      ALU.mult).then_inc(mm_free[k], 1)
                tk = tok.rearrange("p (m n) -> p m n", n=TOK)

                def over_m(v):
                    return v.unsqueeze(1).broadcast_to([P, KH, TOK])
                if n == LN_STEP:
                    read_out(t, "pe", KH - 1)
                    to_points(dve, o, along_x(tok, KH * HB), along_x(tok2, KH * HB))
                    yi, yo = along_y(tok2, KH * HB), along_y(tok, KH * HB)
                    o.done(dve.tensor_tensor(yo(0), yi(0), yi(2), ALU.add))
                    o.done(dve.scalar_tensor_tensor(yo(1), yi(2), -2.0, yi(0), ALU.mult, ALU.add))
                    o.wait()
                    o.link(dve.tensor_tensor(yo(2), yo(0), yi(1), ALU.subtract))
                    dve.tensor_tensor(yo(0), yo(0), yi(1), ALU.add).then_inc(tok_points, 1)
                if n == LN_STEP + 1:
                    dve.wait_ge(ln_sum, 2 * s + 1)
                    o.link(dve.tensor_scalar(rexp[:], ln_ps[:, 0:TOK], 1.0, None, ALU.mult))
                    dve.tensor_tensor(tk, tk, over_m(rexp[:]), ALU.subtract).then_inc(tok_centred, 1)
                if n == LN_STEP + 2:
                    dve.wait_ge(ln_std, s + 1)
                    o.link(dve.reciprocal(rexp[:], rexp[:]))
                    dve.wait_ge(tok_centred, s + 1)
                    dve.tensor_tensor(tk, tk, over_m(rexp[:]), ALU.mult).then_inc(tok_normed, 1)
                for i in on(n - 1, IN_STEP):
                    k = t.bank("in", i)[0]
                    dve.wait_ge(xs_mid, s * KI + i + 1)
                    uv, pv = images(us[:, h, i * TOK:(i + 1) * TOK]), images(mm_ps[:, k, 0:TOK])
                    o.link(dve.scalar_tensor_tensor(uv[:, :, 1:T], pv[:, :, 0:T - 1], half_cw[:, i * 3:i * 3 + 1],
                                                    uv[:, :, 1:T], ALU.mult, ALU.add))
                    dve.scalar_tensor_tensor(uv[:, :, 0:T - 1], pv[:, :, 1:T], half_cw[:, i * 3 + 2:i * 3 + 3],
                                             uv[:, :, 0:T - 1], ALU.mult, ALU.add).then_inc(mm_free[k], 1)
                if n == TANH_STEP:
                    dve.wait_ge(conv_tanh, s + 1)
                    read_out(t, "in", KI - 1)
                    dve.scalar_tensor_tensor(us[:, h, :], xy[:, h, 0:KI * TOK], 1.0, us[:, h, :], ALU.add, ALU.mult
                                             ).then_inc(u_ready, 1)
                if n == STEPS - 1:
                    step_sizes(s, h, 0)

            def drive(s, h, n):
                m, q = n // NQ, n % NQ
                tile = slice(m * TOK, (m + 1) * TOK)
                u, delta = us[:, h, :], xy[:, h, :]
                if n == 0:
                    dve.wait_ge(u_ready, s + 1)
                if n % (MT * NQ) == 0:
                    dve.wait_ge(delta_ready, FREE + s * GROUPS + n // (MT * NQ) + 1)
                if m == 0:
                    dve.wait_ge(bc_full[q], (s + 1) * 32)
                if q == 0:
                    o.link(dve.tensor_tensor(wt[:], delta[:, tile], u[:, tile], ALU.mult))
                v = st[:, n % NST, :].rearrange("p (n t) -> p n t", t=TOK)
                dve.wait_ge(sc_used[n % NST], FREE + s * (STEPS // NST) + n // NST)
                dve.tensor_tensor(v, bc[:, q * NS:(q + 1) * NS, :],
                                  wt[:].unsqueeze(1).broadcast_to([P, NS, TOK]), ALU.mult).then_inc(driven, 1)

            def recurrence(s, h, n):
                q = n % NQ
                if n == 0:
                    drive(s, h, 0)
                buf = st[:, n % NST, :]
                v = buf.rearrange("p (n t) -> p n t", t=TOK)
                dve.wait_ge(driven, s * STEPS + n + 1)
                dve.wait_ge(dA_ready, s * STEPS + n + 1)
                dve.tensor_tensor_scan(buf, dA[:, n % NDA, :], buf, 0.0, ALU.mult, ALU.add).then_inc(dA_free[n % NDA], 1)
                if n + 1 < STEPS:
                    drive(s, h, n + 1)
                dve.wait_ge(dA_free[n % NDA], FREE + s * (STEPS // NDA) + n // NDA + 1)
                o.done(dve.tensor_tensor(v, v, bc[:, STATE + q * NS:STATE + (q + 1) * NS, :], ALU.mult))

            def halve(n):
                v = st[:, n % NST, :].rearrange("p (n t) -> p n t", t=TOK)
                o.wait()
                dve.tensor_tensor(v[:, 0:NS // 2], v[:, 0:NS // 2], v[:, NS // 2:NS], ALU.add).then_inc(sc_ready, 1)

            def gated(t, s, h, m):
                tile = slice(m * TOK, (m + 1) * TOK)
                u = us[:, h, :]
                last = m * NQ + NQ - 1
                dve.wait_ge(sc_used[last % NST], FREE + s * (STEPS // NST) + last // NST + 1)
                dve.scalar_tensor_tensor(u[:, tile], u[:, tile], vec[:, h, V_D + m:V_D + m + 1], y_ps[:, m % 2, 0:TOK],
                                         ALU.mult, ALU.add).then_inc(y_free[m % 2], 1)
                dve.wait_ge(y_free[m % 2], FREE + s * (KI // 2) + m // 2 + 1)
                k, uses = t.bank("z", m)
                dve.wait_ge(mm_free[k], FREE + uses + 1)
                o.link(dve.scalar_tensor_tensor(u[:, tile], u[:, tile], 0.5, zs[:, m % NZ, :], ALU.mult, ALU.mult))
                if m % MT == MT - 1:
                    some = slice((m + 1 - MT) * TOK, (m + 1) * TOK)
                    uv, tmp = u[:, some], xy[:, h, some]
                    to_modes(dve, o, along_x(uv, MT * HB), along_x(tmp, MT * HB))
                    to_modes(dve, o, along_y(tmp, MT * HB), along_y(uv, MT * HB))
                    if m == KI - 1:
                        dve.tensor_tensor(images(uv), images(uv), en, ALU.mult).then_inc(yhat_ready, 1)
                    else:
                        o.done(dve.tensor_tensor(images(uv), images(uv), en, ALU.mult))

            def run(t):
                s, h = t.s, t.h
                for n in range(STEPS):
                    if t.here is not None:
                        recurrence(s, h, n)
                        halve(n)
                        if n % NQ == GATE_STEP and n > NQ:
                            gated(t, s, h, n // NQ - 1)
                        for m in on(n - 2, Z_STEP):
                            dve.wait_ge(z_tanh, s * KI + m + 1)
                            k = t.bank("z", m)[0]
                            dve.scalar_tensor_tensor(zs[:, m % NZ, :], zs[:, m % NZ, :], 1.0, mm_ps[:, k, 0:TOK],
                                                     ALU.add, ALU.mult).then_inc(mm_free[k], 1)
                    if t.back is not None:
                        back_step(t, s - 1, 1 - h, n)
                    if t.front is not None:
                        front_step(t, s + 1, 1 - h, n)
                    if t.here is not None:
                        for g in range(1, GROUPS):
                            if n == DT_STEP[g * MT] + 3:
                                step_sizes(s, h, g)
                if t.here is not None:
                    gated(t, s, h, KI - 1)
            per = 5 + 4 + 2 + 7 + 2 + KI + KI + STEPS + KI + 9 * (KI // MT) - 1
            each_slot(run, lambda a, b: o.loop(a, b, HALVES * per))


def apply(nc, sb, ps, sem, x, con_d, spread_d, s_d, out):
    PB = 2 * QB
    RT = PB * T
    AB = 2 * QB
    con = sb("ap_con", [P, NC], F32)
    spread = sb("ap_spread", [RT, PB, PIX], F32)
    xa = sb("xa", [P, AB, CJ, PIX], F32)
    modes = sb("modes", [P, 2, CJ * RT], F32)
    points = sb("points", [P, CJ * RT], F32)
    turned = sb("turned", [RT, C], F32)
    acc = ps("acc", [P, 2, 4, 512], F32)

    con_full = sem("ap_con_full")
    s_full = [sem(f"ap_s_full{i}") for i in range(2)]
    x_full = [sem(f"xa_full{i}") for i in range(AB)]
    x_stored = [sem(f"xa_stored{i}") for i in range(AB)]
    points_ready = sem("points_ready")
    turned_ps = sem("turned_ps")
    acc_read = sem("acc_read")
    resized = sem("resized")
    own = sem("ap_dve_own")
    xv = x.rearrange("b (p j) h w -> b p (j h w)", p=P)
    ov = out.rearrange("b (p j) h w -> b p (j h w)", p=P)
    GROUPS = B // PB
    QUADS = PB * CHUNKS + 2

    def image(v, b):
        return v[bass.ds(b, 1)].rearrange("o p n -> (o p) n")

    with nc.Block() as block:
        @block.sync
        def _(sp):
            for k in range(2):
                sp.wait_ge(s_full[k], 32)
            for i in range(AB):
                sp.dma_start(xa[:, i].rearrange("p j n -> p (j n)"), image(xv, i)).then_inc(x_full[i], 16)
            with sp.Fori(0, B // AB - 1) as n:
                for i in range(AB):
                    sp.wait_ge(x_stored[i], (n + 1) * 16)
                    sp.dma_start(xa[:, i].rearrange("p j n -> p (j n)"), image(xv, (n + 1) * AB + i)).then_inc(x_full[i], 16)

        @block.gpsimd
        def _(pool):
            pool.dma_start(con[:], con_d).then_inc(con_full, 16)
            pool.dma_start(spread[:].rearrange("p b n -> p (b n)"), spread_d).then_inc(con_full, 16)

            def fetch(h, g, k):
                for gg in range(2):
                    src = s_d[h:h + 1].rearrange("o c p (g n) -> (o p) c g n", g=HG)[:, :, g * 2 + gg, :]
                    pool.dma_start(modes[:, k, :].rearrange("p (c g n) -> p c g n", c=CHUNKS, g=2)[:, :, gg, :],
                                   src).then_inc(s_full[k], 16)
            for g in range(GROUPS):
                if g >= 2:
                    pool.wait_ge(points_ready, g - 1)
                fetch(g // (GROUPS // HALVES), g % (GROUPS // HALVES), g % 2)

        @block.scalar
        def _(act):
            def store(b, i, uses):
                act.wait_ge(acc_read, uses)
                act.dma_start(image(ov, b), xa[:, i].rearrange("p j n -> p (j n)")).then_inc(x_stored[i], 16)
            with act.Fori(0, GROUPS) as g:
                for i in range(PB):
                    store(g * PB + i, i % AB, 2 * FREE + g * QUADS + 2 + (i + 1) * CHUNKS)
            for i in range(AB):
                act.wait_ge(x_stored[i], B // AB * 16)

        @block.tensor
        def _(pe):
            pe.sem_inc(resized, FREE)
            pe.wait_ge(con_full, 32)
            with pe.Fori(0, GROUPS) as g:
                pe.wait_ge(points_ready, g + 1)
                pv = points[:].rearrange("p (j n) -> p j n", j=CJ)
                for e in range(2):
                    pe.wait_ge(acc_read, 2 * FREE + g * QUADS + e - 1)
                    for j in range(CJ // 2):
                        jj = e * (CJ // 2) + j
                        dst = acc[0:RT, e].rearrange("p a n -> p (a n)")[:, j * P:(j + 1) * P]
                        ins = pe.matmul(dst, pv[:, jj, :], con[:, C_ID:C_ID + P], start=True, stop=True)
                    ins.then_inc(turned_ps, 1)
                pe.wait_ge(acc_read, 2 * FREE + g * QUADS + 2)
                for i in range(PB):
                    for c in range(CHUNKS):
                        pe.wait_ge(acc_read, 2 * FREE + g * QUADS + 2 + i * CHUNKS + c - 1)
                        for j in range(JC):
                            ins = pe.matmul(acc[:, c % 2, j, 0:PIX], turned[:, (c * JC + j) * P:(c * JC + j + 1) * P],
                                            spread[:, i, :], start=True, stop=True)
                        ins.then_inc(resized, 1)

        @block.vector
        def _(dve):
            o = Order(dve, own)
            dve.sem_inc(acc_read, 2 * FREE)
            dve.wait_ge(con_full, 32)
            ie = con[:, C_IE:C_IE + T].unsqueeze(1).broadcast_to([P, CJ * PB, T])

            def points_of(k, uses):
                dve.wait_ge(s_full[k], uses * 32)
                m = modes[:, k, :]
                v = m.rearrange("p (r t) -> p r t", t=T)
                o.link(dve.tensor_tensor(v, v, ie, ALU.mult))
                to_points(dve, o, along_x(m, CJ * PB), along_x(points, CJ * PB))
                to_points(dve, o, along_y(points, CJ * PB), along_y(m, CJ * PB))
                pv = points[:].rearrange("p (c j g n) -> p c g j n", c=CHUNKS, j=JC, g=2)
                mv = m.rearrange("p (c g j n) -> p c g j n", c=CHUNKS, g=2, j=JC)
                for c in range(CHUNKS):
                    ins = dve.tensor_copy(pv[:, c], mv[:, c])
                ins.then_inc(points_ready, 1)

            def group(g, following):
                dve.wait_ge(resized, FREE + g * PB * CHUNKS)
                for e in range(2):
                    dve.wait_ge(turned_ps, g * 2 + e + 1)
                    ins = dve.tensor_scalar(turned[:, e * (C // 2):(e + 1) * (C // 2)],
                                            acc[0:RT, e].rearrange("p a n -> p (a n)")[:, 0:C // 2], 1.0, None, ALU.mult)
                    ins.then_inc(acc_read, 1)
                for i in range(PB):
                    dve.wait_ge(x_full[i % AB], (g * (PB // AB) + i // AB + 1) * 16)
                    for c in range(CHUNKS):
                        dve.wait_ge(resized, FREE + (g * PB + i) * CHUNKS + c + 1)
                        v = xa[:, i % AB, c * JC:(c + 1) * JC, :]
                        dve.tensor_tensor(v, v, acc[:, c % 2, :, 0:PIX], ALU.add).then_inc(acc_read, 1)
                    if i == PB // 2 and following:
                        points_of(*following)

            points_of(0, 1)
            with o.loop(0, GROUPS // 2 - 1, 2 * (1 + 8)) as i:
                group(i * 2, (1, i + 1))
                group(i * 2 + 1, (0, i + 2))
            group(GROUPS - 2, (1, GROUPS // 2))
            group(GROUPS - 1, None)


def program(nc, t, out):
    ctx = ExitStack()
    with ctx:
        cperp = ctx.enter_context(nc.sbuf_tensor("cperp", [P, B], F32))
        pr_d = nc.dram_tensor("pr_scratch", (QG, P, 2, CJ * QB * T), F32, kind="Internal").ap()
        s_d = nc.dram_tensor("s_scratch", (HALVES, CHUNKS, P, CHUNK), F32, kind="Internal").ap()
        bc_d = nc.dram_tensor("bc_scratch", (HALVES, 2 * STATE, TOK), F32, kind="Internal").ap()

        def phase(build, *args):
            with ExitStack() as own:
                build(nc, lambda n, shape, dt: own.enter_context(nc.sbuf_tensor(n, shape, dt)),
                      lambda n, shape, dt: own.enter_context(nc.psum_tensor(n, shape, dt)),
                      lambda n: ctx.enter_context(nc.semaphore(n)), *args)
        phase(statistics, t["x"], t["con"], pr_d, s_d, cperp)
        phase(layers, t["con"], t["vec"], t["pe"], t["inp"], t["xp"], t["dt"], t["outw"], pr_d, s_d, bc_d, cperp)
        phase(apply, t["x"], t["con"], t["spread"], s_d, out)


def kernel(**inputs):
    import concourse.bacc as _bacc
    from concourse.bass_utils import run_bass_kernel_spmd as _run

    def layer(l):
        new = {"pe_W": "pe_w", "in_W": "in_w", "xproj_W": "xproj_w", "dt_W": "dtproj_w", "dt_b": "dtproj_b", "out_W": "out_w"}
        pre = f"L{l}_conv_"
        return {new.get(n[len(pre):], n[len(pre):]): np.asarray(v) for n, v in inputs.items() if n.startswith(pre)}

    ls = [layer(l) for l in range(LAYERS)]

    def cols(v, n):
        return v.reshape(n, P, -1).transpose(1, 0, 2).reshape(P, -1)

    con, spread = constants()
    arrays = {
        "x": np.asarray(inputs["x"]),
        "con": con,
        "spread": spread.reshape(2 * QB * T, -1),
        "vec": np.stack([np.concatenate([cols(w["pe_b"], KH), cols(w["ln_g"], KH), cols(w["ln_b"], KH),
                                         cols(w["conv_w"], KI), cols(w["conv_b"], KI), cols(w["dtproj_b"], KI),
                                         cols(w["D_param"], KI), cols(w["A_log"], KI)], axis=1) for w in ls]),
        "pe": np.stack([w["pe_w"].reshape(P, CJ, KH, P).transpose(2, 0, 1, 3).reshape(KH, P, CJ * P) for w in ls]),
        "inp": np.stack([w["in_w"].reshape(KH, P, KI, 2, P).transpose(2, 1, 3, 0, 4).reshape(KI, P, 2 * KH * P) for w in ls]),
        "xp": np.stack([w["xproj_w"].reshape(2, KI // 2, P, DBC).transpose(0, 2, 1, 3).reshape(2, P, KI // 2 * DBC) for w in ls]),
        "dt": np.stack([w["dtproj_w"][None] for w in ls]),
        "outw": np.stack([w["out_w"].reshape(KI, P, P, CJ).transpose(3, 1, 0, 2).reshape(CJ, P, KI * P) for w in ls]),
    }
    nc = _bacc.Bacc("TRN2", target_bir_lowering=False, num_devices=1)
    t = {n: nc.dram_tensor(f"{n}_dram", a.shape, mybir.dt.from_np(a.dtype), kind="ExternalInput").ap() for n, a in arrays.items()}
    out = nc.dram_tensor("out_dram", (B, C, H, W), F32, kind="ExternalOutput").ap()
    program(nc, t, out)
    r = _run(nc, [{f"{n}_dram": np.ascontiguousarray(a) for n, a in arrays.items()}], core_ids=[0])
    return r.results[0]["out_dram"]
```
